# Optimizing a Trainium2 kernel written in Bass

```python
import numpy as np
import jax
import jax.numpy as jnp

def _softmax(x, axis=-1):
    return jax.nn.softmax(x, axis=axis)

def _gelu(x):
    return jax.nn.gelu(x, approximate=True)

def _silu(x):
    return jax.nn.silu(x)

def _sigmoid(x):
    return jax.nn.sigmoid(x)

def _layernorm(x, axis=-1, eps=1e-05):
    m = jnp.mean(x, axis=axis, keepdims=True)
    v = jnp.var(x, axis=axis, keepdims=True)
    return (x - m) / jnp.sqrt(v + eps)

def _scatter_add(tgt, idx, src, axis=0):
    return tgt.at[idx].add(src)

def _segment_sum(src, seg, n):
    return jax.ops.segment_sum(src, seg, n)
kernel_name = 'mk_adaln_ffn_d4_seqx_r8_717b09'

def setup_inputs(seed: int=0):
    np.random.seed(seed)
    _w = jnp.asarray

    def _rec_inputs():
        import jax
        import jax.numpy as jnp
        _rk = jax.random.key(seed)
        x = -0.000125 + 0.9999 * jax.random.normal(jax.random.fold_in(_rk, 1), (64, 32, 512), jnp.float32)
        _lenS = 32 - jax.random.randint(jax.random.fold_in(_rk, 7), (64,), 0, max(1, 32 // 4) + 1, jnp.int32)
        _lenS2 = 32 - jax.random.randint(jax.random.fold_in(_rk, 8), (64,), 0, max(1, 32 // 4) + 1, jnp.int32)
        cond_128 = 0.0061147 + 1.02565 * jax.random.normal(jax.random.fold_in(_rk, 11), (64, 128), jnp.float32)
        fside_S_0 = -0.022604 + 0.987366 * jax.random.normal(jax.random.fold_in(_rk, 12), (32,), jnp.float32)
        return (x, cond_128, fside_S_0)
    x, cond_128, fside_S_0 = _rec_inputs()

    def _L0_cond_setup():
        import jax, jax.numpy as jnp
        import numpy as np
        from jax import lax
        N, C_IN, L = (32, 32, 512)
        C_OUT, K, GROUPS = (32, 9, 4)
        C_DIM, PAD, STRIDE = (128, 4, 1)
        key = jax.random.key(seed)
        k1, k2, k3, k4, k5 = jax.random.split(key, 5)
        x = jax.random.normal(k1, (N, C_IN, L), dtype=jnp.float32)
        c = jax.random.normal(k2, (N, C_DIM), dtype=jnp.float32)
        weight = jax.random.normal(k3, (C_OUT, C_IN // GROUPS, K), dtype=jnp.float32)
        c_weight = jax.random.normal(k4, (C_OUT, C_DIM), dtype=jnp.float32)
        bias = jax.random.normal(k5, (C_OUT,), dtype=jnp.float32)
        return {'x': x, 'c': c, 'weight': weight, 'c_weight': c_weight, 'bias': bias}
    _L0_cond_all = _L0_cond_setup()
    _L0_cond_in = {k: v for k, v in _L0_cond_all.items() if k in ('weight', 'c_weight')}
    del _L0_cond_all

    def _L0_ffn_setup():
        import jax, jax.numpy as jnp
        import numpy as np
        B_, S, D_IN, D_OUT = (4, 256, 512, 512)
        N, RANK, ALPHA = (8, 16, 32)
        SCALE = ALPHA / RANK
        key = jax.random.key(seed)
        kx, ka, kb, kw, kbias = jax.random.split(key, 5)
        x = jax.random.normal(kx, (B_, S, D_IN), dtype=jnp.float32)
        lora_A = jax.random.normal(ka, (N, RANK, D_IN), dtype=jnp.float32) * (1.0 / np.sqrt(D_IN))
        lora_B = jax.random.normal(kb, (N, D_OUT, RANK), dtype=jnp.float32) * (1.0 / np.sqrt(RANK))
        W = jax.random.normal(kw, (D_OUT, D_IN), dtype=jnp.float32) * (1.0 / np.sqrt(D_IN))
        bias = jax.random.normal(kbias, (D_OUT,), dtype=jnp.float32) * 0.01
        lora_weights = jnp.full((N,), 1.0 / N, dtype=jnp.float32)
        return {'x': x, 'lora_A': lora_A, 'lora_B': lora_B, 'W': W, 'bias': bias, 'lora_weights': lora_weights}
    _L0_ffn_all = _L0_ffn_setup()
    _L0_ffn_in = {k: v for k, v in _L0_ffn_all.items() if k in ('lora_A', 'lora_B', 'W', 'bias', 'lora_weights')}
    del _L0_ffn_all

    def _L1_cond_setup():
        import jax, jax.numpy as jnp
        import numpy as np
        K = 8
        T = 1.0
        D_EMBD = 128
        IN_C = 32
        OUT_C = 32
        BS = 32
        H = 512
        HID = 128
        key = jax.random.key(seed)
        ks = jax.random.split(key, 10)
        s = lambda fan_in: 1.0 / np.sqrt(fan_in)
        return {'x': jax.random.normal(ks[0], (BS, IN_C, H), dtype=jnp.float32), 'embedding': jax.random.normal(ks[1], (BS, D_EMBD), dtype=jnp.float32), 'W0': jax.random.normal(ks[2], (D_EMBD, HID), dtype=jnp.float32) * s(D_EMBD), 'b0': jnp.zeros((HID,), dtype=jnp.float32), 'W1': jax.random.normal(ks[3], (HID, HID), dtype=jnp.float32) * s(HID), 'b1': jnp.zeros((HID,), dtype=jnp.float32), 'W2': jax.random.normal(ks[4], (HID, K), dtype=jnp.float32) * s(HID), 'b2': jnp.zeros((K,), dtype=jnp.float32), 'weight': jax.random.normal(ks[5], (K, OUT_C, IN_C, 1), dtype=jnp.float32) * s(IN_C), 'bias_k': jax.random.normal(ks[6], (K, OUT_C), dtype=jnp.float32) * 0.1}
    _L1_cond_all = _L1_cond_setup()
    _L1_cond_in = {k: v for k, v in _L1_cond_all.items() if k in ('W0', 'b0', 'W1', 'b1', 'W2', 'b2', 'weight', 'bias_k')}
    del _L1_cond_all

    def _L1_ffn_setup():
        import jax, jax.numpy as jnp
        import numpy as np

        def sparsemax(z):
            E = z.shape[-1]
            z_sorted = -jnp.sort(-z, axis=-1)
            z_cum = jnp.cumsum(z_sorted, axis=-1)
            k = jnp.arange(1, E + 1, dtype=z.dtype)
            support = 1.0 + k * z_sorted > z_cum
            k_z = jnp.sum(support, axis=-1, keepdims=True)
            tau_sum = jnp.take_along_axis(z_cum, k_z.astype(jnp.int32) - 1, axis=-1)
            tau = (tau_sum - 1.0) / k_z.astype(z.dtype)
            return jnp.maximum(z - tau, 0.0)
        key = jax.random.key(seed)
        ks = jax.random.split(key, 6)
        B, S, D_IN, D_OUT, E, R = (8, 256, 512, 512, 8, 16)
        x = jax.random.normal(ks[0], (B, S, D_IN), dtype=jnp.float32)
        W_base = jax.random.normal(ks[1], (D_OUT, D_IN), dtype=jnp.float32) * D_IN ** (-0.5)
        b_base = jax.random.normal(ks[2], (D_OUT,), dtype=jnp.float32) * 0.01
        W_router = jax.random.normal(ks[3], (E, D_IN), dtype=jnp.float32) * D_IN ** (-0.5)
        b_router = jnp.zeros((E,), dtype=jnp.float32)
        lora_A = jax.random.normal(ks[4], (E, D_IN, R), dtype=jnp.float32) * D_IN ** (-0.5)
        lora_B = jnp.zeros((E, R, D_OUT), dtype=jnp.float32)
        return {'x': x, 'W_base': W_base, 'b_base': b_base, 'W_router': W_router, 'b_router': b_router, 'lora_A': lora_A, 'lora_B': lora_B}
    _L1_ffn_all = _L1_ffn_setup()
    _L1_ffn_in = {k: v for k, v in _L1_ffn_all.items() if k in ('W_base', 'b_base', 'W_router', 'b_router', 'lora_A', 'lora_B')}
    del _L1_ffn_all

    def _L2_cond_setup():
        import jax, jax.numpy as jnp
        import numpy as np
        K = 8
        T = 1.0
        D_EMBD = 128
        IN_C = 32
        OUT_C = 32
        BS = 32
        H = 512
        HID = 128
        key = jax.random.key(seed)
        ks = jax.random.split(key, 10)
        s = lambda fan_in: 1.0 / np.sqrt(fan_in)
        return {'x': jax.random.normal(ks[0], (BS, IN_C, H), dtype=jnp.float32), 'embedding': jax.random.normal(ks[1], (BS, D_EMBD), dtype=jnp.float32), 'W0': jax.random.normal(ks[2], (D_EMBD, HID), dtype=jnp.float32) * s(D_EMBD), 'b0': jnp.zeros((HID,), dtype=jnp.float32), 'W1': jax.random.normal(ks[3], (HID, HID), dtype=jnp.float32) * s(HID), 'b1': jnp.zeros((HID,), dtype=jnp.float32), 'W2': jax.random.normal(ks[4], (HID, K), dtype=jnp.float32) * s(HID), 'b2': jnp.zeros((K,), dtype=jnp.float32), 'weight': jax.random.normal(ks[5], (K, OUT_C, IN_C, 1), dtype=jnp.float32) * s(IN_C), 'bias_k': jax.random.normal(ks[6], (K, OUT_C), dtype=jnp.float32) * 0.1}
    _L2_cond_all = _L2_cond_setup()
    _L2_cond_in = {k: v for k, v in _L2_cond_all.items() if k in ('W0', 'b0', 'W1', 'b1', 'W2', 'b2', 'weight', 'bias_k')}
    del _L2_cond_all

    def _L2_ffn_setup():
        import jax, jax.numpy as jnp
        import numpy as np
        B, S, D = (4, 256, 512)
        NUM_EXPERTS, TOP_K = (3, 2)

        def _expert_outputs(h, w1, b1, w2, b2):
            pre = jnp.einsum('bsd,edf->ebsf', h, w1) + b1[:, None, None, :]
            act = jnp.stack([jnp.tanh(pre[0]), jax.nn.gelu(pre[1], approximate=False), jax.nn.silu(pre[2])])
            return jnp.einsum('ebsf,efd->ebsd', act, w2) + b2[:, None, None, :]
        key = jax.random.key(seed)
        ks = jax.random.split(key, 8)
        scale_in = 1.0 / np.sqrt(D)
        scale_gate = 1.0 / np.sqrt(D + 1)
        return {'h': jax.random.normal(ks[0], (B, S, D), dtype=jnp.float32), 'gate_w': jax.random.uniform(ks[1], (D + 1, NUM_EXPERTS), minval=-scale_gate, maxval=scale_gate, dtype=jnp.float32), 'gate_b': jnp.zeros((NUM_EXPERTS,), dtype=jnp.float32), 'w1': jax.random.uniform(ks[2], (NUM_EXPERTS, D, D), minval=-scale_in, maxval=scale_in, dtype=jnp.float32), 'b1': jnp.zeros((NUM_EXPERTS, D), dtype=jnp.float32), 'w2': jax.random.uniform(ks[3], (NUM_EXPERTS, D, D), minval=-scale_in, maxval=scale_in, dtype=jnp.float32), 'b2': jnp.zeros((NUM_EXPERTS, D), dtype=jnp.float32)}
    _L2_ffn_all = _L2_ffn_setup()
    _L2_ffn_in = {k: v for k, v in _L2_ffn_all.items() if k in ('gate_w', 'gate_b', 'w1', 'b1', 'w2', 'b2')}
    del _L2_ffn_all

    def _L3_cond_setup():
        import jax, jax.numpy as jnp
        import numpy as np
        K = 8
        T = 1.0
        D_EMBD = 128
        IN_C = 32
        OUT_C = 32
        BS = 32
        H = 512
        HID = 128
        key = jax.random.key(seed)
        ks = jax.random.split(key, 10)
        s = lambda fan_in: 1.0 / np.sqrt(fan_in)
        return {'x': jax.random.normal(ks[0], (BS, IN_C, H), dtype=jnp.float32), 'embedding': jax.random.normal(ks[1], (BS, D_EMBD), dtype=jnp.float32), 'W0': jax.random.normal(ks[2], (D_EMBD, HID), dtype=jnp.float32) * s(D_EMBD), 'b0': jnp.zeros((HID,), dtype=jnp.float32), 'W1': jax.random.normal(ks[3], (HID, HID), dtype=jnp.float32) * s(HID), 'b1': jnp.zeros((HID,), dtype=jnp.float32), 'W2': jax.random.normal(ks[4], (HID, K), dtype=jnp.float32) * s(HID), 'b2': jnp.zeros((K,), dtype=jnp.float32), 'weight': jax.random.normal(ks[5], (K, OUT_C, IN_C, 1), dtype=jnp.float32) * s(IN_C), 'bias_k': jax.random.normal(ks[6], (K, OUT_C), dtype=jnp.float32) * 0.1}
    _L3_cond_all = _L3_cond_setup()
    _L3_cond_in = {k: v for k, v in _L3_cond_all.items() if k in ('W0', 'b0', 'W1', 'b1', 'W2', 'b2', 'weight', 'bias_k')}
    del _L3_cond_all

    def _L3_ffn_setup():
        import jax, jax.numpy as jnp
        import numpy as np

        def _simulate_fp8_e4m3(w):
            return w.astype(jnp.float8_e4m3fn).astype(jnp.float32)
        key = jax.random.key(seed)
        k_x, k_w, k_s, k_b = jax.random.split(key, 4)
        B, S, D_in, D_out = (4, 256, 512, 512)
        x = jax.random.normal(k_x, (B, S, D_in), dtype=jnp.bfloat16)
        w_real = jax.random.normal(k_w, (D_out, D_in), dtype=jnp.float32) * 0.02
        weight_scale = jnp.array([0.001], dtype=jnp.float32)
        weight = _simulate_fp8_e4m3(w_real / weight_scale)
        bias = jax.random.normal(k_b, (D_out,), dtype=jnp.float32) * 0.02
        return {'x': x, 'weight': weight, 'weight_scale': weight_scale, 'bias': bias}
    _L3_ffn_all = _L3_ffn_setup()
    _L3_ffn_in = {k: v for k, v in _L3_ffn_all.items() if k in ('weight', 'weight_scale', 'bias')}
    del _L3_ffn_all
    return {'x': x, 'cond_128': cond_128, 'fside_S_0': fside_S_0, 'L0_cond_weight': _L0_cond_in['weight'], 'L0_cond_c_weight': _L0_cond_in['c_weight'], 'L0_ffn_lora_A': _L0_ffn_in['lora_A'], 'L0_ffn_lora_B': _L0_ffn_in['lora_B'], 'L0_ffn_W': _L0_ffn_in['W'], 'L0_ffn_bias': _L0_ffn_in['bias'], 'L0_ffn_lora_weights': _L0_ffn_in['lora_weights'], 'L1_cond_W0': _L1_cond_in['W0'], 'L1_cond_b0': _L1_cond_in['b0'], 'L1_cond_W1': _L1_cond_in['W1'], 'L1_cond_b1': _L1_cond_in['b1'], 'L1_cond_W2': _L1_cond_in['W2'], 'L1_cond_b2': _L1_cond_in['b2'], 'L1_cond_weight': _L1_cond_in['weight'], 'L1_cond_bias_k': _L1_cond_in['bias_k'], 'L1_ffn_W_base': _L1_ffn_in['W_base'], 'L1_ffn_b_base': _L1_ffn_in['b_base'], 'L1_ffn_W_router': _L1_ffn_in['W_router'], 'L1_ffn_b_router': _L1_ffn_in['b_router'], 'L1_ffn_lora_A': _L1_ffn_in['lora_A'], 'L1_ffn_lora_B': _L1_ffn_in['lora_B'], 'L2_cond_W0': _L2_cond_in['W0'], 'L2_cond_b0': _L2_cond_in['b0'], 'L2_cond_W1': _L2_cond_in['W1'], 'L2_cond_b1': _L2_cond_in['b1'], 'L2_cond_W2': _L2_cond_in['W2'], 'L2_cond_b2': _L2_cond_in['b2'], 'L2_cond_weight': _L2_cond_in['weight'], 'L2_cond_bias_k': _L2_cond_in['bias_k'], 'L2_ffn_gate_w': _L2_ffn_in['gate_w'], 'L2_ffn_gate_b': _L2_ffn_in['gate_b'], 'L2_ffn_w1': _L2_ffn_in['w1'], 'L2_ffn_b1': _L2_ffn_in['b1'], 'L2_ffn_w2': _L2_ffn_in['w2'], 'L2_ffn_b2': _L2_ffn_in['b2'], 'L3_cond_W0': _L3_cond_in['W0'], 'L3_cond_b0': _L3_cond_in['b0'], 'L3_cond_W1': _L3_cond_in['W1'], 'L3_cond_b1': _L3_cond_in['b1'], 'L3_cond_W2': _L3_cond_in['W2'], 'L3_cond_b2': _L3_cond_in['b2'], 'L3_cond_weight': _L3_cond_in['weight'], 'L3_cond_bias_k': _L3_cond_in['bias_k'], 'L3_ffn_weight': _L3_ffn_in['weight'], 'L3_ffn_weight_scale': _L3_ffn_in['weight_scale'], 'L3_ffn_bias': _L3_ffn_in['bias']}

def reference(x, cond_128, fside_S_0, L0_cond_weight, L0_cond_c_weight, L0_ffn_lora_A, L0_ffn_lora_B, L0_ffn_W, L0_ffn_bias, L0_ffn_lora_weights, L1_cond_W0, L1_cond_b0, L1_cond_W1, L1_cond_b1, L1_cond_W2, L1_cond_b2, L1_cond_weight, L1_cond_bias_k, L1_ffn_W_base, L1_ffn_b_base, L1_ffn_W_router, L1_ffn_b_router, L1_ffn_lora_A, L1_ffn_lora_B, L2_cond_W0, L2_cond_b0, L2_cond_W1, L2_cond_b1, L2_cond_W2, L2_cond_b2, L2_cond_weight, L2_cond_bias_k, L2_ffn_gate_w, L2_ffn_gate_b, L2_ffn_w1, L2_ffn_b1, L2_ffn_w2, L2_ffn_b2, L3_cond_W0, L3_cond_b0, L3_cond_W1, L3_cond_b1, L3_cond_W2, L3_cond_b2, L3_cond_weight, L3_cond_bias_k, L3_ffn_weight, L3_ffn_weight_scale, L3_ffn_bias):
    import jax
    import jax.numpy as jnp

    def _L0_cond_ref(x, c, weight, c_weight, bias):
        import jax, jax.numpy as jnp
        import numpy as np
        from jax import lax
        N, C_IN, L = (32, 32, 512)
        C_OUT, K, GROUPS = (32, 9, 4)
        C_DIM, PAD, STRIDE = (128, 4, 1)
        out = lax.conv_general_dilated(x, weight, window_strides=(STRIDE,), padding=[(PAD, PAD)], dimension_numbers=('NCH', 'OIH', 'NCH'), feature_group_count=GROUPS)
        ctx = jnp.einsum('nd,od->no', c, c_weight)
        out = out + ctx[:, :, None] + bias[None, :, None]
        return out

    def _L0_ffn_ref(x, lora_A, lora_B, W, bias, lora_weights):
        import jax, jax.numpy as jnp
        import numpy as np
        B_, S, D_IN, D_OUT = (4, 256, 512, 512)
        N, RANK, ALPHA = (8, 16, 32)
        SCALE = ALPHA / RANK
        h = jnp.einsum('bsd,nrd->nbsr', x, lora_A)
        coef = (SCALE * lora_weights)[:, None, None]
        lora_out = jnp.einsum('nbsr,nor->bso', h, lora_B * coef)
        base = jnp.einsum('bsd,od->bso', x, W) + bias
        return base + lora_out

    def _L1_cond_ref(x, embedding, W0, b0, W1, b1, W2, b2, weight, bias_k):
        import jax, jax.numpy as jnp
        import numpy as np
        K = 8
        T = 1.0
        D_EMBD = 128
        IN_C = 32
        OUT_C = 32
        BS = 32
        H = 512
        HID = 128
        h = jax.nn.gelu(embedding @ W0 + b0, approximate=False)
        h = jax.nn.gelu(h @ W1 + b1, approximate=False)
        att = jax.nn.softmax((h @ W2 + b2) / T, axis=-1)
        agg_w = jnp.einsum('bk,koi->boi', att, weight[..., 0])
        agg_b = att @ bias_k
        out = jnp.einsum('boi,bih->boh', agg_w, x) + agg_b[:, :, None]
        return out

    def _L1_ffn_ref(x, W_base, b_base, W_router, b_router, lora_A, lora_B):
        import jax, jax.numpy as jnp
        import numpy as np

        def sparsemax(z):
            E = z.shape[-1]
            z_sorted = -jnp.sort(-z, axis=-1)
            z_cum = jnp.cumsum(z_sorted, axis=-1)
            k = jnp.arange(1, E + 1, dtype=z.dtype)
            support = 1.0 + k * z_sorted > z_cum
            k_z = jnp.sum(support, axis=-1, keepdims=True)
            tau_sum = jnp.take_along_axis(z_cum, k_z.astype(jnp.int32) - 1, axis=-1)
            tau = (tau_sum - 1.0) / k_z.astype(z.dtype)
            return jnp.maximum(z - tau, 0.0)
        base_out = jnp.einsum('bsd,od->bso', x, W_base) + b_base
        logits = jnp.einsum('bsd,ed->bse', x, W_router) + b_router
        weights = sparsemax(logits)
        h = jnp.einsum('bsd,edr->bser', x, lora_A)
        expert_out = jnp.einsum('bser,bse,ero->bso', h, weights, lora_B)
        return base_out + expert_out

    def _L2_cond_ref(x, embedding, W0, b0, W1, b1, W2, b2, weight, bias_k):
        import jax, jax.numpy as jnp
        import numpy as np
        K = 8
        T = 1.0
        D_EMBD = 128
        IN_C = 32
        OUT_C = 32
        BS = 32
        H = 512
        HID = 128
        h = jax.nn.gelu(embedding @ W0 + b0, approximate=False)
        h = jax.nn.gelu(h @ W1 + b1, approximate=False)
        att = jax.nn.softmax((h @ W2 + b2) / T, axis=-1)
        agg_w = jnp.einsum('bk,koi->boi', att, weight[..., 0])
        agg_b = att @ bias_k
        out = jnp.einsum('boi,bih->boh', agg_w, x) + agg_b[:, :, None]
        return out

    def _L2_ffn_ref(h, gate_w, gate_b, w1, b1, w2, b2):
        import jax, jax.numpy as jnp
        import numpy as np
        B, S, D = (4, 256, 512)
        NUM_EXPERTS, TOP_K = (3, 2)

        def _expert_outputs(h, w1, b1, w2, b2):
            pre = jnp.einsum('bsd,edf->ebsf', h, w1) + b1[:, None, None, :]
            act = jnp.stack([jnp.tanh(pre[0]), jax.nn.gelu(pre[1], approximate=False), jax.nn.silu(pre[2])])
            return jnp.einsum('ebsf,efd->ebsd', act, w2) + b2[:, None, None, :]
        b, s, d = h.shape
        vision_len = int(s * 0.3)
        text_strength = jnp.mean(jnp.abs(h[:, vision_len:, :]), axis=(1, 2), keepdims=True)
        vision_strength = jnp.mean(jnp.abs(h[:, :vision_len, :]), axis=(1, 2), keepdims=True)
        modality_ratio = text_strength / (vision_strength + 1e-08)
        modality_ratio = jnp.broadcast_to(modality_ratio, (b, s, 1))
        router_input = jnp.concatenate([h, modality_ratio], axis=-1)
        gate_logits = router_input @ gate_w + gate_b
        gate_scores = jax.nn.softmax(gate_logits, axis=-1)
        top_val, top_idx = jax.lax.top_k(gate_scores, TOP_K)
        top_val = top_val / (jnp.sum(top_val, axis=-1, keepdims=True) + 1e-08)
        expert_out = _expert_outputs(h, w1, b1, w2, b2)
        moe_out = jnp.zeros_like(h)
        batch_idx = jnp.arange(b)
        for i in range(TOP_K):
            j = top_idx[:, 0, i]
            out_i = expert_out[j, batch_idx]
            moe_out = moe_out + top_val[..., i:i + 1] * out_i
        return moe_out

    def _L3_cond_ref(x, embedding, W0, b0, W1, b1, W2, b2, weight, bias_k):
        import jax, jax.numpy as jnp
        import numpy as np
        K = 8
        T = 1.0
        D_EMBD = 128
        IN_C = 32
        OUT_C = 32
        BS = 32
        H = 512
        HID = 128
        h = jax.nn.gelu(embedding @ W0 + b0, approximate=False)
        h = jax.nn.gelu(h @ W1 + b1, approximate=False)
        att = jax.nn.softmax((h @ W2 + b2) / T, axis=-1)
        agg_w = jnp.einsum('bk,koi->boi', att, weight[..., 0])
        agg_b = att @ bias_k
        out = jnp.einsum('boi,bih->boh', agg_w, x) + agg_b[:, :, None]
        return out

    def _L3_ffn_ref(x, weight, weight_scale, bias):
        import jax, jax.numpy as jnp
        import numpy as np

        def _simulate_fp8_e4m3(w):
            return w.astype(jnp.float8_e4m3fn).astype(jnp.float32)
        out_dtype = x.dtype
        w_deq = (weight * weight_scale).astype(out_dtype)
        out = jnp.einsum('bsi,oi->bso', x, w_deq)
        out = out + bias.astype(out_dtype)
        return out.astype(out_dtype)
    x = x + _L0_ffn_ref(_L0_cond_ref(x, cond_128, L0_cond_weight, L0_cond_c_weight, fside_S_0), L0_ffn_lora_A, L0_ffn_lora_B, L0_ffn_W, L0_ffn_bias, L0_ffn_lora_weights)
    x = x + _L1_ffn_ref(_L1_cond_ref(x, cond_128, L1_cond_W0, L1_cond_b0, L1_cond_W1, L1_cond_b1, L1_cond_W2, L1_cond_b2, L1_cond_weight, L1_cond_bias_k), L1_ffn_W_base, L1_ffn_b_base, L1_ffn_W_router, L1_ffn_b_router, L1_ffn_lora_A, L1_ffn_lora_B)
    x = x + _L2_ffn_ref(_L2_cond_ref(x, cond_128, L2_cond_W0, L2_cond_b0, L2_cond_W1, L2_cond_b1, L2_cond_W2, L2_cond_b2, L2_cond_weight, L2_cond_bias_k), L2_ffn_gate_w, L2_ffn_gate_b, L2_ffn_w1, L2_ffn_b1, L2_ffn_w2, L2_ffn_b2)
    x = x + _L3_ffn_ref(_L3_cond_ref(x, cond_128, L3_cond_W0, L3_cond_b0, L3_cond_W1, L3_cond_b1, L3_cond_W2, L3_cond_b2, L3_cond_weight, L3_cond_bias_k), L3_ffn_weight, L3_ffn_weight_scale, L3_ffn_bias)
    return x

_drawn_inputs = setup_inputs


def setup_inputs(seed=0):
    import zlib

    import numpy as np

    out = dict(_drawn_inputs(seed))
    spreads = {'L0_ffn_lora_weights': (0.125, 0.2),
     'L1_cond_b0': (0.0, 0.431),
     'L1_cond_b1': (0.0, 0.289),
     'L1_cond_b2': (0.0, 0.1),
     'L1_ffn_b_router': (0.0, 0.8),
     'L1_ffn_lora_B': (0.0, 0.1),
     'L2_cond_b0': (0.0, 2.0),
     'L2_cond_b1': (0.0, 0.495),
     'L2_cond_b2': (0.0, 0.561),
     'L2_ffn_gate_b': (0.0, 0.745),
     'L2_ffn_b1': (0.0, 2.0),
     'L2_ffn_b2': (0.0, 0.8),
     'L3_cond_b0': (0.0, 0.8),
     'L3_cond_b1': (0.0, 0.8),
     'L3_cond_b2': (0.0, 0.623)}
    factors = {'L0_ffn_bias': 64.0,
     'L1_cond_bias_k': 8.0,
     'L1_ffn_b_base': 45.686,
     'L2_cond_bias_k': 22.829,
     'L3_cond_bias_k': 63.541,
     'L3_ffn_bias': 64.0}
    for name, (base, spread) in spreads.items():
        noise = np.random.default_rng([zlib.crc32(name.encode()), seed]).standard_normal(out[name].shape)
        drawn = base * np.exp(spread * noise) if base else spread * noise
        out[name] = jnp.asarray(drawn.astype(out[name].dtype))
    for name, factor in factors.items():
        out[name] = (out[name] * factor).astype(out[name].dtype)
    return out
```

```python
from contextlib import ExitStack

import concourse.bass as bass
from concourse import mybir

F32 = mybir.dt.float32
F32R = mybir.dt.float32r
ALU = mybir.AluOpType
ACT = mybir.ActivationFunctionType
AX = mybir.AxisListType

P = 128
B, S, D = 64, 32, 512
ROWS = B * S
TB = P // S
TILES = ROWS // P
GT = 2
GROUPS = TILES // GT
GR = GT * P
C = D // P
KM = 8
E1, R1 = 8, 16
E2 = 3
VIS = int(S * 0.3)
PH = 4
HALF = D // 2
WA, WB = HALF + E1 * R1, HALF + E1
GM = 72
AGG = S * S + S
NET_IN, LORA_IN, CONST_IN = 10, 3, 10
PAIRS = (GROUPS - 2) // 2
FIRST = 2
EV2 = 2 * (E2 + 1)
CHAIN0, CHAIN1, CHAIN2 = 4, 14, 17


class Group:

    def __init__(self, L, i, j):
        self.L, self.i, self.j = L, i, j
        self.g = 2 * i + j
        self.tiles = 2 * GROUPS * L + GT * self.g
        self.outs = {0: 2 * self.g, 1: 2 * GROUPS + 2 * self.g, 2: 4 * GROUPS + EV2 * self.g,
                     3: (4 + EV2) * GROUPS + 2 * self.g}[L]

    def later(self, by):
        i, j = self.i + (self.j + by) // 2, (self.j + by) % 2
        if isinstance(i, int) and i >= GROUPS // 2:
            return Group(self.L + 1, i - GROUPS // 2, j) if self.L < 3 else None
        return Group(self.L, i, j)

    def rows(self, tt):
        return GT * self.g + tt

    def x_count(self, tt):
        return self.outs + (EV2 - 2 if self.L == 2 else 0) + tt + 1 + FIRST


def build(nc, t):
    out_v = t["out"].rearrange("(g t p) d -> g p t d", t=GT, p=P)
    x_v = t["x"].rearrange("(g t p) d -> g p t d", t=GT, p=P)
    mix_d = nc.dram_tensor("mix_scratch", [3, B, S * S], F32, kind="Internal").ap()
    rowbias_d = nc.dram_tensor("rowbias_scratch", [4, ROWS], F32, kind="Internal").ap()

    with ExitStack() as ctx:
        def sb(name, shape, dt=F32, where=None):
            return (where or ctx).enter_context(nc.sbuf_tensor(name, shape, dt))

        def sem(name):
            return ctx.enter_context(nc.semaphore(name))

        x = sb("x_rows", [P, TILES, D])
        w0h, w0l = sb("w0_hi", [P, C, D], F32R), sb("w0_lo", [P, C, D], F32R)
        l1h, l1l = sb("l1_hi", [P, C, WA + WB], F32R), sb("l1_lo", [P, C, WA + WB], F32R)
        w5h, w5l = sb("w2e1_hi", [P, C, D], F32R), sb("w2e1_lo", [P, C, D], F32R)
        lbh, lbl = sb("lora_b1_hi", [P, D], F32R), sb("lora_b1_lo", [P, D], F32R)
        gwh, gwl = sb("gate_hi", [P, C, GM], F32R), sb("gate_lo", [P, C, GM], F32R)
        b2s = sb("b2_split", [96, D], F32R)
        stage = [sb(f"stage{k}", [P, 2 * D]) for k in range(2)]
        conv_w = sb("conv_w", [P, 3, P])
        xs = sb("x_mix", [P, GT * TB, P + 2])
        mix = [sb(f"mix{k}", [P, GT, P]) for k in range(2)]
        rowbias = [sb(f"rowbias{k}", [P, GR]) for k in range(2)]
        cf = sb("cond_f32", [P, GT, C, P])
        ch = [sb(f"cond_hi{k}", [P, C, GR], F32R) for k in range(2)]
        cl = [sb(f"cond_lo{k}", [P, C, GR], F32R) for k in range(2)]
        biasrow = sb("ffn_bias", [P, D])
        af = sb("act_f32", [P, 2, 2, GR])
        ah = [sb(f"act_hi{k}", [P, C, GR], F32R) for k in range(2)]
        al = [sb(f"act_lo{k}", [P, C, GR], F32R) for k in range(2)]
        by_tile = "p (t r) -> p t r"
        hs = af[:, 0, 0, :].rearrange(by_tile, t=GT)
        hth, htl = (al[0][:, k, :].rearrange(by_tile, t=GT) for k in range(2))
        ident, token0, ones = sb("ident", [P, P]), sb("token0", [P, P]), sb("ones", [P, P])
        ranks8, brouter = sb("ranks8", [P, E1]), sb("brouter", [P, E1])
        b1c = sb("b1_cols", [P, E2 * C])
        gate_tail = sb("gate_tail", [E2, 2])
        wscale = sb("l3_scale", [P, 1])
        sz = sb("sparsemax", [P, GT, 8, E1])
        sc = sb("sparsemax_scalars", [P, GT, 4])
        absum = sb("abs_sums", [P, 2, GT * TB])
        ratio = sb("ratio", [E2, 3, GT * TB])
        gl = sb("gate_logits", [E2, 2, GR])
        g3 = sb("gate_scores", [P, 6, GT, E2])
        g1 = sb("gate_scalars", [P, 16, GT])
        top = sb("gate_top", [P, 2, GT, E2])
        coef = sb("coef", [P, GT, E2])
        coef96 = sb("coef_split", [P, GT, 96])
        coefT = sb("coef_t", [96, GR], F32R)

        ps = [ctx.enter_context(nc.psum_tensor(f"bank{k}", [P, D], F32)) for k in range(8)]
        OUT = (2, 4)
        SIDE = (3, 5)

        nets_in, lora_in, const_in, phase_in = sem("nets_in"), sem("lora_in"), sem("const_in"), sem("phase_in")
        stage_in = [sem(f"stage_in{k}") for k in range(2)]
        rowbias_in = [sem(f"rowbias_in{k}") for k in range(2)]
        mix_in = [sem(f"mix_in{k}") for k in range(2)]
        x_in = [sem(f"x_in{k}") for k in range(2)]
        biasrow_in = sem("biasrow_in")
        ctx_out, agg_out = sem("ctx_out"), sem("agg_out")
        y_out = [sem(f"y_out{k}") for k in range(2)]
        net_mm, agg_mm, lora_mm, cond_mm = sem("net_mm"), sem("agg_mm"), sem("lora_mm"), sem("cond_mm")
        main_mm, ht_mm, out_mm = sem("main_mm"), sem("ht_mm"), sem("out_mm")
        gate_mm, gatet_mm, top_mm, coeft_mm, pre_mm = (sem("gate_mm"), sem("gatet_mm"), sem("top_mm"),
                                                       sem("coeft_mm"), sem("pre_mm"))
        net_act, w_hi, small_hi, c_hi, xs_copy = (sem("net_act"), sem("w_hi"), sem("small_hi"), sem("c_hi"),
                                                  sem("xs_copy"))
        agg_act, ht_hi, act_f, act_hi = sem("agg_act"), sem("ht_hi"), sem("act_f"), sem("act_hi")
        gate_exp, coeft_copy = sem("gate_exp"), sem("coeft_copy")
        net_dve, agg_dve, chain, w_sum, w_lo = sem("net_dve"), sem("agg_dve"), sem("chain"), sem("w_sum"), sem("w_lo")
        c_sum, hs_done, ht_lo, abs_done = sem("c_sum"), sem("hs_done"), sem("ht_lo"), sem("abs_done")
        logit_done, gate_sub, top_done, coef_done, x_new = (sem("logit_done"), sem("gate_sub"), sem("top_done"),
                                                            sem("coef_done"), sem("x_new"))
        zeroed, c_lo, xb_done, act_lo = sem("zeroed"), sem("c_lo"), sem("xb_done"), sem("act_lo")

        def halves(src, h, l):
            return [(src[:, 2 * k:2 * k + 2, :], 2, D, h[:, 2 * k:2 * k + 2, 0:D], l[:, 2 * k:2 * k + 2, 0:D])
                    for k in range(2)]

        flat = "p (c n) -> p c n"
        setup_pieces = halves(t["w0T"], w0h, w0l)
        setup_pieces += [(t["l1w"][:, c:c + 1, :], 1, WA + WB, l1h[:, c:c + 1, :], l1l[:, c:c + 1, :])
                         for c in range(C)]
        setup_pieces += [(t["lora_b1"].rearrange(flat, c=1), 1, D, lbh[:, :].rearrange(flat, c=1),
                          lbl[:, :].rearrange(flat, c=1))]
        N_L1 = len(setup_pieces)
        N_W1 = N_L1 + 2 * E2
        N_E1, N_E0, N_E2, N_L3 = N_W1 + 2, N_W1 + 4, N_W1 + 6, N_W1 + 8

        def staged(n, piece):
            return stage[n % 2][:, 0:piece[1] * piece[2]].rearrange(flat, c=piece[1])

        def load_piece(sp, n, par, piece):
            if not isinstance(n, int) or n >= 2:
                sp.wait_ge(w_lo, n - 1)
            sp.dma_start(staged(par, piece), piece[0]).then_inc(stage_in[par], 16)

        def split_hi(act, n, par, nth, piece, scaled=False):
            act.wait_ge(stage_in[par], 16 * nth)
            act.activation(piece[3], staged(par, piece), ACT.Copy,
                           scale=wscale[:, 0:1] if scaled else 1.0).then_inc(w_hi, 1)

        def split_lo(dve, n, par, piece, scaled=False):
            dve.wait_ge(w_hi, n + 1)
            if scaled:
                dve.scalar_tensor_tensor(out=piece[4], in0=staged(par, piece), scalar=wscale[:, 0:1],
                                         in1=piece[3].bitcast(F32), op0=ALU.mult,
                                         op1=ALU.subtract).then_inc(w_lo, 1)
            else:
                dve.tensor_tensor(piece[4], staged(par, piece), piece[3].bitcast(F32),
                                  ALU.subtract).then_inc(w_lo, 1)

        def cond_view(bank):
            return ps[bank][:, :].rearrange(flat, c=C)

        THREE = ((1, 0), (0, 1), (0, 0))

        def cond(pe, G, tt, first=False):
            if not first:
                pe.wait_ge(c_sum, G.tiles + tt + 1 - GT)
            if G.L == 0:
                pe.wait_ge(phase_in, 16 * (G.g + 1))
                dst = ps[tt][:, :].rearrange("p (c b o) -> p c b o", c=PH, b=TB)
                for b in range(TB):
                    for tap in range(3):
                        mm = pe.matmul(dst[:, :, b, :], xs[:, TB * tt + b, tap:tap + P],
                                       conv_w[:, tap, :].rearrange("k (c o) -> k c o", c=PH),
                                       start=(tap == 0), stop=(tap == 2))
            else:
                pe.wait_ge(mix_in[G.j], 16 * TB * (GROUPS // 2 * (G.L - 1) + G.i + 1))
                pe.wait_ge(xs_copy, G.tiles - 2 * GROUPS + tt + 1)
                for c in range(C):
                    mm = pe.matmul(ps[tt][:, c * P:(c + 1) * P], x_tile(tt)[:, c * P:(c + 1) * P],
                                   mix[G.j][:, tt, :], start=True, stop=True)
            mm.then_inc(cond_mm, 1)

        def x_tile(tt):
            return xs[:, TB * tt:TB * (tt + 1), :].rearrange("p b m -> p (b m)")[:, 0:D]

        def cond_ready(pe, G, tt):
            pe.wait_ge(c_lo, G.tiles + tt + 1)

        def out_free(pe, n):
            pe.wait_ge(x_new, n)

        def dense(pe, G, tt, wh, wl):
            cond_ready(pe, G, tt)
            out_free(pe, G.outs + tt + 1)
            for c in range(C):
                for a, w in THREE:
                    mm = pe.matmul(ps[OUT[tt]][:, :], (ch, cl)[a][G.j][:, c, tt * P:(tt + 1) * P],
                                   (wh, wl)[w][:, c, 0:D], start=(c == 0 and (a, w) == THREE[0]),
                                   stop=(c == C - 1 and (a, w) == THREE[-1]))
            mm.then_inc(out_mm, 1)

        def l1_main(pe, G, tt):
            cond_ready(pe, G, tt)
            out_free(pe, G.outs + tt + 1)
            for c in range(C):
                for a, w in THREE:
                    lhs = (ch, cl)[a][G.j][:, c, tt * P:(tt + 1) * P]
                    for bank, lo, hi in ((OUT[tt], 0, WA), (SIDE[tt], WA, WA + WB)):
                        mm = pe.matmul(ps[bank][:, 0:hi - lo], lhs, (l1h, l1l)[w][:, c, lo:hi],
                                       start=(c == 0 and (a, w) == THREE[0]),
                                       stop=(c == C - 1 and (a, w) == THREE[-1]))
            mm.then_inc(main_mm, 1)

        def l1_turn(pe, G, tt):
            pe.wait_ge(hs_done, GT * G.g + tt + 1)
            pe.transpose(ps[6 + tt][:, 0:P], hs[:, tt, :], ident[:, :]).then_inc(ht_mm, 1)

        def l1_adapt(pe, G, tt):
            pe.wait_ge(ht_lo, GT * G.g + tt + 1)
            for a, w in THREE:
                for bank, lo in ((OUT[tt], 0), (SIDE[tt], HALF)):
                    mm = pe.matmul(ps[bank][:, 0:HALF], (hth, htl)[a][:, tt, :], (lbh, lbl)[w][:, lo:lo + HALF],
                                   start=False, stop=True, skip_group_check=True)
            mm.then_inc(out_mm, 1)

        def gate_logits(pe, G):
            cond_ready(pe, G, GT - 1)
            for c in range(C):
                for a, w in THREE:
                    pe.matmul(ps[6][0:GM, 0:GR], (gwh, gwl)[a][:, c, :], (ch, cl)[w][G.j][:, c, :],
                              start=(c == 0 and (a, w) == THREE[0]),
                              stop=(c == C - 1 and (a, w) == THREE[-1]))
            pe.wait_ge(abs_done, GT * (G.g + 1))
            pe.matmul(ps[6][:, GR:GR + 2 * GT * TB], ones[:, :], absum[:, :, :].rearrange("p k b -> p (k b)"),
                      start=True, stop=True).then_inc(gate_mm, 1)

        def gate_turn(pe, G):
            pe.wait_ge(logit_done, G.g + 1)
            for tt in range(GT):
                mm = pe.matmul(ps[7][:, 4 * tt:4 * tt + E2], gl[:, 1, tt * P:(tt + 1) * P], ident[0:E2, 0:E2],
                               start=True, stop=True)
            mm.then_inc(gatet_mm, 1)

        def gate_top(pe, G):
            pe.wait_ge(top_done, G.g + 1)
            pe.matmul(ps[6][:, 0:2 * GT * E2], token0[:, :], top[:, :, :, :].rearrange("p k t e -> p (k t e)"),
                      start=True, stop=True).then_inc(top_mm, 1)

        def coef_turn(pe, G):
            pe.wait_ge(coef_done, G.g + 1)
            for tt in range(GT):
                mm = pe.transpose(ps[7][0:96, tt * P:(tt + 1) * P], coef96[:, tt, :], ident[:, :])
            mm.then_inc(coeft_mm, 1)

        def expert_in(pe, G, e):
            for k in range(2):
                n = 2 * E2 * G.g + 2 * e + k + 1
                pe.wait_ge(act_f, n)
                for f in (2 * k, 2 * k + 1):
                    for c in range(C):
                        for a, w in THREE:
                            mm = pe.matmul(ps[SIDE[k]][:, (f % 2) * GR:(f % 2 + 1) * GR],
                                           (w1h, w1l)[a][:, e, c, f * P:(f + 1) * P], (ch, cl)[w][G.j][:, c, :],
                                           start=(c == 0 and (a, w) == THREE[0]),
                                           stop=(c == C - 1 and (a, w) == THREE[-1]))
                mm.then_inc(pre_mm, 1)

        def expert_out(pe, G, e):
            buf = (3 * G.j + e) % 2
            pe.wait_ge(act_lo, 2 * E2 * G.g + 2 * e + 2 + FIRST)
            pe.wait_ge(w_lo, (N_E0, N_E1, N_E2)[e])
            wh, wl = ((w0h, w0l), (w5h, w5l), (l1h, l1l))[e]
            for tt in range(GT):
                out_free(pe, G.outs + EXPERT_EV[e] + tt + 1)
                for c in range(C):
                    for a, w in THREE:
                        mm = pe.matmul(ps[OUT[tt]][:, :], (ah, al)[a][buf][:, c, tt * P:(tt + 1) * P],
                                       (wh, wl)[w][:, c, 0:D], start=(c == 0 and (a, w) == THREE[0]),
                                       stop=(c == C - 1 and (a, w) == THREE[-1]))
                mm.then_inc(out_mm, 1)

        def expert_bias(pe, G):
            pe.wait_ge(coeft_copy, G.g + 1)
            for tt in range(GT):
                out_free(pe, G.outs + BIAS_EV + tt + 1)
                pe.matmul(ps[OUT[tt]][:, :], coefT[:, tt * P:(tt + 1) * P], b2s[:, :],
                          start=True, stop=True).then_inc(out_mm, 1)

        EXPERT_EV, BIAS_EV = (0, 4, 6), 2

        def cond_hi(act, G, tt):
            act.wait_ge(c_sum, G.tiles + tt + 1)
            act.activation(ch[G.j][:, :, tt * P:(tt + 1) * P], cf[:, tt, :, :], ACT.Copy).then_inc(c_hi, 1)

        def copy_x(act, G, tt, before):
            act.wait_ge(cond_mm, before.tiles + tt + 1)
            act.wait_ge(x_new, Group(G.L - 1, G.i, G.j).x_count(tt))
            act.activation(x_tile(tt), x[:, G.rows(tt), :], ACT.Copy).then_inc(xs_copy, 1)

        def ahead_act(act, G):
            n1, n2 = G.later(1), G.later(2)
            for tt in range(GT):
                if n1:
                    cond_hi(act, n1, tt)
                if n2 and n2.L:
                    copy_x(act, n2, tt, n1)

        def expert_act(act, G, e):
            buf = (3 * G.j + e) % 2
            for k in range(2):
                n = 2 * E2 * G.g + 2 * e + k + 1
                act.wait_ge(pre_mm, n)
                act.wait_ge(act_lo, n)
                for f in range(2):
                    a = act.activation(af[:, k, f, :], ps[SIDE[k]][:, f * GR:(f + 1) * GR],
                                       (ACT.Tanh, ACT.Gelu, ACT.Silu)[e],
                                       bias=b1c[:, e * C + 2 * k + f:e * C + 2 * k + f + 1])
                a.then_inc(act_f, 1)
                act.wait_ge(out_mm, G.outs + (-2, 0, 2)[e])
                act.wait_ge(act_f, n + FIRST)
                act.activation(ah[buf][:, 2 * k:2 * k + 2, :], af[:, k, :, :], ACT.Copy).then_inc(act_hi, 1)

        def linker(dve, base):
            n = [0]

            def link(ins):
                n[0] += 1
                ins.then_inc(chain, 1)
                dve.wait_ge(chain, base + n[0])
            return link, n

        def cond_sum(dve, G, tt, first=False):
            dve.wait_ge(rowbias_in[G.j], 16 * (GROUPS // 2 * G.L + G.i + 1))
            dve.wait_ge(cond_mm, G.tiles + tt + 1)
            if not first:
                dve.wait_ge(c_lo, G.tiles + tt + 1 - GT)
            dve.tensor_tensor(cf[:, tt, :, :], cond_view(tt),
                              rowbias[G.j][:, tt * P:(tt + 1) * P].unsqueeze(1).to_broadcast([P, C, P]),
                              ALU.add).then_inc(c_sum, 1)
            if G.L == 2:
                dve.wait_ge(c_sum, G.tiles + tt + 1)
                v = cf[:, tt, :, :].rearrange("p c (b r) -> p b c r", b=TB)
                for k, (lo, hi) in enumerate(((0, VIS), (VIS, S))):
                    r = dve.tensor_reduce(absum[:, k, tt * TB:(tt + 1) * TB], v[:, :, :, lo:hi], AX.XY, ALU.add,
                                          apply_absolute_value=True)
                r.then_inc(abs_done, 1)

        def ahead_dve(dve, G):
            n1 = G.later(1)
            if n1:
                for tt in range(GT):
                    cond_sum(dve, n1, tt)

        def add_out(dve, G, tt):
            dve.wait_ge(xb_done, GROUPS * min(G.L, 2) + G.g + 1)
            dve.wait_ge(out_mm, G.outs + tt + 1)
            row = x[:, G.rows(tt), :]
            if G.L == 1:
                dve.tensor_tensor(row[:, 0:HALF], ps[OUT[tt]][:, 0:HALF], row[:, 0:HALF], ALU.add)
                dve.tensor_tensor(row[:, HALF:D], ps[SIDE[tt]][:, 0:HALF], row[:, HALF:D], ALU.add)\
                   .then_inc(x_new, 1)
            else:
                dve.tensor_tensor(row, ps[OUT[tt]][:, :], row, ALU.add).then_inc(x_new, 1)

        def add_expert(dve, G, ev, e):
            for tt in range(GT):
                n = G.outs + ev + tt + 1
                dve.wait_ge(out_mm, n)
                dve.wait_ge(x_new, n)
                row = x[:, G.rows(tt), :]
                if e is None:
                    dve.tensor_tensor(row, ps[OUT[tt]][:, :], row, ALU.add).then_inc(x_new, 1)
                else:
                    dve.scalar_tensor_tensor(out=row, in0=ps[OUT[tt]][:, :], scalar=coef[:, tt, e:e + 1], in1=row,
                                             op0=ALU.mult, op1=ALU.add).then_inc(x_new, 1)

        def router(dve, G, tt, link):
            z, zs, cum, kz, sup, kk, w, one = (sz[:, tt, k, :] for k in range(8))
            count, total, inv, tau = (sc[:, tt, k:k + 1] for k in range(4))
            dve.wait_ge(main_mm, GT * G.g + tt + 1)
            link(dve.tensor_tensor(z, ps[SIDE[tt]][:, HALF:HALF + E1], brouter[:, :], ALU.add))
            dve.memset(sc[:, tt, :], 0.0)
            link(dve.max(zs, z))
            dve.tensor_tensor(kz, zs, ranks8[:, :], ALU.mult)
            link(dve.tensor_tensor_scan(cum, ones[:, 0:E1], zs, 0.0, ALU.mult, ALU.add))
            link(dve.scalar_tensor_tensor(out=sup, in0=kz, scalar=1.0, in1=cum, op0=ALU.add, op1=ALU.is_gt,
                                          accum_out=count))
            dve.scalar_tensor_tensor(out=kk, in0=ranks8[:, :], scalar=count, in1=cum, op0=ALU.is_equal,
                                     op1=ALU.mult, accum_out=total)
            link(dve.reciprocal(inv, count))
            link(dve.tensor_scalar(tau, total, -1.0, inv, ALU.add, ALU.mult))
            link(dve.tensor_scalar(w, z, tau, 0.0, ALU.subtract, ALU.max))
            dve.tensor_tensor(hs[:, tt, :].rearrange("p (e r) -> p e r", e=E1),
                              ps[OUT[tt]][:, HALF:WA].rearrange("p (e r) -> p e r", e=E1),
                              w.unsqueeze(2).to_broadcast([P, E1, R1]), ALU.mult).then_inc(hs_done, 1)

        def turned_lo(dve, G, tt):
            dve.wait_ge(ht_hi, GT * G.g + tt + 1)
            dve.tensor_tensor(htl[:, tt, :], ps[6 + tt][:, 0:P], hth[:, tt, :].bitcast(F32), ALU.subtract)\
               .then_inc(ht_lo, 1)

        def gate_ratio(dve, G, link):
            dve.wait_ge(gate_mm, G.g + 1)
            vis, text = (ps[6][0:E2, GR + k * GT * TB:GR + (k + 1) * GT * TB] for k in range(2))
            dve.tensor_scalar(gl[:, 0, :], ps[6][0:E2, 0:GR], gate_tail[:, 1:2], None, ALU.add)
            link(dve.tensor_scalar(ratio[:, 0, :], vis, 1.0 / (VIS * D), 1e-8, ALU.mult, ALU.add))
            link(dve.reciprocal(ratio[:, 1, :], ratio[:, 0, :]))
            link(dve.scalar_tensor_tensor(out=ratio[:, 2, :], in0=text, scalar=1.0 / ((S - VIS) * D),
                                          in1=ratio[:, 1, :], op0=ALU.mult, op1=ALU.mult))
            by_batch = "e (b r) -> e b r"
            dve.scalar_tensor_tensor(out=gl[:, 1, :].rearrange(by_batch, r=S),
                                     in0=ratio[:, 2, :].unsqueeze(2).to_broadcast([E2, GT * TB, S]),
                                     scalar=gate_tail[:, 0:1], in1=gl[:, 0, :].rearrange(by_batch, r=S),
                                     op0=ALU.mult, op1=ALU.add).then_inc(logit_done, 1)

        def wide(v):
            return v.unsqueeze(2).to_broadcast([P, GT, E2])

        def gate_softmax(dve, G, link):
            dve.wait_ge(gatet_mm, G.g + 1)
            logits = ps[7][:, 0:4 * GT].rearrange("p (t e) -> p t e", t=GT)[:, :, 0:E2]
            link(dve.tensor_reduce(g1[:, 0, :], logits, AX.X, ALU.max))
            dve.tensor_tensor(g3[:, 0, :, :], logits, wide(g1[:, 0, :]), ALU.subtract).then_inc(gate_sub, 1)
            dve.wait_ge(gate_exp, G.g + 1)
            link(dve.tensor_reduce(g1[:, 1, :], g3[:, 1, :, :], AX.X, ALU.add))
            link(dve.reciprocal(g1[:, 2, :], g1[:, 1, :]))
            link(dve.tensor_tensor(g3[:, 2, :, :], g3[:, 1, :, :], wide(g1[:, 2, :]), ALU.mult))
            s0, s1, s2 = (g3[:, 2, :, e] for e in range(E2))
            dve.tensor_reduce(g1[:, 3, :], g3[:, 2, :, :], AX.X, ALU.max)
            dve.tensor_tensor(g1[:, 4, :], s0, s1, ALU.max)
            dve.tensor_tensor(g1[:, 5, :], s0, s1, ALU.min)
            dve.tensor_tensor(g1[:, 6, :], s0, s1, ALU.is_ge)
            dve.tensor_tensor(g1[:, 7, :], s0, s2, ALU.is_ge)
            link(dve.tensor_tensor(g1[:, 8, :], s1, s2, ALU.is_ge))
            dve.tensor_tensor(g1[:, 9, :], g1[:, 4, :], s2, ALU.min)
            dve.tensor_tensor(g3[:, 3, :, 0], g1[:, 6, :], g1[:, 7, :], ALU.add)
            dve.tensor_tensor(g1[:, 10, :], g1[:, 8, :], g1[:, 6, :], ALU.subtract)
            link(dve.tensor_tensor(g1[:, 11, :], g1[:, 7, :], g1[:, 8, :], ALU.add))
            dve.tensor_scalar(g3[:, 3, :, 1], g1[:, 10, :], 1.0, None, ALU.add)
            dve.tensor_tensor(g1[:, 12, :], g1[:, 5, :], g1[:, 9, :], ALU.max)
            link(dve.tensor_scalar(g3[:, 3, :, 2], g1[:, 11, :], -1.0, 2.0, ALU.mult, ALU.add))
            dve.tensor_scalar(top[:, 0, :, :], g3[:, 3, :, :], 2.0, None, ALU.is_equal)
            dve.tensor_scalar(top[:, 1, :, :], g3[:, 3, :, :], 1.0, None, ALU.is_equal).then_inc(top_done, 1)
            link(dve.tensor_tensor(g1[:, 13, :], g1[:, 3, :], g1[:, 12, :], ALU.add))
            link(dve.tensor_scalar(g1[:, 14, :], g1[:, 13, :], 1e-8, None, ALU.add))
            link(dve.reciprocal(g1[:, 15, :], g1[:, 14, :]))
            dve.tensor_tensor(g1[:, 0, :], g1[:, 3, :], g1[:, 15, :], ALU.mult)
            link(dve.tensor_tensor(g1[:, 1, :], g1[:, 12, :], g1[:, 15, :], ALU.mult))

        def gate_coef(dve, G, link):
            dve.wait_ge(top_mm, G.g + 1)
            ranked = ps[6][:, 0:2 * GT * E2].rearrange("p (k t e) -> p k t e", k=2, t=GT)
            dve.tensor_tensor(g3[:, 4, :, :], ranked[:, 0, :, :], wide(g1[:, 0, :]), ALU.mult)
            link(dve.tensor_tensor(g3[:, 5, :, :], ranked[:, 1, :, :], wide(g1[:, 1, :]), ALU.mult))
            link(dve.tensor_tensor(coef[:, :, :], g3[:, 4, :, :], g3[:, 5, :, :], ALU.add))
            dve.tensor_copy(coef96[:, :, 0:E2].bitcast(F32R), coef[:, :, :])
            link(dve.tensor_copy(coef96[:, :, 32:32 + E2].bitcast(F32R), coef[:, :, :]))
            dve.tensor_tensor(coef96[:, :, 64:64 + E2], coef[:, :, :], coef96[:, :, 32:32 + E2], ALU.subtract)\
               .then_inc(coef_done, 1)

        def cond_lo(pool, G, tt):
            pool.wait_ge(c_hi, G.tiles + tt + 1)
            pool.tensor_tensor(cl[G.j][:, :, tt * P:(tt + 1) * P], cf[:, tt, :, :],
                               ch[G.j][:, :, tt * P:(tt + 1) * P].bitcast(F32), ALU.subtract).then_inc(c_lo, 1)

        def add_bias(pool, G):
            if G.L == 0:
                pool.wait_ge(x_in[G.j], 16 * (G.i + 1))
            else:
                pool.wait_ge(xs_copy, G.tiles - 2 * GROUPS + GT)
            rows = x[:, bass.ds(G.rows(0), GT), :]
            pool.tensor_tensor(rows, rows, biasrow[:, :].unsqueeze(1).to_broadcast([P, GT, D]), ALU.add)\
                .then_inc(xb_done, 1)

        def ahead_pool(pool, G):
            n1 = G.later(1)
            if n1:
                for tt in range(GT):
                    cond_lo(pool, n1, tt)

        def load_rowbias(sp, G):
            src = rowbias_d[G.L].rearrange("(g a r) -> g a r", a=1, r=GR)
            src = src[bass.ds(G.g, 1), :, :].rearrange("g a r -> (g a) r").to_broadcast([P, GR])
            sp.dma_start(rowbias[G.j][:, :], src).then_inc(rowbias_in[G.j], 16)

        def load_mix(sp, G):
            src = mix_d[G.L - 1].rearrange("(g t b) (i o) -> g b i t o", t=GT, b=TB, i=S)
            for b in range(TB):
                sp.dma_start(mix[G.j][b * S:(b + 1) * S, :, b * S:(b + 1) * S],
                             src[bass.ds(G.g, 1), b].rearrange("g i t o -> (g i) t o")).then_inc(mix_in[G.j], 16)

        def load_x(sp, G):
            sp.dma_start(x[:, bass.ds(G.rows(0), GT), :],
                         x_v[bass.ds(G.g, 1)].rearrange("g p t d -> (g p) t d")).then_inc(x_in[G.j], 16)

        def load_phases(sp, G):
            src = t["phases"].rearrange("p (g b) m -> g p b m", g=GROUPS)
            sp.dma_start(xs[:, :, 1:1 + P], src[bass.ds(G.g, 1)].rearrange("g p b m -> (g p) b m"))\
              .then_inc(phase_in, 16)

        def store_y(sp, G):
            sp.wait_ge(x_new, G.x_count(GT - 1))
            sp.dma_start(out_v[bass.ds(G.g, 1)].rearrange("g p t d -> (g p) t d"),
                         x[:, bass.ds(G.rows(0), GT), :]).then_inc(y_out[G.j], 16)

        def prefetch(sp, G):
            n1, n2 = G.later(1), G.later(2)
            sp.wait_ge(cond_mm, G.tiles + GT)
            if n1 and n1.L == 0:
                load_phases(sp, n1)
            if n2 and n2.L:
                load_mix(sp, n2)
            if n2:
                sp.wait_ge(c_sum, G.tiles + GT)
                load_rowbias(sp, n2)
            if n2 and n2.L == 0:
                sp.wait_ge(x_in[G.j], 16 * (G.i + 1))
                load_x(sp, n2)

        def layer(eng, L, step):
            with eng.Fori(0, PAIRS) as i:
                for j in range(2):
                    step(Group(L, i, j))
            for j in range(2):
                step(Group(L, PAIRS, j))

        G0 = Group(0, 0, 0)

        with ExitStack() as tmp:
            condT = sb("cond_t", [P, B], where=tmp)
            cwT = sb("c_weight_t", [P, S], where=tmp)
            fside = sb("fside", [B, S], where=tmp)
            netw = sb("net_w", [P, 2, 3, P], where=tmp)
            netb = sb("net_b", [P, 2, 3], where=tmp)
            netw2 = sb("net_w2", [P, 3, KM], where=tmp)
            netb2 = sb("net_b2", [B, 3 * KM], where=tmp)
            kern = sb("mix_kernels", [KM, 3, AGG], where=tmp)
            hid = sb("net_hidden", [P, 2, 3, B], where=tmp)
            att = sb("att", [B, 4, 3, KM], where=tmp)
            attm = sb("att_stat", [B, 3, 3], where=tmp)
            attT = sb("att_t", [KM, 3, B], where=tmp)
            agg = sb("mixed", [B, 3, AGG], where=tmp)
            ctx0 = sb("ctx0", [B, S], where=tmp)
            loraA = sb("lora_a0", [P, C, P], where=tmp)
            loraB = sb("lora_b0", [P, D], where=tmp)
            loraw = sb("lora_w0", [P, 1], where=tmp)
            lbs = sb("lora_b0_scaled", [P, D], where=tmp)
            b2raw = sb("b2_raw", [96, D], where=tmp)
            gate_raw = sb("gate_raw", [P, C, E2], where=tmp)

            with nc.Block() as block:
                @block.sync
                def _(sp):
                    for dst, name in ((condT, "condT"), (cwT, "cwT"), (netw, "netw"), (netb, "netb"),
                                      (netw2, "netw2"), (kern, "kern"), (ident, "ident"), (conv_w, "conv_w")):
                        sp.dma_start(dst[:], t[name]).then_inc(nets_in, 16)
                    sp.dma_start(fside[:, :], t["fside"].to_broadcast([B, S])).then_inc(nets_in, 16)
                    sp.dma_start(netb2[:, :], t["netb2"].to_broadcast([B, 3 * KM])).then_inc(nets_in, 16)
                    for dst, name in ((loraA, "loraA"), (loraB, "loraB"), (loraw, "loraw")):
                        sp.dma_start(dst[:], t[name]).then_inc(lora_in, 16)
                    sp.wait_ge(zeroed, 1)
                    load_phases(sp, G0)
                    for n in range(2):
                        load_piece(sp, n, n, setup_pieces[n])
                    sp.wait_ge(net_dve, 1)
                    sp.dma_start(rowbias_d[0].rearrange("(b o) -> b o", o=S), ctx0[:, :]).then_inc(ctx_out, 16)
                    sp.dma_start(token0[:, :], t["token0"]).then_inc(const_in, 16)
                    sp.dma_start(ranks8[:, :], t["ranks8"].to_broadcast([P, E1])).then_inc(const_in, 16)
                    sp.dma_start(brouter[:, :], t["brouter"].to_broadcast([P, E1])).then_inc(const_in, 16)
                    sp.dma_start(b1c[:, :], t["b1c"]).then_inc(const_in, 16)
                    sp.dma_start(gate_tail[:, :], t["gate_tail"]).then_inc(const_in, 16)
                    sp.dma_start(wscale[:, :], t["wscale"].to_broadcast([P, 1])).then_inc(const_in, 16)
                    sp.dma_start(gate_raw[:, :, :], t["gate_w"]).then_inc(const_in, 16)
                    for k in range(3):
                        sp.dma_start(b2raw[32 * k:32 * k + E2, :], t["b2"]).then_inc(const_in, 16)
                    sp.wait_ge(ctx_out, 16)
                    for j in range(2):
                        load_rowbias(sp, Group(0, 0, j))
                    for j in range(2):
                        load_x(sp, Group(0, 0, j))
                    sp.dma_start(biasrow[:, :], t["bias0"].to_broadcast([P, D])).then_inc(biasrow_in, 16)
                    for n in range(2, N_L1):
                        load_piece(sp, n, n % 2, setup_pieces[n])
                    for L in range(3):
                        sp.wait_ge(agg_act, L + 1)
                        sp.wait_ge(agg_dve, L + 1)
                        sp.dma_start(mix_d[L], agg[:, L, 0:S * S]).then_inc(agg_out, 16)
                        sp.dma_start(rowbias_d[L + 1].rearrange("(b o) -> b o", o=S), agg[:, L, S * S:AGG])\
                          .then_inc(agg_out, 16)
                    sp.wait_ge(agg_out, 16 * 6)

                @block.gpsimd
                def _(pool):
                    pool.memset(xs[:, :, :], 0.0).then_inc(zeroed, 1)
                    for k in range(FIRST):
                        pool.memset(mix[k][:, :, :], 0.0).then_inc(act_lo, 1)
                    pool.memset(gwh[:, :, :].bitcast(F32), 0.0).then_inc(zeroed, 1)
                    pool.memset(gwl[:, :, :].bitcast(F32), 0.0).then_inc(zeroed, 1)
                    pool.memset(b2s[:, :].bitcast(F32), 0.0).then_inc(zeroed, 1)
                    pool.memset(ones[:, :], 1.0).then_inc(zeroed, 1)
                    pool.memset(coef96[:, :, :], 0.0).then_inc(zeroed, 1)
                    for tt in range(GT):
                        cond_lo(pool, G0, tt)

                @block.tensor
                def _(pe):
                    pe.wait_ge(nets_in, 16 * NET_IN)
                    pe.matmul(ps[3][0:B, 0:S], condT[:, :], cwT[:, :], start=True, stop=True).then_inc(net_mm, 1)
                    for L in range(3):
                        mm = pe.matmul(ps[2][:, B * L:B * L + B], netw[:, 0, L, :], condT[:, :], start=True, stop=True)
                    mm.then_inc(net_mm, 1)
                    for tt in range(GT):
                        cond(pe, G0, tt, first=True)
                    pe.wait_ge(net_act, 1)
                    for L in range(3):
                        mm = pe.matmul(ps[4][:, B * L:B * L + B], netw[:, 1, L, :], hid[:, 0, L, :],
                                       start=True, stop=True)
                    mm.then_inc(net_mm, 1)
                    pe.wait_ge(net_act, 2)
                    for L in range(3):
                        mm = pe.matmul(ps[5][0:B, KM * L:KM * (L + 1)], hid[:, 1, L, :], netw2[:, L, :],
                                       start=True, stop=True)
                    mm.then_inc(net_mm, 1)
                    pe.wait_ge(lora_in, 16 * LORA_IN)
                    pe.wait_ge(net_dve, 2)
                    for c in range(C):
                        if c == 2:
                            pe.wait_ge(w_sum, 1)
                        pe.matmul(ps[6 + c % 2][:, :], loraA[:, c, :], lbs[:, :], start=True, stop=True)\
                          .then_inc(lora_mm, 1)
                    pe.wait_ge(net_dve, 4)
                    for L in range(3):
                        mm = pe.transpose(ps[2][0:KM, B * L:B * (L + 1)], att[:, 3, L, :], ident[0:B, 0:B])
                    mm.then_inc(net_mm, 1)
                    pe.wait_ge(net_dve, 5)
                    for L in range(3):
                        if L:
                            pe.wait_ge(agg_act, L)
                            pe.wait_ge(agg_dve, L)
                        for bank, lo, hi in ((3, 0, D), (4, D, 2 * D), (5, 2 * D, AGG)):
                            mm = pe.matmul(ps[bank][0:B, 0:hi - lo], attT[:, L, :], kern[:, L, lo:hi],
                                           start=True, stop=True)
                        mm.then_inc(agg_mm, 1)

                @block.scalar
                def _(act):
                    act.wait_ge(nets_in, 16 * NET_IN)
                    for k, (bank, n) in enumerate(((2, 2), (4, 3))):
                        act.wait_ge(net_mm, n)
                        for L in range(3):
                            a = act.activation(hid[:, k, L, :], ps[bank][:, B * L:B * L + B], ACT.Gelu,
                                               bias=netb[:, k, L:L + 1])
                        a.then_inc(net_act, 1)
                    act.wait_ge(net_dve, 3)
                    act.activation(att[:, 2, :, :], att[:, 1, :, :], ACT.Exp).then_inc(net_act, 1)
                    for n in range(2):
                        act.wait_ge(w_sum, n + 1)
                        split_hi(act, n, n, 1, setup_pieces[n])
                    for tt in range(GT):
                        cond_hi(act, G0, tt)
                    for L in range(3):
                        act.wait_ge(agg_mm, L + 1)
                        act.activation(agg[:, L, 0:D], ps[3][0:B, :], ACT.Copy).then_inc(agg_act, 1)
                    act.wait_ge(const_in, 16 * CONST_IN)
                    act.wait_ge(zeroed, 6)
                    for k in range(3):
                        act.activation(b2s[32 * k:32 * k + E2, :], b2raw[32 * k:32 * k + E2, :], ACT.Copy)\
                           .then_inc(small_hi, 1)
                    act.activation(gwh[:, :, 0:E2], gate_raw[:, :, :], ACT.Copy).then_inc(small_hi, 1)
                    for n in range(2, N_L1):
                        split_hi(act, n, n % 2, n // 2 + 1, setup_pieces[n])

                @block.vector
                def _(dve):
                    link, n = linker(dve, 0)
                    dve.wait_ge(nets_in, 16 * NET_IN)
                    dve.wait_ge(net_mm, 1)
                    dve.tensor_tensor(ctx0[:, :], ps[3][0:B, 0:S], fside[:, :], ALU.add).then_inc(net_dve, 1)
                    dve.wait_ge(lora_in, 16 * LORA_IN)
                    dve.tensor_scalar(lbs[:, :], loraB[:, :], loraw[:, 0:1], 2.0, ALU.mult, ALU.mult)\
                       .then_inc(net_dve, 1)
                    by_net = "p (l k) -> p l k"
                    dve.wait_ge(net_mm, 4)
                    link(dve.tensor_tensor(att[:, 0, :, :], ps[5][0:B, 0:3 * KM].rearrange(by_net, l=3),
                                           netb2[:, :].rearrange(by_net, l=3), ALU.add))
                    link(dve.tensor_reduce(attm[:, 0, :], att[:, 0, :, :], AX.X, ALU.max))
                    dve.tensor_tensor(att[:, 1, :, :], att[:, 0, :, :],
                                      attm[:, 0, :].unsqueeze(2).to_broadcast([B, 3, KM]), ALU.subtract)\
                       .then_inc(net_dve, 1)
                    for k in range(2):
                        dve.wait_ge(stage_in[k], 16)
                        for c in range(2):
                            dve.wait_ge(lora_mm, 2 * k + c + 1)
                            part = stage[k][:, c * D:(c + 1) * D]
                            a = dve.tensor_tensor(part, ps[6 + c][:, :], part, ALU.add)
                        a.then_inc(w_sum, 1)
                        split_lo(dve, k, k, setup_pieces[k])
                    dve.wait_ge(net_act, 3)
                    link(dve.tensor_reduce(attm[:, 1, :], att[:, 2, :, :], AX.X, ALU.add))
                    link(dve.reciprocal(attm[:, 2, :], attm[:, 1, :]))
                    dve.tensor_tensor(att[:, 3, :, :], att[:, 2, :, :],
                                      attm[:, 2, :].unsqueeze(2).to_broadcast([B, 3, KM]), ALU.mult)\
                       .then_inc(net_dve, 1)
                    dve.wait_ge(net_mm, 5)
                    dve.tensor_copy(attT[:, :, :], ps[2][0:KM, 0:3 * B].rearrange("p (l b) -> p l b", l=3))\
                       .then_inc(net_dve, 1)
                    for tt in range(GT):
                        cond_sum(dve, G0, tt, first=True)
                    for L in range(3):
                        dve.wait_ge(agg_mm, L + 1)
                        dve.tensor_copy(agg[:, L, D:2 * D], ps[4][0:B, :])
                        dve.tensor_copy(agg[:, L, 2 * D:AGG], ps[5][0:B, 0:S]).then_inc(agg_dve, 1)
                    dve.wait_ge(const_in, 16 * CONST_IN)
                    dve.wait_ge(small_hi, 4)
                    dve.tensor_tensor(b2s[32:32 + E2, :], b2raw[32:32 + E2, :], b2s[32:32 + E2, :].bitcast(F32),
                                      ALU.subtract).then_inc(x_new, 1)
                    dve.tensor_tensor(gwl[:, :, 0:E2], gate_raw[:, :, :], gwh[:, :, 0:E2].bitcast(F32),
                                      ALU.subtract).then_inc(x_new, 1)
                    for k in range(2, N_L1):
                        split_lo(dve, k, k % 2, setup_pieces[k])
                    assert n[0] == CHAIN0

        w1h, w1l = sb("w1_hi", [P, E2, C, D], F32R), sb("w1_lo", [P, E2, C, D], F32R)

        def w1_piece(G):
            e = bass.ds(G.i, 1)
            c = slice(2 * G.j, 2 * G.j + 2)
            piece = (t["w1"][e, :, c, :].rearrange("e p c f -> (e p) c f"), 2, D,
                     w1h[:, e, c, :].rearrange("p e c f -> p (e c) f"),
                     w1l[:, e, c, :].rearrange("p e c f -> p (e c) f"))
            n, par = N_L1 + G.g, (N_L1 + G.j) % 2
            return n, par, (N_L1 + G.j) // 2 + 1 + G.i, piece

        static_pieces = (halves(t["w2"][1], w5h, w5l) + halves(t["w2"][0], w0h, w0l) +
                         halves(t["w2"][2], l1h, l1l) + halves(t["w3T"], w1h[:, 0], w1l[:, 0]))

        def piece_of(G):
            if G.L == 0 and not isinstance(G.i, int):
                return w1_piece(G)
            if G.L in (0, 1) and isinstance(G.i, int):
                return fixed_piece(2 * G.L + G.j)
            return None

        def fixed_piece(k):
            n = N_W1 + k
            return n, n % 2, n // 2 + 1, static_pieces[k]

        with nc.Block() as block:
            @block.sync
            def _(sp):
                def step(G):
                    p = piece_of(G)
                    if p:
                        load_piece(sp, p[0], p[1], p[3])
                    prefetch(sp, G)

                for L in range(3):
                    if L == 2:
                        for k in (4, 5):
                            n, par, _, piece = fixed_piece(k)
                            load_piece(sp, n, par, piece)
                    layer(sp, L, step)
                    if L == 0 or L == 2:
                        k = 1 + L // 2
                        sp.wait_ge(xb_done, GROUPS * k)
                        sp.dma_start(biasrow[:, :], t[f"bias{1 if k == 1 else 3}"].to_broadcast([P, D]))\
                          .then_inc(biasrow_in, 16)
                    if L == 2:
                        for k in (6, 7):
                            n, par, _, piece = fixed_piece(k)
                            load_piece(sp, n, par, piece)

                def last(G):
                    prefetch(sp, G)
                    store_y(sp, G)

                layer(sp, 3, last)
                for j in range(2):
                    sp.wait_ge(y_out[j], 16 * GROUPS // 2)

            @block.tensor
            def _(pe):
                def step0(G):
                    for tt in range(GT):
                        cond(pe, G.later(1), tt)
                    for tt in range(GT):
                        dense(pe, G, tt, w0h, w0l)

                def step1(G):
                    n1 = G.later(1)
                    l1_main(pe, G, 0)
                    l1_main(pe, G, 1)
                    l1_turn(pe, G, 0)
                    cond(pe, n1, 0)
                    l1_adapt(pe, G, 0)
                    cond(pe, n1, 1)
                    l1_turn(pe, G, 1)
                    l1_adapt(pe, G, 1)

                def step2(G):
                    gate_logits(pe, G)
                    for tt in range(GT):
                        cond(pe, G.later(1), tt)
                    expert_in(pe, G, 0)
                    gate_turn(pe, G)
                    expert_in(pe, G, 1)
                    gate_top(pe, G)
                    expert_out(pe, G, 0)
                    coef_turn(pe, G)
                    expert_in(pe, G, 2)
                    expert_bias(pe, G)
                    expert_out(pe, G, 1)
                    expert_out(pe, G, 2)

                def step3(G):
                    n1 = G.later(1)
                    if n1:
                        for tt in range(GT):
                            cond(pe, n1, tt)
                    for tt in range(GT):
                        dense(pe, G, tt, w1h[:, 0], w1l[:, 0])

                pe.wait_ge(w_lo, 2)
                layer(pe, 0, step0)
                pe.wait_ge(w_lo, N_L1)
                layer(pe, 1, step1)
                pe.wait_ge(w_lo, N_W1)
                pe.wait_ge(x_new, Group(2, 0, 0).outs + FIRST)
                layer(pe, 2, step2)
                pe.wait_ge(w_lo, N_L3)
                layer(pe, 3, step3)

            @block.scalar
            def _(act):
                def step0(G):
                    p = piece_of(G)
                    split_hi(act, *p)
                    ahead_act(act, G)

                def step1(G):
                    act.wait_ge(ht_mm, GT * G.g + 1)
                    act.activation(hth[:, 0, :], ps[6][:, 0:P], ACT.Copy).then_inc(ht_hi, 1)
                    ahead_act(act, G)
                    act.wait_ge(ht_mm, GT * G.g + 2)
                    act.activation(hth[:, 1, :], ps[7][:, 0:P], ACT.Copy).then_inc(ht_hi, 1)
                    p = piece_of(G)
                    if p:
                        split_hi(act, *p)

                def step2(G):
                    ahead_act(act, G)
                    expert_act(act, G, 0)
                    act.wait_ge(gate_sub, G.g + 1)
                    act.activation(g3[:, 1, :, :], g3[:, 0, :, :], ACT.Exp).then_inc(gate_exp, 1)
                    expert_act(act, G, 1)
                    act.wait_ge(coeft_mm, G.g + 1)
                    act.activation(coefT[:, :], ps[7][0:96, 0:GR], ACT.Copy).then_inc(coeft_copy, 1)
                    expert_act(act, G, 2)

                for k in range(FIRST):
                    act.activation(hth[:, k, :], ident[:, :], ACT.Copy).then_inc(act_f, 1)
                layer(act, 0, step0)
                act.wait_ge(out_mm, 2 * GROUPS)
                layer(act, 1, step1)
                act.wait_ge(out_mm, 4 * GROUPS)
                for k in (4, 5):
                    split_hi(act, *fixed_piece(k))
                layer(act, 2, step2)
                act.wait_ge(pre_mm, 2 * E2 * GROUPS)
                for k in (6, 7):
                    split_hi(act, *fixed_piece(k), scaled=True)
                layer(act, 3, lambda G: ahead_act(act, G))

            @block.vector
            def _(dve):
                def step0(G):
                    n, par, _, piece = piece_of(G)
                    split_lo(dve, n, par, piece)
                    ahead_dve(dve, G)
                    for tt in range(GT):
                        add_out(dve, G, tt)

                def step1(G):
                    link, n = linker(dve, CHAIN0 + CHAIN1 * G.g)
                    n1 = G.later(1)
                    router(dve, G, 0, link)
                    turned_lo(dve, G, 0)
                    router(dve, G, 1, link)
                    cond_sum(dve, n1, 0)
                    add_out(dve, G, 0)
                    cond_sum(dve, n1, 1)
                    turned_lo(dve, G, 1)
                    add_out(dve, G, 1)
                    p = piece_of(G)
                    if p:
                        split_lo(dve, p[0], p[1], p[3])
                    assert n[0] == CHAIN1, n

                def step2(G):
                    link, n = linker(dve, CHAIN0 + CHAIN1 * GROUPS + CHAIN2 * G.g)
                    gate_ratio(dve, G, link)
                    ahead_dve(dve, G)
                    gate_softmax(dve, G, link)
                    gate_coef(dve, G, link)
                    add_expert(dve, G, EXPERT_EV[0], 0)
                    add_expert(dve, G, BIAS_EV, None)
                    add_expert(dve, G, EXPERT_EV[1], 1)
                    add_expert(dve, G, EXPERT_EV[2], 2)
                    assert n[0] == CHAIN2, n

                def step3(G):
                    ahead_dve(dve, G)
                    for tt in range(GT):
                        add_out(dve, G, tt)

                layer(dve, 0, step0)
                layer(dve, 1, step1)
                for k in (4, 5):
                    n, par, _, piece = fixed_piece(k)
                    split_lo(dve, n, par, piece)
                layer(dve, 2, step2)
                for k in (6, 7):
                    n, par, _, piece = fixed_piece(k)
                    split_lo(dve, n, par, piece, scaled=True)
                layer(dve, 3, step3)

            @block.gpsimd
            def _(pool):
                def step(G):
                    add_bias(pool, G)
                    ahead_pool(pool, G)

                def step2(G):
                    ahead_pool(pool, G)
                    for e in range(E2):
                        buf = (3 * G.j + e) % 2
                        for k in range(2):
                            pool.wait_ge(act_hi, 2 * E2 * G.g + 2 * e + k + 1)
                            pool.tensor_tensor(al[buf][:, 2 * k:2 * k + 2, :], af[:, k, :, :],
                                               ah[buf][:, 2 * k:2 * k + 2, :].bitcast(F32), ALU.subtract)\
                                .then_inc(act_lo, 1)

                for L, count in ((0, 1), (1, 2), (2, 0), (3, 3)):
                    if L != 2:
                        pool.wait_ge(biasrow_in, 16 * count)
                    layer(pool, L, step2 if L == 2 else step)


def lay_out(i):
    import numpy as np

    a = {k: np.asarray(v) for k, v in i.items()}
    f = np.float32
    q = {}
    x = a["x"]
    q["x"] = x.reshape(ROWS, D)
    q["phases"] = x.reshape(B, S, D // PH, PH).transpose(3, 1, 0, 2).reshape(P, B, D // PH)
    w = a["L0_cond_weight"]
    per, taps = w.shape[1], w.shape[2]
    cw = np.zeros((PH, S, 3, PH, S), f)
    for qi in range(PH):
        for tap in range(3):
            for po in range(PH):
                k = PH * (tap - 1) + qi - po + taps // 2
                if 0 <= k < taps:
                    for g in range(S // per):
                        r = slice(g * per, (g + 1) * per)
                        cw[qi, r, tap, po, r] = w[r, :, k].T
    q["conv_w"] = cw.reshape(P, 3, P)
    q["condT"] = a["cond_128"].T
    q["cwT"] = a["L0_cond_c_weight"].T
    q["fside"] = a["fside_S_0"].reshape(1, S)
    q["w0T"] = a["L0_ffn_W"].T.reshape(P, PH, D)
    q["loraA"] = a["L0_ffn_lora_A"].reshape(P, D // PH, PH).transpose(0, 2, 1)
    q["loraB"] = a["L0_ffn_lora_B"].transpose(0, 2, 1).reshape(P, D)
    q["loraw"] = np.repeat(a["L0_ffn_lora_weights"], R1).reshape(P, 1)
    nets = [{k: a[f"L{L}_cond_{k}"] for k in ("W0", "b0", "W1", "b1", "W2", "b2", "weight", "bias_k")}
            for L in (1, 2, 3)]
    q["netw"] = np.stack([np.stack([n[k] for n in nets], 1) for k in ("W0", "W1")], 1)
    q["netb"] = np.stack([np.stack([n[k] for n in nets], 1) for k in ("b0", "b1")], 1)
    q["netw2"] = np.stack([n["W2"] for n in nets], 1)
    q["netb2"] = np.concatenate([n["b2"] for n in nets]).reshape(1, 3 * KM)
    q["kern"] = np.stack([np.concatenate([n["weight"][..., 0].transpose(0, 2, 1).reshape(KM, S * S),
                                          n["bias_k"]], 1) for n in nets], 1)

    def chunks(m):
        return m.reshape(C, P, -1).transpose(1, 0, 2)

    base, router = a["L1_ffn_W_base"].T, a["L1_ffn_W_router"].T
    adapt = a["L1_ffn_lora_A"].transpose(1, 0, 2).reshape(D, E1 * R1)
    q["l1w"] = chunks(np.concatenate([base[:, :HALF], adapt, base[:, HALF:], router], 1))
    q["lora_b1"] = a["L1_ffn_lora_B"].reshape(E1 * R1, D)
    q["brouter"] = a["L1_ffn_b_router"].reshape(1, E1)
    q["w1"] = np.stack([chunks(m) for m in a["L2_ffn_w1"]])
    q["w2"] = np.stack([chunks(m) for m in a["L2_ffn_w2"]])
    q["b1c"] = a["L2_ffn_b1"].reshape(E2 * C, P).T
    q["b2"] = a["L2_ffn_b2"]
    q["gate_w"] = chunks(a["L2_ffn_gate_w"][:D])
    q["gate_tail"] = np.stack([a["L2_ffn_gate_w"][D], a["L2_ffn_gate_b"]], 1)
    q["w3T"] = chunks(a["L3_ffn_weight"].T)
    q["wscale"] = a["L3_ffn_weight_scale"].reshape(1, 1)
    q["bias0"] = a["L0_ffn_bias"].reshape(1, D)
    q["bias1"] = a["L1_ffn_b_base"].reshape(1, D)
    q["bias3"] = a["L3_ffn_bias"].reshape(1, D)
    q["ident"] = np.eye(P, dtype=f)
    q["token0"] = (np.arange(P)[:, None] == np.arange(P)[None, :] // S * S).astype(f)
    q["ranks8"] = np.arange(1, E1 + 1, dtype=f).reshape(1, E1)
    return {k: np.ascontiguousarray(v) for k, v in q.items()}


def kernel(**inputs):
    import numpy as np
    import concourse.bacc as bacc
    from concourse.bass_utils import run_bass_kernel_spmd

    nc = bacc.Bacc("TRN2", target_bir_lowering=False, num_devices=1)
    arrays = lay_out(inputs)
    arrays = {"in_" + k: v for k, v in arrays.items()}
    t = {k[3:]: nc.dram_tensor(k, list(v.shape), mybir.dt.from_np(v.dtype), kind="ExternalInput").ap()
         for k, v in arrays.items()}
    t["out"] = nc.dram_tensor("out", [ROWS, D], F32, kind="ExternalOutput").ap()
    build(nc, t)
    r = run_bass_kernel_spmd(nc, [arrays], core_ids=[0])
    return np.asarray(r.results[0]["out"]).reshape(B, S, D)
```

```python
from contextlib import ExitStack

import concourse.bass as bass
from concourse import mybir

F32 = mybir.dt.float32
F32R = mybir.dt.float32r
ALU = mybir.AluOpType
ACT = mybir.ActivationFunctionType
AX = mybir.AxisListType

P = 128
B, S, D = 64, 32, 512
ROWS = B * S
TB = P // S
TILES = ROWS // P
GT = 2
GROUPS = TILES // GT
GR = GT * P
C = D // P
KM = 8
E1, R1 = 8, 16
E2 = 3
VIS = int(S * 0.3)
PH = 4
HALF = D // 2
WA, WB = HALF + E1 * R1, HALF + E1
GM = 72
GK = 64
L1W = C * (WA + WB) + D
L1PIECE = -(-L1W // (GROUPS - 2))
AGG = S * S + S
CONST_IN = 4
PAIRS = (GROUPS - 2) // 2
FIRST = 2
EV2 = 2 * E2
CHAIN0, CHAIN1, CHAIN2 = 4, 14, 17


class Group:

    def __init__(self, L, i, j):
        self.L, self.i, self.j = L, i, j
        self.g = 2 * i + j
        self.tiles = 2 * GROUPS * L + GT * self.g
        self.outs = {0: 2 * self.g, 1: 2 * GROUPS + 2 * self.g, 2: 4 * GROUPS + EV2 * self.g,
                     3: (4 + EV2) * GROUPS + 2 * self.g}[L]

    def later(self, by):
        i, j = self.i + (self.j + by) // 2, (self.j + by) % 2
        if isinstance(i, int) and i >= GROUPS // 2:
            return Group(self.L + 1, i - GROUPS // 2, j) if self.L < 3 else None
        return Group(self.L, i, j)

    def rows(self, tt):
        return GT * self.g + tt

    def x_count(self, tt):
        return self.outs + (EV2 - 2 if self.L == 2 else 0) + tt + 1 + FIRST


def build(nc, t):
    out_v = t["out"].rearrange("(g t p) d -> g p t d", t=GT, p=P)
    x_v = t["x"].rearrange("(g t p) d -> g p t d", t=GT, p=P)
    mix_d = nc.dram_tensor("mix_scratch", [3, B, S * S], F32, kind="Internal").ap()
    rowbias_d = nc.dram_tensor("rowbias_scratch", [4, ROWS], F32, kind="Internal").ap()

    with ExitStack() as ctx:
        def sb(name, shape, dt=F32, where=None):
            return (where or ctx).enter_context(nc.sbuf_tensor(name, shape, dt))

        def sem(name):
            return ctx.enter_context(nc.semaphore(name))

        x = sb("x_rows", [P, TILES, D])
        w0h, w0l = sb("w0_hi", [P, C, D], F32R), sb("w0_lo", [P, C, D], F32R)
        l1row = [sb(f"l1_{k}", [P, (GROUPS - 2) * L1PIECE], F32R) for k in ("hi", "lo")]
        l1h, l1l = (r[:, 0:C * (WA + WB)].rearrange("p (c n) -> p c n", c=C) for r in l1row)
        lbh, lbl = (r[:, C * (WA + WB):L1W] for r in l1row)
        w5h, w5l = sb("w2e1_hi", [P, C, D], F32R), sb("w2e1_lo", [P, C, D], F32R)
        gw = sb("gate_split", [P, C, GM], F32R)
        b2s = sb("b2_split", [96, D], F32R)
        stage = [sb(f"stage{k}", [P, 2 * D]) for k in range(2)]
        conv_w = sb("conv_w", [P, 3, P])
        xs = sb("x_mix", [P, GT * TB, P + 2])
        mix = [sb(f"mix{k}", [P, GT, P]) for k in range(2)]
        rowbias = [sb(f"rowbias{k}", [P, GR]) for k in range(2)]
        cf = sb("cond_f32", [P, GT, C, P])
        ch = [sb(f"cond_hi{k}", [P, C, GR], F32R) for k in range(2)]
        cl = [sb(f"cond_lo{k}", [P, C, GR], F32R) for k in range(2)]
        biasrow = sb("ffn_bias", [P, D])
        af = sb("act_f32", [P, 2, 2, GR])
        ah = [sb(f"act_hi{k}", [P, C, GR], F32R) for k in range(2)]
        al = [sb(f"act_lo{k}", [P, C, GR], F32R) for k in range(2)]
        by_tile = "p (t r) -> p t r"
        hs = af[:, 0, 0, :].rearrange(by_tile, t=GT)
        hth, htl = (al[0][:, k, :].rearrange(by_tile, t=GT) for k in range(2))
        ident, token0, ones = sb("ident", [P, P]), sb("token0", [P, P]), sb("ones", [P, P])
        small = sb("small", [P, E1 + E2 + E2 * C + 2 + C * E2])
        ranks8, gate_sum = small[:, 0:E1], small[0:GK, E1:E1 + E2]
        b1c = small[:, E1 + E2:E1 + E2 + E2 * C]
        tail_at = E1 + E2 + E2 * C
        gate_tail = small[0:GK, tail_at:tail_at + 2]
        gate_raw = small[:, tail_at + 2:].rearrange("p (c e) -> p c e", c=C)
        wide_row = sb("wide_row", [P, E1 + 1])
        brouter, wscale = wide_row[:, 0:E1], wide_row[:, E1:E1 + 1]
        sz = sb("sparsemax", [P, GT, 8, E1])
        sc = sb("sparsemax_scalars", [P, GT, 4])
        absum = sb("abs_sums", [P, 2, GT * TB])
        ratio = sb("ratio", [GK, 3, GT * TB])
        gl = sb("gate_logits", [GK, 2, GR])
        g3 = sb("gate_scores", [P, 6, GT, E2])
        g1 = sb("gate_scalars", [P, 16, GT])
        top = sb("gate_top", [P, 2, GT, E2])
        coef = sb("coef", [P, GT, E2])
        coef96 = sb("coef_split", [P, GT, 96])
        coefT = sb("coef_t", [96, GR], F32R)

        ps = [ctx.enter_context(nc.psum_tensor(f"bank{k}", [P, D], F32)) for k in range(8)]
        OUT = (2, 4)
        SIDE = (3, 5)

        net0_in, nets_in, conv_in, lora_in, kern_in = (sem("net0_in"), sem("nets_in"), sem("conv_in"), sem("lora_in"),
                                                       sem("kern_in"))
        const_in, phase_in = sem("const_in"), sem("phase_in")
        stage_in = [sem(f"stage_in{k}") for k in range(2)]
        rowbias_in = [sem(f"rowbias_in{k}") for k in range(2)]
        mix_in = [sem(f"mix_in{k}") for k in range(2)]
        x_in = [sem(f"x_in{k}") for k in range(2)]
        biasrow_in = sem("biasrow_in")
        ctx_out, agg_out = sem("ctx_out"), sem("agg_out")
        y_out = [sem(f"y_out{k}") for k in range(2)]
        net_mm, agg_mm, lora_mm, cond_mm = sem("net_mm"), sem("agg_mm"), sem("lora_mm"), sem("cond_mm")
        main_mm, ht_mm, out_mm = sem("main_mm"), sem("ht_mm"), sem("out_mm")
        gate_mm, gatet_mm, top_mm, coeft_mm, pre_mm = (sem("gate_mm"), sem("gatet_mm"), sem("top_mm"),
                                                       sem("coeft_mm"), sem("pre_mm"))
        bias_mm, bias_new = sem("bias_mm"), sem("bias_new")
        net_act, w_hi, small_hi, c_hi, xs_copy = (sem("net_act"), sem("w_hi"), sem("small_hi"), sem("c_hi"),
                                                  sem("xs_copy"))
        agg_act, ht_hi, act_f, act_hi = sem("agg_act"), sem("ht_hi"), sem("act_f"), sem("act_hi")
        gate_exp, coeft_copy = sem("gate_exp"), sem("coeft_copy")
        net_dve, agg_dve, chain, w_sum, w_lo = sem("net_dve"), sem("agg_dve"), sem("chain"), sem("w_sum"), sem("w_lo")
        c_sum, hs_done, ht_lo, abs_done = sem("c_sum"), sem("hs_done"), sem("ht_lo"), sem("abs_done")
        logit_done, gate_sub, top_done, coef_done, x_new = (sem("logit_done"), sem("gate_sub"), sem("top_done"),
                                                            sem("coef_done"), sem("x_new"))
        zeroed, c_lo, xb_done, act_lo = sem("zeroed"), sem("c_lo"), sem("xb_done"), sem("act_lo")

        def halves(src, h, l):
            return [(src[:, 2 * k:2 * k + 2, :], 2, D, h[:, 2 * k:2 * k + 2, 0:D], l[:, 2 * k:2 * k + 2, 0:D])
                    for k in range(2)]

        flat = "p (c n) -> p c n"
        setup_pieces = halves(t["w0T"], w0h, w0l)
        N_L0 = len(setup_pieces)
        N_W1 = N_L0 + 2 * (GROUPS - 2)
        N_E1, N_E0, N_E2, N_L3 = N_W1 + 2, N_W1 + 4, N_W1 + 6, N_W1 + 8

        def staged(n, piece):
            return stage[n % 2][:, 0:piece[1] * piece[2]].rearrange(flat, c=piece[1])

        def load_piece(sp, n, par, piece):
            if not isinstance(n, int) or n >= 2:
                sp.wait_ge(w_lo, n - 1)
            sp.dma_start(staged(par, piece), piece[0]).then_inc(stage_in[par], 16)

        def split_hi(act, n, par, nth, piece, scaled=False):
            act.wait_ge(stage_in[par], 16 * nth)
            act.activation(piece[3], staged(par, piece), ACT.Copy,
                           scale=wscale if scaled else 1.0).then_inc(w_hi, 1)

        def split_lo(dve, n, par, piece, scaled=False):
            dve.wait_ge(w_hi, n + 1)
            if scaled:
                dve.scalar_tensor_tensor(out=piece[4], in0=staged(par, piece), scalar=wscale,
                                         in1=piece[3].bitcast(F32), op0=ALU.mult,
                                         op1=ALU.subtract).then_inc(w_lo, 1)
            else:
                dve.tensor_tensor(piece[4], staged(par, piece), piece[3].bitcast(F32),
                                  ALU.subtract).then_inc(w_lo, 1)

        def cond_view(bank):
            return ps[bank][:, :].rearrange(flat, c=C)

        THREE = ((0, 1), (0, 0), (1, 0))
        STEPS = [(a, w, c) for a, w in THREE for c in range(C)]

        def cond(pe, G, tt, first=False):
            if not first:
                pe.wait_ge(c_sum, G.tiles + tt + 1 - GT)
            if G.L == 0:
                pe.wait_ge(phase_in, 16 * (G.g + 1))
                dst = ps[tt][:, :].rearrange("p (c b o) -> p c b o", c=PH, b=TB)
                for b in range(TB):
                    for tap in range(3):
                        mm = pe.matmul(dst[:, :, b, :], xs[:, TB * tt + b, tap:tap + P],
                                       conv_w[:, tap, :].rearrange("k (c o) -> k c o", c=PH),
                                       start=(tap == 0), stop=(tap == 2))
            else:
                pe.wait_ge(mix_in[G.j], 16 * TB * (GROUPS // 2 * (G.L - 1) + G.i + 1))
                pe.wait_ge(xs_copy, G.tiles - 2 * GROUPS + tt + 1)
                for c in range(C):
                    mm = pe.matmul(ps[tt][:, c * P:(c + 1) * P], x_tile(tt)[:, c * P:(c + 1) * P],
                                   mix[G.j][:, tt, :], start=True, stop=True)
            mm.then_inc(cond_mm, 1)

        def x_tile(tt):
            return xs[:, TB * tt:TB * (tt + 1), :].rearrange("p b m -> p (b m)")[:, 0:D]

        def cond_ready(pe, G, tt, k):
            if k == 0:
                pe.wait_ge(c_hi, G.tiles + tt + 1)
            if STEPS[k][0] == 1 and STEPS[k][2] == 0:
                pe.wait_ge(c_lo, G.tiles + tt + 1)

        def out_free(pe, n):
            pe.wait_ge(x_new, n)

        def dense(pe, G, tt, wh, wl):
            out_free(pe, G.outs + tt + 1)
            for k, (a, w, c) in enumerate(STEPS):
                cond_ready(pe, G, tt, k)
                mm = pe.matmul(ps[OUT[tt]][:, :], (ch, cl)[a][G.j][:, c, tt * P:(tt + 1) * P],
                               (wh, wl)[w][:, c, 0:D], start=(k == 0), stop=(k == len(STEPS) - 1))
            mm.then_inc(out_mm, 1)

        def l1_main(pe, G, tt, steps=range(len(STEPS))):
            if steps[0] == 0:
                out_free(pe, G.outs + tt + 1)
            for k in steps:
                a, w, c = STEPS[k]
                cond_ready(pe, G, tt, k)
                for bank, lo, hi in ((OUT[tt], 0, WA), (SIDE[tt], WA, WA + WB)):
                    mm = pe.matmul(ps[bank][:, 0:hi - lo], (ch, cl)[a][G.j][:, c, tt * P:(tt + 1) * P],
                                   (l1h, l1l)[w][:, c, lo:hi], start=(k == 0), stop=(k == len(STEPS) - 1))
            if steps[-1] == len(STEPS) - 1:
                mm.then_inc(main_mm, 1)

        def l1_turn(pe, G, tt):
            pe.wait_ge(hs_done, GT * G.g + tt + 1)
            pe.transpose(ps[6 + tt][:, 0:P], hs[:, tt, :], ident[:, :]).then_inc(ht_mm, 1)

        def l1_adapt(pe, G, tt):
            pe.wait_ge(ht_lo, GT * G.g + tt + 1)
            for a, w in THREE:
                for bank, lo in ((OUT[tt], 0), (SIDE[tt], HALF)):
                    mm = pe.matmul(ps[bank][:, 0:HALF], (hth, htl)[a][:, tt, :], (lbh, lbl)[w][:, lo:lo + HALF],
                                   start=False, stop=True, skip_group_check=True)
            mm.then_inc(out_mm, 1)

        def gate_logits(pe, G):
            pe.wait_ge(c_lo, G.tiles + GT)
            for c in range(C):
                for w in (1, 0):
                    pe.matmul(ps[6][0:GM, 0:GR], gw[:, c, :], (ch, cl)[w][G.j][:, c, :],
                              start=(c == 0 and w == 1), stop=(c == C - 1 and w == 0))
            pe.wait_ge(abs_done, GT * (G.g + 1))
            pe.matmul(ps[6][:, GR:GR + 2 * GT * TB], ones[:, :], absum[:, :, :].rearrange("p k b -> p (k b)"),
                      start=True, stop=True).then_inc(gate_mm, 1)

        def gate_turn(pe, G):
            pe.wait_ge(logit_done, G.g + 1)
            for tt in range(GT):
                mm = pe.matmul(ps[7][:, 4 * tt:4 * tt + E2], gl[:, 1, tt * P:(tt + 1) * P], gate_sum,
                               start=True, stop=True)
            mm.then_inc(gatet_mm, 1)

        def gate_top(pe, G):
            pe.wait_ge(top_done, G.g + 1)
            pe.matmul(ps[6][:, 0:2 * GT * E2], token0[:, :], top[:, :, :, :].rearrange("p k t e -> p (k t e)"),
                      start=True, stop=True).then_inc(top_mm, 1)

        def coef_turn(pe, G):
            pe.wait_ge(coef_done, G.g + 1)
            for tt in range(GT):
                mm = pe.transpose(ps[7][0:96, tt * P:(tt + 1) * P], coef96[:, tt, :], ident[:, :])
            mm.then_inc(coeft_mm, 1)

        def expert_in(pe, G, e):
            for k in range(2):
                n = 2 * E2 * G.g + 2 * e + k + 1
                pe.wait_ge(act_f, n)
                for f in (2 * k, 2 * k + 1):
                    for c in range(C):
                        for a, w in THREE:
                            mm = pe.matmul(ps[SIDE[k]][:, (f % 2) * GR:(f % 2 + 1) * GR],
                                           (w1h, w1l)[a][:, e, c, f * P:(f + 1) * P], (ch, cl)[w][G.j][:, c, :],
                                           start=(c == 0 and (a, w) == THREE[0]),
                                           stop=(c == C - 1 and (a, w) == THREE[-1]))
                mm.then_inc(pre_mm, 1)

        def expert_out(pe, G, e):
            buf = (3 * G.j + e) % 2
            pe.wait_ge(act_lo, 2 * E2 * G.g + 2 * e + 2 + FIRST)
            pe.wait_ge(w_lo, (N_E0, N_E1, N_E2)[e])
            wh, wl = ((w0h, w0l), (w5h, w5l), (l1h, l1l))[e]
            for tt in range(GT):
                out_free(pe, G.outs + 2 * e + tt + 1)
                for c in range(C):
                    for a, w in THREE:
                        mm = pe.matmul(ps[OUT[tt]][:, :], (ah, al)[a][buf][:, c, tt * P:(tt + 1) * P],
                                       (wh, wl)[w][:, c, 0:D], start=(c == 0 and (a, w) == THREE[0]),
                                       stop=(c == C - 1 and (a, w) == THREE[-1]))
                mm.then_inc(out_mm, 1)

        def expert_bias(pe, G):
            pe.wait_ge(coeft_copy, G.g + 1)
            for tt in range(GT):
                pe.matmul(ps[6 + tt][:, :], coefT[:, tt * P:(tt + 1) * P], b2s[:, :],
                          start=True, stop=True).then_inc(bias_mm, 1)

        def cond_hi(act, G, tt):
            act.wait_ge(c_sum, G.tiles + tt + 1)
            act.activation(ch[G.j][:, :, tt * P:(tt + 1) * P], cf[:, tt, :, :], ACT.Copy).then_inc(c_hi, 1)

        def copy_x(act, G, tt, before):
            act.wait_ge(cond_mm, before.tiles + tt + 1)
            act.wait_ge(x_new, Group(G.L - 1, G.i, G.j).x_count(tt))
            act.activation(x_tile(tt), x[:, G.rows(tt), :], ACT.Copy).then_inc(xs_copy, 1)

        def ahead_act(act, G, tiles=range(GT)):
            n1, n2 = G.later(1), G.later(2)
            for tt in tiles:
                if n1:
                    cond_hi(act, n1, tt)
                if n2 and n2.L:
                    copy_x(act, n2, tt, n1)

        def expert_act(act, G, e):
            buf = (3 * G.j + e) % 2
            for k in range(2):
                n = 2 * E2 * G.g + 2 * e + k + 1
                act.wait_ge(pre_mm, n)
                act.wait_ge(act_lo, n)
                for f in range(2):
                    a = act.activation(af[:, k, f, :], ps[SIDE[k]][:, f * GR:(f + 1) * GR],
                                       (ACT.Tanh, ACT.Gelu, ACT.Silu)[e],
                                       bias=b1c[:, e * C + 2 * k + f:e * C + 2 * k + f + 1])
                a.then_inc(act_f, 1)
                act.wait_ge(out_mm, G.outs + 2 * e - 2)
                act.wait_ge(act_f, n + FIRST)
                act.activation(ah[buf][:, 2 * k:2 * k + 2, :], af[:, k, :, :], ACT.Copy).then_inc(act_hi, 1)

        def linker(dve, base):
            n = [0]

            def link(ins):
                n[0] += 1
                ins.then_inc(chain, 1)
                dve.wait_ge(chain, base + n[0])
            return link, n

        def cond_sum(dve, G, tt, first=False):
            dve.wait_ge(rowbias_in[G.j], 16 * (GROUPS // 2 * G.L + G.i + 1))
            dve.wait_ge(cond_mm, G.tiles + tt + 1)
            if not first:
                dve.wait_ge(c_lo, G.tiles + tt + 1 - GT)
            dve.tensor_tensor(cf[:, tt, :, :], cond_view(tt),
                              rowbias[G.j][:, tt * P:(tt + 1) * P].unsqueeze(1).to_broadcast([P, C, P]),
                              ALU.add).then_inc(c_sum, 1)
            if G.L == 2:
                dve.wait_ge(c_sum, G.tiles + tt + 1)
                v = cf[:, tt, :, :].rearrange("p c (b r) -> p b c r", b=TB)
                for k, (lo, hi) in enumerate(((0, VIS), (VIS, S))):
                    r = dve.tensor_reduce(absum[:, k, tt * TB:(tt + 1) * TB], v[:, :, :, lo:hi], AX.XY, ALU.add,
                                          apply_absolute_value=True)
                r.then_inc(abs_done, 1)

        def ahead_dve(dve, G):
            n1 = G.later(1)
            if n1:
                for tt in range(GT):
                    cond_sum(dve, n1, tt)

        def add_out(dve, G, tt):
            dve.wait_ge(xb_done, GROUPS * min(G.L, 2) + G.g + 1)
            dve.wait_ge(out_mm, G.outs + tt + 1)
            row = x[:, G.rows(tt), :]
            if G.L == 1:
                dve.tensor_tensor(row[:, 0:HALF], ps[OUT[tt]][:, 0:HALF], row[:, 0:HALF], ALU.add)
                dve.tensor_tensor(row[:, HALF:D], ps[SIDE[tt]][:, 0:HALF], row[:, HALF:D], ALU.add)\
                   .then_inc(x_new, 1)
            else:
                dve.tensor_tensor(row, ps[OUT[tt]][:, :], row, ALU.add).then_inc(x_new, 1)

        def add_expert(dve, G, e, tt):
            n = G.outs + 2 * e + tt + 1
            dve.wait_ge(out_mm, n)
            if e == 1:
                dve.wait_ge(bias_new, GT * (G.g + 1))
            else:
                dve.wait_ge(x_new, n)
            row = x[:, G.rows(tt), :]
            dve.scalar_tensor_tensor(out=row, in0=ps[OUT[tt]][:, :], scalar=coef[:, tt, e:e + 1], in1=row,
                                     op0=ALU.mult, op1=ALU.add).then_inc(x_new, 1)

        def add_expert_bias(dve, G):
            for tt in range(GT):
                dve.wait_ge(bias_mm, GT * G.g + tt + 1)
                dve.wait_ge(x_new, G.outs + tt + 1 + FIRST)
                row = x[:, G.rows(tt), :]
                dve.tensor_tensor(row, ps[6 + tt][:, :], row, ALU.add).then_inc(bias_new, 1)

        def router(dve, G, tt, link):
            z, zs, cum, kz, sup, kk, w, one = (sz[:, tt, k, :] for k in range(8))
            count, total, inv, tau = (sc[:, tt, k:k + 1] for k in range(4))
            dve.wait_ge(main_mm, GT * G.g + tt + 1)
            link(dve.tensor_tensor(z, ps[SIDE[tt]][:, HALF:HALF + E1], brouter, ALU.add))
            dve.memset(sc[:, tt, :], 0.0)
            link(dve.max(zs, z))
            dve.tensor_tensor(kz, zs, ranks8, ALU.mult)
            link(dve.tensor_tensor_scan(cum, ones[:, 0:E1], zs, 0.0, ALU.mult, ALU.add))
            link(dve.scalar_tensor_tensor(out=sup, in0=kz, scalar=1.0, in1=cum, op0=ALU.add, op1=ALU.is_gt,
                                          accum_out=count))
            dve.scalar_tensor_tensor(out=kk, in0=ranks8, scalar=count, in1=cum, op0=ALU.is_equal,
                                     op1=ALU.mult, accum_out=total)
            link(dve.reciprocal(inv, count))
            link(dve.tensor_scalar(tau, total, -1.0, inv, ALU.add, ALU.mult))
            link(dve.tensor_scalar(w, z, tau, 0.0, ALU.subtract, ALU.max))
            dve.tensor_tensor(hs[:, tt, :].rearrange("p (e r) -> p e r", e=E1),
                              ps[OUT[tt]][:, HALF:WA].rearrange("p (e r) -> p e r", e=E1),
                              w.unsqueeze(2).to_broadcast([P, E1, R1]), ALU.mult).then_inc(hs_done, 1)

        def turned_lo(dve, G, tt):
            dve.wait_ge(ht_hi, GT * G.g + tt + 1)
            dve.tensor_tensor(htl[:, tt, :], ps[6 + tt][:, 0:P], hth[:, tt, :].bitcast(F32), ALU.subtract)\
               .then_inc(ht_lo, 1)

        def gate_ratio(dve, G, link):
            dve.wait_ge(gate_mm, G.g + 1)
            vis, text = (ps[6][0:GK, GR + k * GT * TB:GR + (k + 1) * GT * TB] for k in range(2))
            dve.tensor_scalar(gl[:, 0, :], ps[6][0:GK, 0:GR], gate_tail[:, 1:2], None, ALU.add)
            link(dve.tensor_scalar(ratio[:, 0, :], vis, 1.0 / (VIS * D), 1e-8, ALU.mult, ALU.add))
            link(dve.reciprocal(ratio[:, 1, :], ratio[:, 0, :]))
            link(dve.scalar_tensor_tensor(out=ratio[:, 2, :], in0=text, scalar=1.0 / ((S - VIS) * D),
                                          in1=ratio[:, 1, :], op0=ALU.mult, op1=ALU.mult))
            by_batch = "e (b r) -> e b r"
            dve.scalar_tensor_tensor(out=gl[:, 1, :].rearrange(by_batch, r=S),
                                     in0=ratio[:, 2, :].unsqueeze(2).to_broadcast([GK, GT * TB, S]),
                                     scalar=gate_tail[:, 0:1], in1=gl[:, 0, :].rearrange(by_batch, r=S),
                                     op0=ALU.mult, op1=ALU.add).then_inc(logit_done, 1)

        def wide(v):
            return v.unsqueeze(2).to_broadcast([P, GT, E2])

        def gate_softmax(dve, G, link):
            dve.wait_ge(gatet_mm, G.g + 1)
            logits = ps[7][:, 0:4 * GT].rearrange("p (t e) -> p t e", t=GT)[:, :, 0:E2]
            link(dve.tensor_reduce(g1[:, 0, :], logits, AX.X, ALU.max))
            dve.tensor_tensor(g3[:, 0, :, :], logits, wide(g1[:, 0, :]), ALU.subtract).then_inc(gate_sub, 1)
            dve.wait_ge(gate_exp, G.g + 1)
            link(dve.tensor_reduce(g1[:, 1, :], g3[:, 1, :, :], AX.X, ALU.add))
            link(dve.reciprocal(g1[:, 2, :], g1[:, 1, :]))
            link(dve.tensor_tensor(g3[:, 2, :, :], g3[:, 1, :, :], wide(g1[:, 2, :]), ALU.mult))
            s0, s1, s2 = (g3[:, 2, :, e] for e in range(E2))
            dve.tensor_reduce(g1[:, 3, :], g3[:, 2, :, :], AX.X, ALU.max)
            dve.tensor_tensor(g1[:, 4, :], s0, s1, ALU.max)
            dve.tensor_tensor(g1[:, 5, :], s0, s1, ALU.min)
            dve.tensor_tensor(g1[:, 6, :], s0, s1, ALU.is_ge)
            dve.tensor_tensor(g1[:, 7, :], s0, s2, ALU.is_ge)
            link(dve.tensor_tensor(g1[:, 8, :], s1, s2, ALU.is_ge))
            dve.tensor_tensor(g1[:, 9, :], g1[:, 4, :], s2, ALU.min)
            dve.tensor_tensor(g3[:, 3, :, 0], g1[:, 6, :], g1[:, 7, :], ALU.add)
            dve.tensor_tensor(g1[:, 10, :], g1[:, 8, :], g1[:, 6, :], ALU.subtract)
            link(dve.tensor_tensor(g1[:, 11, :], g1[:, 7, :], g1[:, 8, :], ALU.add))
            dve.tensor_scalar(g3[:, 3, :, 1], g1[:, 10, :], 1.0, None, ALU.add)
            dve.tensor_tensor(g1[:, 12, :], g1[:, 5, :], g1[:, 9, :], ALU.max)
            link(dve.tensor_scalar(g3[:, 3, :, 2], g1[:, 11, :], -1.0, 2.0, ALU.mult, ALU.add))
            dve.tensor_scalar(top[:, 0, :, :], g3[:, 3, :, :], 2.0, None, ALU.is_equal)
            dve.tensor_scalar(top[:, 1, :, :], g3[:, 3, :, :], 1.0, None, ALU.is_equal).then_inc(top_done, 1)
            link(dve.tensor_tensor(g1[:, 13, :], g1[:, 3, :], g1[:, 12, :], ALU.add))
            link(dve.tensor_scalar(g1[:, 14, :], g1[:, 13, :], 1e-8, None, ALU.add))
            link(dve.reciprocal(g1[:, 15, :], g1[:, 14, :]))
            dve.tensor_tensor(g1[:, 0, :], g1[:, 3, :], g1[:, 15, :], ALU.mult)
            link(dve.tensor_tensor(g1[:, 1, :], g1[:, 12, :], g1[:, 15, :], ALU.mult))

        def gate_coef(dve, G, link):
            dve.wait_ge(top_mm, G.g + 1)
            ranked = ps[6][:, 0:2 * GT * E2].rearrange("p (k t e) -> p k t e", k=2, t=GT)
            dve.tensor_tensor(g3[:, 4, :, :], ranked[:, 0, :, :], wide(g1[:, 0, :]), ALU.mult)
            link(dve.tensor_tensor(g3[:, 5, :, :], ranked[:, 1, :, :], wide(g1[:, 1, :]), ALU.mult))
            link(dve.tensor_tensor(coef[:, :, :], g3[:, 4, :, :], g3[:, 5, :, :], ALU.add))
            dve.tensor_copy(coef96[:, :, 0:E2].bitcast(F32R), coef[:, :, :])
            link(dve.tensor_copy(coef96[:, :, 32:32 + E2].bitcast(F32R), coef[:, :, :]))
            dve.tensor_tensor(coef96[:, :, 64:64 + E2], coef[:, :, :], coef96[:, :, 32:32 + E2], ALU.subtract)\
               .then_inc(coef_done, 1)

        def cond_lo(pool, G, tt):
            pool.wait_ge(c_hi, G.tiles + tt + 1)
            pool.tensor_tensor(cl[G.j][:, :, tt * P:(tt + 1) * P], cf[:, tt, :, :],
                               ch[G.j][:, :, tt * P:(tt + 1) * P].bitcast(F32), ALU.subtract).then_inc(c_lo, 1)

        def add_bias(pool, G):
            if G.L == 0:
                pool.wait_ge(x_in[G.j], 16 * (G.i + 1))
            else:
                pool.wait_ge(xs_copy, G.tiles - 2 * GROUPS + GT)
            rows = x[:, bass.ds(G.rows(0), GT), :]
            pool.tensor_tensor(rows, rows, biasrow[:, :].unsqueeze(1).to_broadcast([P, GT, D]), ALU.add)\
                .then_inc(xb_done, 1)

        def ahead_pool(pool, G):
            n1 = G.later(1)
            if n1:
                for tt in range(GT):
                    cond_lo(pool, n1, tt)

        def load_rowbias(sp, G):
            src = rowbias_d[G.L].rearrange("(g a r) -> g a r", a=1, r=GR)
            src = src[bass.ds(G.g, 1), :, :].rearrange("g a r -> (g a) r").to_broadcast([P, GR])
            sp.dma_start(rowbias[G.j][:, :], src).then_inc(rowbias_in[G.j], 16)

        def load_mix(sp, G):
            src = mix_d[G.L - 1].rearrange("(g t b) (i o) -> g b i t o", t=GT, b=TB, i=S)
            for b in range(TB):
                sp.dma_start(mix[G.j][b * S:(b + 1) * S, :, b * S:(b + 1) * S],
                             src[bass.ds(G.g, 1), b].rearrange("g i t o -> (g i) t o")).then_inc(mix_in[G.j], 16)

        def load_x(sp, G):
            sp.dma_start(x[:, bass.ds(G.rows(0), GT), :],
                         x_v[bass.ds(G.g, 1)].rearrange("g p t d -> (g p) t d")).then_inc(x_in[G.j], 16)

        def load_phases(sp, G):
            src = t["phases"].rearrange("p (g b) m -> g p b m", g=GROUPS)
            sp.dma_start(xs[:, :, 1:1 + P], src[bass.ds(G.g, 1)].rearrange("g p b m -> (g p) b m"))\
              .then_inc(phase_in, 16)

        def store_y(sp, G):
            for tt in range(GT):
                sp.wait_ge(x_new, G.x_count(tt))
                sp.dma_start(out_v[bass.ds(G.g, 1)][:, :, tt, :].rearrange("g p d -> (g p) d"),
                             x[:, G.rows(tt), :]).then_inc(y_out[tt], 16)

        def prefetch(sp, G):
            n1, n2 = G.later(1), G.later(2)
            sp.wait_ge(cond_mm, G.tiles + GT)
            if n2 and n2.L:
                load_mix(sp, n2)
            if n2:
                sp.wait_ge(c_sum, G.tiles + GT)
                load_rowbias(sp, n2)
            if n2 and n2.L == 0:
                sp.wait_ge(x_in[G.j], 16 * (G.i + 1))
                load_x(sp, n2)
                sp.wait_ge(cond_mm, n1.tiles + GT)
                load_phases(sp, n2)

        def layer(eng, L, step):
            if L == 2:
                for j in range(2):
                    step(Group(L, 0, j))
            with eng.Fori(1 if L == 2 else 0, PAIRS) as i:
                for j in range(2):
                    step(Group(L, i, j))
            for j in range(2):
                step(Group(L, PAIRS, j))

        def first_of(G):
            return isinstance(G.i, int) and G.g == 0

        G0 = Group(0, 0, 0)

        with ExitStack() as tmp:
            NETS = (("condT", B), ("cwT", S), ("netb", 2 * 3), ("netw", 2 * 3 * P), ("netw2", 3 * KM))
            NET0 = B + S + 2 * 3 + 3 * P
            netpack = sb("net_pack", [P, sum(w for _, w in NETS)], where=tmp)
            at = [0]

            def part(width):
                at[0] += width
                return netpack[:, at[0] - width:at[0]]

            condT, cwT, netb, netw, netw2 = (part(w) for _, w in NETS)
            netw = netw.rearrange("p (k l n) -> p k l n", k=2, l=3)
            netb = netb.rearrange("p (k l) -> p k l", k=2)
            netw2 = netw2.rearrange("p (l n) -> p l n", l=3)
            rows64 = sb("rows64", [B, S + 3 * KM], where=tmp)
            fside, netb2 = rows64[:, 0:S], rows64[:, S:]
            kern = sb("mix_kernels", [KM, 3, AGG], where=tmp)
            hid = sb("net_hidden", [P, 2, 3, B], where=tmp)
            att = sb("att", [B, 4, 3, KM], where=tmp)
            attm = sb("att_stat", [B, 3, 3], where=tmp)
            attT = sb("att_t", [KM, 3, B], where=tmp)
            agg = sb("mixed", [B, 3, AGG], where=tmp)
            ctx0 = sb("ctx0", [B, S], where=tmp)
            lora = sb("lora0", [P, 2 * D + 1], where=tmp)
            lbs = sb("lora_b0_scaled", [P, D], where=tmp)
            b2raw = sb("b2_raw", [96, D], where=tmp)
            AGG_BANKS, BIAS_BANK = ((4, 5), (2, 6), (7, 3)), 2

            def store_mixed(sp, L):
                sp.wait_ge(agg_act, L + 1)
                sp.wait_ge(agg_dve, L + 2)
                sp.dma_start(mix_d[L], agg[:, L, 0:S * S]).then_inc(agg_out, 16)
                sp.dma_start(rowbias_d[L + 1].rearrange("(b o) -> b o", o=S), agg[:, L, S * S:AGG])\
                  .then_inc(agg_out, 16)

            def setup_sync(sp):
                sp.dma_start(netpack[:, 0:NET0], t["netpack"][:, 0:NET0]).then_inc(net0_in, 16)
                sp.dma_start(conv_w[:, :, :], t["conv_w"]).then_inc(conv_in, 16)
                sp.wait_ge(zeroed, 1)
                load_phases(sp, G0)
                sp.dma_start(rows64[:, :], t["rows64"].to_broadcast([B, S + 3 * KM])).then_inc(nets_in, 16)
                sp.dma_start(netpack[:, NET0:], t["netpack"][:, NET0:]).then_inc(nets_in, 16)
                sp.dma_start(lora[:, :], t["lora0"]).then_inc(lora_in, 16)
                for n in range(2):
                    load_piece(sp, n, n, setup_pieces[n])
                sp.wait_ge(net_dve, 1)
                sp.dma_start(rowbias_d[0].rearrange("(b o) -> b o", o=S), ctx0[:, :]).then_inc(ctx_out, 16)
                sp.dma_start(ident[:, :], t["ident"]).then_inc(kern_in, 16)
                sp.dma_start(kern[:, :, :], t["kern"]).then_inc(kern_in, 16)
                sp.dma_start(small[:, :], t["small"]).then_inc(const_in, 16)
                sp.dma_start(b2raw[:, :], t["b2"]).then_inc(const_in, 16)
                sp.dma_start(wide_row[:, :], t["wide_row"].to_broadcast([P, E1 + 1])).then_inc(const_in, 16)
                sp.dma_start(token0[:, :], t["token0"]).then_inc(const_in, 16)
                sp.wait_ge(ctx_out, 16)
                for j in range(2):
                    load_rowbias(sp, Group(0, 0, j))
                sp.wait_ge(cond_mm, GT)
                load_phases(sp, Group(0, 0, 1))
                sp.dma_start(biasrow[:, :], t["bias0"].to_broadcast([P, D])).then_inc(biasrow_in, 16)
                for j in range(2):
                    load_x(sp, Group(0, 0, j))
                for L in range(3):
                    store_mixed(sp, L)

            def setup_gpsimd(pool):
                pool.memset(xs[:, :, :], 0.0).then_inc(zeroed, 1)
                pool.memset(gw[:, :, :].bitcast(F32), 0.0).then_inc(zeroed, 1)
                for k in range(FIRST):
                    pool.memset(mix[k][:, :, :], 0.0).then_inc(act_lo, 1)
                pool.memset(ones[:, :], 1.0).then_inc(zeroed, 1)
                pool.memset(coef96[:, :, :], 0.0).then_inc(zeroed, 1)
                for tt in range(GT):
                    cond_lo(pool, G0, tt)

            def setup_tensor(pe):
                pe.wait_ge(net0_in, 16)
                pe.matmul(ps[3][0:B, 0:S], condT, cwT, start=True, stop=True).then_inc(net_mm, 1)
                for L in range(3):
                    mm = pe.matmul(ps[2][:, B * L:B * L + B], netw[:, 0, L, :], condT, start=True, stop=True)
                mm.then_inc(net_mm, 1)
                pe.wait_ge(conv_in, 16)
                cond(pe, G0, 0, first=True)
                pe.wait_ge(nets_in, 16 * 2)
                pe.wait_ge(net_act, 1)
                pe.wait_ge(net_dve, 1)
                for L in range(3):
                    mm = pe.matmul(ps[3][:, B * L:B * L + B], netw[:, 1, L, :], hid[:, 0, L, :],
                                   start=True, stop=True)
                mm.then_inc(net_mm, 1)
                cond(pe, G0, 1, first=True)
                pe.wait_ge(net_act, 2)
                for L in range(3):
                    mm = pe.matmul(ps[2][0:B, KM * L:KM * (L + 1)], hid[:, 1, L, :], netw2[:, L, :],
                                   start=True, stop=True)
                mm.then_inc(net_mm, 1)
                pe.wait_ge(net_dve, 2)
                for c in range(C):
                    pe.matmul(ps[4 + c][:, :], lora[:, c * P:(c + 1) * P], lbs[:, :], start=True, stop=True)\
                      .then_inc(lora_mm, 1)
                pe.wait_ge(kern_in, 16 * 2)
                pe.wait_ge(net_dve, 4)
                for L in range(3):
                    mm = pe.transpose(ps[3][0:KM, B * L:B * (L + 1)], att[:, 3, L, :], ident[0:B, 0:B])
                mm.then_inc(net_mm, 1)
                pe.wait_ge(net_dve, 5)
                pe.wait_ge(w_sum, 2)
                for L in range(3):
                    mm = pe.matmul(ps[BIAS_BANK][0:B, L * S:(L + 1) * S], attT[:, L, :], kern[:, L, 2 * D:AGG],
                                   start=True, stop=True)
                mm.then_inc(agg_mm, 1)
                for L in range(3):
                    if L == 1:
                        pe.wait_ge(agg_dve, 1)
                    for k in range(2):
                        mm = pe.matmul(ps[AGG_BANKS[L][k]][0:B, :], attT[:, L, :], kern[:, L, k * D:(k + 1) * D],
                                       start=True, stop=True)
                    mm.then_inc(agg_mm, 1)

            def setup_scalar(act):
                act.wait_ge(net0_in, 16)
                for k, bank in enumerate((2, 3)):
                    act.wait_ge(net_mm, k + 2)
                    for L in range(3):
                        a = act.activation(hid[:, k, L, :], ps[bank][:, B * L:B * L + B], ACT.Gelu,
                                           bias=netb[:, k, L:L + 1])
                    a.then_inc(net_act, 1)
                act.wait_ge(net_dve, 3)
                act.activation(att[:, 2, :, :], att[:, 1, :, :], ACT.Exp).then_inc(net_act, 1)
                for n in range(2):
                    act.wait_ge(w_sum, n + 1)
                    split_hi(act, n, n, 1, setup_pieces[n])
                act.wait_ge(const_in, 16 * CONST_IN)
                act.wait_ge(zeroed, 4)
                act.activation(b2s[:, :], b2raw[:, :], ACT.Copy).then_inc(small_hi, 1)
                act.activation(gw[:, :, 0:E2], gate_raw, ACT.Copy).then_inc(small_hi, 1)
                cond_hi(act, G0, 0)
                for L in range(3):
                    act.wait_ge(agg_mm, L + 2)
                    act.activation(agg[:, L, 0:D], ps[AGG_BANKS[L][0]][0:B, :], ACT.Copy)\
                       .then_inc(agg_act, 1)
                    if L == 0:
                        cond_hi(act, G0, 1)

            def setup_vector(dve):
                link, n = linker(dve, 0)
                dve.wait_ge(nets_in, 16 * 2)
                dve.wait_ge(net_mm, 1)
                dve.tensor_tensor(ctx0[:, :], ps[3][0:B, 0:S], fside, ALU.add).then_inc(net_dve, 1)
                dve.wait_ge(lora_in, 16)
                dve.tensor_scalar(lbs[:, :], lora[:, D:2 * D], lora[:, 2 * D:2 * D + 1], 2.0, ALU.mult, ALU.mult)\
                   .then_inc(net_dve, 1)
                by_net = "p (l k) -> p l k"
                dve.wait_ge(net_mm, 4)
                link(dve.tensor_tensor(att[:, 0, :, :], ps[2][0:B, 0:3 * KM].rearrange(by_net, l=3),
                                       netb2.rearrange(by_net, l=3), ALU.add))
                link(dve.tensor_reduce(attm[:, 0, :], att[:, 0, :, :], AX.X, ALU.max))
                dve.tensor_tensor(att[:, 1, :, :], att[:, 0, :, :],
                                  attm[:, 0, :].unsqueeze(2).to_broadcast([B, 3, KM]), ALU.subtract)\
                   .then_inc(net_dve, 1)

                def add_adapters(k):
                    dve.wait_ge(stage_in[k], 16)
                    for c in range(2):
                        dve.wait_ge(lora_mm, 2 * k + c + 1)
                        rows = stage[k][:, c * D:(c + 1) * D]
                        a = dve.tensor_tensor(rows, ps[4 + 2 * k + c][:, :], rows, ALU.add)
                    a.then_inc(w_sum, 1)

                add_adapters(0)
                dve.wait_ge(net_act, 3)
                link(dve.tensor_reduce(attm[:, 1, :], att[:, 2, :, :], AX.X, ALU.add))
                link(dve.reciprocal(attm[:, 2, :], attm[:, 1, :]))
                dve.tensor_tensor(att[:, 3, :, :], att[:, 2, :, :],
                                  attm[:, 2, :].unsqueeze(2).to_broadcast([B, 3, KM]), ALU.mult)\
                   .then_inc(net_dve, 1)
                add_adapters(1)
                dve.wait_ge(net_mm, 5)
                dve.tensor_copy(attT[:, :, :], ps[3][0:KM, 0:3 * B].rearrange("p (l b) -> p l b", l=3))\
                   .then_inc(net_dve, 1)
                split_lo(dve, 0, 0, setup_pieces[0])
                cond_sum(dve, G0, 0, first=True)
                dve.wait_ge(agg_mm, 1)
                dve.tensor_copy(agg[:, :, 2 * D:AGG], ps[BIAS_BANK][0:B, 0:3 * S].rearrange(by_net, l=3))\
                   .then_inc(agg_dve, 1)
                split_lo(dve, 1, 1, setup_pieces[1])
                cond_sum(dve, G0, 1, first=True)
                for L in range(3):
                    dve.wait_ge(agg_mm, L + 2)
                    dve.tensor_copy(agg[:, L, D:2 * D], ps[AGG_BANKS[L][1]][0:B, :]).then_inc(agg_dve, 1)
                    if L == 1:
                        dve.wait_ge(agg_act, 2)
                        dve.wait_ge(small_hi, 2)
                        dve.tensor_tensor(b2s[32:64, :], b2raw[32:64, :], b2s[32:64, :].bitcast(F32),
                                          ALU.subtract).then_inc(x_new, 1)
                        dve.tensor_tensor(gw[:, :, 32:32 + E2], gate_raw, gw[:, :, 0:E2].bitcast(F32),
                                          ALU.subtract).then_inc(x_new, 1)
                assert n[0] == CHAIN0

        w1h, w1l = sb("w1_hi", [P, E2, C, D], F32R), sb("w1_lo", [P, E2, C, D], F32R)

        def l1_piece(G):
            g, by_group = bass.ds(G.g, 1), "p (g n) -> p g n"
            hi, lo = (r[:, :].rearrange(by_group, n=L1PIECE)[:, g, :] for r in l1row)
            return N_L0 + 2 * G.g, 0, 2 + G.g, (t["l1row"][:, g, :], 1, L1PIECE, hi, lo)

        def w1_piece(G):
            e, c = bass.ds(G.i, 1), slice(2 * G.j, 2 * G.j + 2)
            hi, lo = (w[:, e, c, :].rearrange("p e c f -> p (e c) f") for w in (w1h, w1l))
            return N_L0 + 2 * G.g + 1, 1, 2 + G.g, (
                t["w1"][e, :, c, :].rearrange("e p c f -> (e p) c f"), 2, D, hi, lo)

        static_pieces = (halves(t["w2"][1], w5h, w5l) + halves(t["w2"][0], w0h, w0l) +
                         halves(t["w2"][2], l1h, l1l) + halves(t["w3T"], w1h[:, 0], w1l[:, 0]))

        def pieces_of(G):
            if G.L == 0 and not isinstance(G.i, int):
                return [l1_piece(G), w1_piece(G)]
            if G.L in (0, 1) and isinstance(G.i, int):
                return [fixed_piece(2 * G.L + G.j)]
            return []

        def fixed_piece(k):
            n = N_W1 + k
            return n, n % 2, n // 2 + 1, static_pieces[k]

        with nc.Block() as block:
            @block.sync
            def _(sp):
                def step(G):
                    for n, par, _, piece in pieces_of(G):
                        load_piece(sp, n, par, piece)
                    prefetch(sp, G)

                setup_sync(sp)
                sp.wait_ge(agg_out, 16 * 6)
                for L in range(3):
                    if L == 2:
                        for k in (4, 5):
                            n, par, _, piece = fixed_piece(k)
                            load_piece(sp, n, par, piece)
                    layer(sp, L, step)
                    if L == 0 or L == 2:
                        k = 1 + L // 2
                        sp.wait_ge(xb_done, GROUPS * k)
                        sp.dma_start(biasrow[:, :], t[f"bias{1 if k == 1 else 3}"].to_broadcast([P, D]))\
                          .then_inc(biasrow_in, 16)
                    if L == 2:
                        for k in (6, 7):
                            n, par, _, piece = fixed_piece(k)
                            load_piece(sp, n, par, piece)

                def last(G):
                    prefetch(sp, G)
                    store_y(sp, G)

                layer(sp, 3, last)
                for j in range(2):
                    sp.wait_ge(y_out[j], 16 * GROUPS)

            @block.tensor
            def _(pe):
                def step0(G):
                    for tt in range(GT):
                        cond(pe, G.later(1), tt)
                    for tt in range(GT):
                        dense(pe, G, tt, w0h, w0l)

                EARLY, MIDDLE, LATE = range(8), range(8, 11), range(11, len(STEPS))

                def step1(G):
                    n1 = G.later(1)
                    for tt, main in ((0, (G, 1)), (1, (n1, 0))):
                        runs = main[0].L == 1
                        if runs:
                            l1_main(pe, *main, EARLY)
                        l1_turn(pe, G, tt)
                        if runs:
                            l1_main(pe, *main, MIDDLE)
                        else:
                            cond(pe, G.later(2), 1)
                        l1_adapt(pe, G, tt)
                        if runs:
                            l1_main(pe, *main, LATE)
                        if tt == 0:
                            cond(pe, n1, 1)
                            if n1.L == 2:
                                cond(pe, G.later(2), 0)
                        elif runs:
                            cond(pe, G.later(2), 0)

                def step2(G):
                    gate_logits(pe, G)
                    if not first_of(G):
                        for tt in range(GT):
                            cond(pe, G.later(1), tt)
                    expert_in(pe, G, 0)
                    gate_turn(pe, G)
                    expert_in(pe, G, 1)
                    gate_top(pe, G)
                    expert_out(pe, G, 0)
                    coef_turn(pe, G)
                    expert_in(pe, G, 2)
                    expert_bias(pe, G)
                    expert_out(pe, G, 1)
                    expert_out(pe, G, 2)

                def step3(G):
                    n1 = G.later(1)
                    if n1:
                        for tt in range(GT):
                            cond(pe, n1, tt)
                    for tt in range(GT):
                        dense(pe, G, tt, w1h[:, 0], w1l[:, 0])

                setup_tensor(pe)
                pe.wait_ge(w_lo, N_L0)
                layer(pe, 0, step0)
                pe.wait_ge(w_lo, N_W1)
                l1_main(pe, Group(1, 0, 0), 0)
                cond(pe, Group(1, 0, 1), 0)
                layer(pe, 1, step1)
                pe.wait_ge(x_new, Group(2, 0, 0).outs + FIRST)
                layer(pe, 2, step2)
                pe.wait_ge(w_lo, N_L3)
                layer(pe, 3, step3)

            @block.scalar
            def _(act):
                def step0(G):
                    pieces = pieces_of(G)
                    for tt in range(GT):
                        ahead_act(act, G, [tt])
                        for p in pieces[tt:tt + 1]:
                            split_hi(act, *p)

                def step1(G):
                    n1, n2 = G.later(1), G.later(2)
                    for tt in range(GT):
                        copy_x(act, n2, tt, n1)
                        act.wait_ge(ht_mm, GT * G.g + tt + 1)
                        act.activation(hth[:, tt, :], ps[6 + tt][:, 0:P], ACT.Copy).then_inc(ht_hi, 1)
                        cond_hi(act, n1, tt)
                    for p in pieces_of(G):
                        split_hi(act, *p)

                def step2(G):
                    ahead_act(act, G)
                    expert_act(act, G, 0)
                    act.wait_ge(gate_sub, G.g + 1)
                    act.activation(g3[:, 1, :, :], g3[:, 0, :, :], ACT.Exp).then_inc(gate_exp, 1)
                    expert_act(act, G, 1)
                    if first_of(G):
                        act.wait_ge(out_mm, 4 * GROUPS)
                        for k in (4, 5):
                            split_hi(act, *fixed_piece(k))
                    act.wait_ge(coeft_mm, G.g + 1)
                    act.activation(coefT[:, :], ps[7][0:96, 0:GR], ACT.Copy).then_inc(coeft_copy, 1)
                    expert_act(act, G, 2)

                setup_scalar(act)
                for k in range(FIRST):
                    act.activation(hth[:, k, :], ident[:, :], ACT.Copy).then_inc(act_f, 1)
                layer(act, 0, step0)
                act.wait_ge(out_mm, 2 * GROUPS)
                layer(act, 1, step1)
                layer(act, 2, step2)
                act.wait_ge(pre_mm, 2 * E2 * GROUPS)
                for k in (6, 7):
                    split_hi(act, *fixed_piece(k), scaled=True)
                layer(act, 3, lambda G: ahead_act(act, G))

            @block.vector
            def _(dve):
                def step0(G):
                    pieces = pieces_of(G)
                    for tt in range(GT):
                        cond_sum(dve, G.later(1), tt)
                        for n, par, _, piece in pieces[tt:tt + 1]:
                            split_lo(dve, n, par, piece)
                    for tt in range(GT):
                        add_out(dve, G, tt)

                def step1(G):
                    link, n = linker(dve, CHAIN0 + CHAIN1 * G.g)
                    for tt in range(GT):
                        router(dve, G, tt, link)
                        cond_sum(dve, G.later(1), tt)
                        turned_lo(dve, G, tt)
                        add_out(dve, G, tt)
                    for k, par, _, piece in pieces_of(G):
                        split_lo(dve, k, par, piece)
                    assert n[0] == CHAIN1, n

                def step2(G):
                    link, n = linker(dve, CHAIN0 + CHAIN1 * GROUPS + CHAIN2 * G.g)
                    gate_ratio(dve, G, link)
                    ahead_dve(dve, G)
                    gate_softmax(dve, G, link)
                    gate_coef(dve, G, link)
                    assert n[0] == CHAIN2, n
                    for tt in range(GT):
                        add_expert(dve, G, 0, tt)
                        if first_of(G):
                            k, par, _, piece = fixed_piece(4 + tt)
                            split_lo(dve, k, par, piece)
                    add_expert_bias(dve, G)
                    last = isinstance(G.i, int) and G.g == GROUPS - 1
                    for tt in range(GT):
                        add_expert(dve, G, 1, tt)
                        if last:
                            k, par, _, piece = fixed_piece(6 + tt)
                            split_lo(dve, k, par, piece, scaled=True)
                    for tt in range(GT):
                        add_expert(dve, G, 2, tt)

                def step3(G):
                    ahead_dve(dve, G)
                    for tt in range(GT):
                        add_out(dve, G, tt)

                setup_vector(dve)
                layer(dve, 0, step0)
                layer(dve, 1, step1)
                layer(dve, 2, step2)
                layer(dve, 3, step3)

            @block.gpsimd
            def _(pool):
                def step(G):
                    add_bias(pool, G)
                    ahead_pool(pool, G)

                def step2(G):
                    ahead_pool(pool, G)
                    for e in range(E2):
                        buf = (3 * G.j + e) % 2
                        for k in range(2):
                            pool.wait_ge(act_hi, 2 * E2 * G.g + 2 * e + k + 1)
                            pool.tensor_tensor(al[buf][:, 2 * k:2 * k + 2, :], af[:, k, :, :],
                                               ah[buf][:, 2 * k:2 * k + 2, :].bitcast(F32), ALU.subtract)\
                                .then_inc(act_lo, 1)

                setup_gpsimd(pool)
                for L, count in ((0, 1), (1, 2), (2, 0), (3, 3)):
                    if L != 2:
                        pool.wait_ge(biasrow_in, 16 * count)
                    layer(pool, L, step2 if L == 2 else step)


def lay_out(i):
    import numpy as np

    a = {k: np.asarray(v) for k, v in i.items()}
    f = np.float32
    q = {}
    x = a["x"]
    q["x"] = x.reshape(ROWS, D)
    q["phases"] = x.reshape(B, S, D // PH, PH).transpose(3, 1, 0, 2).reshape(P, B, D // PH)
    w = a["L0_cond_weight"]
    per, taps = w.shape[1], w.shape[2]
    cw = np.zeros((PH, S, 3, PH, S), f)
    for qi in range(PH):
        for tap in range(3):
            for po in range(PH):
                k = PH * (tap - 1) + qi - po + taps // 2
                if 0 <= k < taps:
                    for g in range(S // per):
                        r = slice(g * per, (g + 1) * per)
                        cw[qi, r, tap, po, r] = w[r, :, k].T
    q["conv_w"] = cw.reshape(P, 3, P)
    q["w0T"] = a["L0_ffn_W"].T.reshape(P, PH, D)
    q["lora0"] = np.concatenate([
        a["L0_ffn_lora_A"].reshape(P, D // PH, PH).transpose(0, 2, 1).reshape(P, D),
        a["L0_ffn_lora_B"].transpose(0, 2, 1).reshape(P, D),
        np.repeat(a["L0_ffn_lora_weights"], R1).reshape(P, 1)], 1)
    nets = [{k: a[f"L{L}_cond_{k}"] for k in ("W0", "b0", "W1", "b1", "W2", "b2", "weight", "bias_k")}
            for L in (1, 2, 3)]
    q["netpack"] = np.concatenate(
        [a["cond_128"].T, a["L0_cond_c_weight"].T] + [n[k].reshape(P, 1) for k in ("b0", "b1") for n in nets] +
        [n[k] for k in ("W0", "W1") for n in nets] + [n["W2"] for n in nets], 1)
    q["rows64"] = np.concatenate([a["fside_S_0"]] + [n["b2"] for n in nets]).reshape(1, S + 3 * KM)
    q["kern"] = np.stack([np.concatenate([n["weight"][..., 0].transpose(0, 2, 1).reshape(KM, S * S),
                                          n["bias_k"]], 1) for n in nets], 1)

    def chunks(m):
        return m.reshape(C, P, -1).transpose(1, 0, 2)

    base, router = a["L1_ffn_W_base"].T, a["L1_ffn_W_router"].T
    adapt = a["L1_ffn_lora_A"].transpose(1, 0, 2).reshape(D, E1 * R1)
    l1 = chunks(np.concatenate([base[:, :HALF], adapt, base[:, HALF:], router], 1)).reshape(P, -1)
    l1 = np.concatenate([l1, a["L1_ffn_lora_B"].reshape(E1 * R1, D)], 1)
    q["l1row"] = np.pad(l1, ((0, 0), (0, (GROUPS - 2) * L1PIECE - L1W))).reshape(P, GROUPS - 2, L1PIECE)
    q["w1"] = np.stack([chunks(m) for m in a["L2_ffn_w1"]])
    q["w2"] = np.stack([chunks(m) for m in a["L2_ffn_w2"]])
    b2 = a["L2_ffn_b2"]
    q["b2"] = np.concatenate([np.pad(b2, ((0, 32 - E2), (0, 0)))] * 3)
    small = [np.tile(np.arange(1, E1 + 1, dtype=f), (P, 1)),
             (np.arange(P)[:, None] % 32 == np.arange(E2)[None, :]).astype(f),
             a["L2_ffn_b1"].reshape(E2 * C, P).T,
             np.pad(np.stack([a["L2_ffn_gate_w"][D], a["L2_ffn_gate_b"]], 1), ((0, P - E2), (0, 0))),
             chunks(a["L2_ffn_gate_w"][:D]).reshape(P, C * E2)]
    q["small"] = np.concatenate(small, 1)
    q["wide_row"] = np.concatenate([a["L1_ffn_b_router"], a["L3_ffn_weight_scale"]]).reshape(1, E1 + 1)
    q["w3T"] = chunks(a["L3_ffn_weight"].T)
    q["bias0"] = a["L0_ffn_bias"].reshape(1, D)
    q["bias1"] = a["L1_ffn_b_base"].reshape(1, D)
    q["bias3"] = a["L3_ffn_bias"].reshape(1, D)
    q["ident"] = np.eye(P, dtype=f)
    q["token0"] = (np.arange(P)[:, None] == np.arange(P)[None, :] // S * S).astype(f)
    return {k: np.ascontiguousarray(v) for k, v in q.items()}


def kernel(**inputs):
    import numpy as np
    import concourse.bacc as bacc
    from concourse.bass_utils import run_bass_kernel_spmd

    nc = bacc.Bacc("TRN2", target_bir_lowering=False, num_devices=1)
    arrays = lay_out(inputs)
    arrays = {"in_" + k: v for k, v in arrays.items()}
    t = {k[3:]: nc.dram_tensor(k, list(v.shape), mybir.dt.from_np(v.dtype), kind="ExternalInput").ap()
         for k, v in arrays.items()}
    t["out"] = nc.dram_tensor("out", [ROWS, D], F32, kind="ExternalOutput").ap()
    build(nc, t)
    r = run_bass_kernel_spmd(nc, [arrays], core_ids=[0])
    return np.asarray(r.results[0]["out"]).reshape(B, S, D)
```

```python
from contextlib import ExitStack

import concourse.bass as bass
from concourse import mybir

F32 = mybir.dt.float32
F32R = mybir.dt.float32r
ALU = mybir.AluOpType
ACT = mybir.ActivationFunctionType
AX = mybir.AxisListType

P = 128
B, S, D = 64, 32, 512
ROWS = B * S
TB = P // S
TILES = ROWS // P
GT = 2
GROUPS = TILES // GT
GR = GT * P
C = D // P
KM = 8
E1, R1 = 8, 16
E2 = 3
VIS = int(S * 0.3)
PH = 4
HALF = D // 2
WA, WB = HALF + E1 * R1, HALF + E1
GM = 72
GK = 64
L1W = C * (WA + WB) + D
L1PIECE = -(-L1W // (GROUPS - 2))
SPLIT = 96
AGG = S * S + S
CONST_IN = 3
WARM_UP = 7
PAIRS = (GROUPS - 2) // 2
FIRST = 2
EV2 = 2 * E2
CHAIN0, CHAIN1, CHAIN2 = 6, 14, 16


class Group:

    def __init__(self, L, i, j):
        self.L, self.i, self.j = L, i, j
        self.g = 2 * i + j
        self.tiles = 2 * GROUPS * L + GT * self.g
        self.outs = {0: 2 * self.g, 1: 2 * GROUPS + 2 * self.g, 2: 4 * GROUPS + EV2 * self.g,
                     3: (4 + EV2) * GROUPS + 2 * self.g}[L]

    def later(self, by):
        i, j = self.i + (self.j + by) // 2, (self.j + by) % 2
        if isinstance(i, int) and i >= GROUPS // 2:
            return Group(self.L + 1, i - GROUPS // 2, j) if self.L < 3 else None
        return Group(self.L, i, j)

    def rows(self, tt):
        return GT * self.g + tt

    def x_count(self, tt):
        return self.outs + (EV2 - 2 if self.L == 2 else 0) + tt + 1 + FIRST


def build(nc, t):
    out_v = t["out"].rearrange("(g t p) d -> g p t d", t=GT, p=P)
    x_v = t["x"].rearrange("(g t p) d -> g p t d", t=GT, p=P)
    mix_d = nc.dram_tensor("mix_scratch", [3, B, S * S], F32, kind="Internal").ap()
    rowbias_d = nc.dram_tensor("rowbias_scratch", [4, ROWS], F32, kind="Internal").ap()

    with ExitStack() as ctx:
        def sb(name, shape, dt=F32, where=None):
            return (where or ctx).enter_context(nc.sbuf_tensor(name, shape, dt))

        def sem(name):
            return ctx.enter_context(nc.semaphore(name))

        x = sb("x_rows", [P, TILES, D])
        w0h, w0l = sb("w0_hi", [P, C, D], F32R), sb("w0_lo", [P, C, D], F32R)
        l1row = [sb(f"l1_{k}", [P, (GROUPS - 2) * L1PIECE], F32R) for k in ("hi", "lo")]
        l1h, l1l = (r[:, 0:C * (WA + WB)].rearrange("p (c n) -> p c n", c=C) for r in l1row)
        lbh, lbl = (r[:, C * (WA + WB):L1W] for r in l1row)
        w5h, w5l = sb("w2e1_hi", [P, C, D], F32R), sb("w2e1_lo", [P, C, D], F32R)
        gw = sb("gate_split", [P, C, GM], F32R)
        stage = [sb(f"stage{k}", [P, 2 * D]) for k in range(2)]
        conv_w = sb("conv_w", [P, 3, P])
        xs = sb("x_mix", [P, GT * TB, P + 2])
        mix = [sb(f"mix{k}", [P, GT, P]) for k in range(2)]
        rowbias = [sb(f"rowbias{k}", [P, GR]) for k in range(2)]
        cf = sb("cond_f32", [P, GT, C, P])
        ch = [sb(f"cond_hi{k}", [P, C, GR], F32R) for k in range(2)]
        cl = [sb(f"cond_lo{k}", [P, C, GR], F32R) for k in range(2)]
        bias = sb("ffn_bias", [P, E2, D])
        af = sb("act_f32", [P, 2, 2, GR])
        ah = [sb(f"act_hi{k}", [P, C, GR], F32R) for k in range(2)]
        al = [sb(f"act_lo{k}", [P, C, GR], F32R) for k in range(2)]
        by_tile = "p (t r) -> p t r"
        hs = af[:, 0, 0, :].rearrange(by_tile, t=GT)
        hth, htl = (al[0][:, k, :].rearrange(by_tile, t=GT) for k in range(2))
        ident, token0, ones = sb("ident", [P, P]), sb("token0", [P, P]), sb("ones", [P, P])
        small = sb("small", [P, E1 + E2 + E2 * C + 2 + C * E2])
        ranks8, gate_sum = small[:, 0:E1], small[0:GK, E1:E1 + E2]
        b1c = small[:, E1 + E2:E1 + E2 + E2 * C]
        tail_at = E1 + E2 + E2 * C
        gate_tail = small[0:GK, tail_at:tail_at + 2]
        gate_raw = small[:, tail_at + 2:].rearrange("p (c e) -> p c e", c=C)
        wide_row = sb("wide_row", [P, E1 + 1])
        brouter, wscale = wide_row[:, 0:E1], wide_row[:, E1:E1 + 1]
        sz = sb("sparsemax", [P, GT, 8, E1])
        sc = sb("sparsemax_scalars", [P, GT, 4])
        absum = sb("abs_sums", [P, 2, GT * TB])
        ratio = sb("ratio", [GK, 3, GT * TB])
        gl = sb("gate_logits", [GK, 2, GR])
        g3 = sb("gate_scores", [P, 6, GT, E2])
        g1 = sb("gate_scalars", [P, 16, GT])
        top = sb("gate_top", [P, 2, GT, E2])
        coef = sb("coef", [P, GT, E2])

        ps = [ctx.enter_context(nc.psum_tensor(f"bank{k}", [P, D], F32)) for k in range(8)]
        OUT = (2, 4)
        SIDE = (3, 5)

        net0_in, nets_in, conv_in, lora_in = sem("net0_in"), sem("nets_in"), sem("conv_in"), sem("lora_in")
        kern_in, ident_in = sem("kern_in"), sem("ident_in")
        const_in, phase_in = sem("const_in"), sem("phase_in")
        stage_in = [sem(f"stage_in{k}") for k in range(2)]
        rowbias_in = [sem(f"rowbias_in{k}") for k in range(2)]
        mix_in = [sem(f"mix_in{k}") for k in range(2)]
        x_in = [sem(f"x_in{k}") for k in range(2)]
        bias_in = sem("bias_in")
        ctx_out, agg_out = sem("ctx_out"), sem("agg_out")
        y_out = [sem(f"y_out{k}") for k in range(2)]
        net_mm, agg_mm, lora_mm, cond_mm = sem("net_mm"), sem("agg_mm"), sem("lora_mm"), sem("cond_mm")
        main_mm, ht_mm, out_mm = sem("main_mm"), sem("ht_mm"), sem("out_mm")
        gate_mm, gatet_mm, top_mm, pre_mm = sem("gate_mm"), sem("gatet_mm"), sem("top_mm"), sem("pre_mm")
        net_act, w_hi, small_hi, c_hi, xs_copy = (sem("net_act"), sem("w_hi"), sem("small_hi"), sem("c_hi"),
                                                  sem("xs_copy"))
        kern_hi = sem("kern_hi")
        agg_act, ht_hi, act_f, act_hi = sem("agg_act"), sem("ht_hi"), sem("act_f"), sem("act_hi")
        gate_exp = sem("gate_exp")
        kern_lo = sem("kern_lo")
        net_dve, agg_dve, chain, w_sum, w_lo = sem("net_dve"), sem("agg_dve"), sem("chain"), sem("w_sum"), sem("w_lo")
        c_sum, hs_done, ht_lo, abs_done = sem("c_sum"), sem("hs_done"), sem("ht_lo"), sem("abs_done")
        logit_done, gate_sub, top_done, bias_new, x_new = (sem("logit_done"), sem("gate_sub"), sem("top_done"),
                                                           sem("bias_new"), sem("x_new"))
        ones_set, zeroed = sem("ones_set"), sem("zeroed")
        c_lo, xb_done, act_lo = sem("c_lo"), sem("xb_done"), sem("act_lo")

        def halves(src, h, l):
            return [(src[:, 2 * k:2 * k + 2, :], 2, D, h[:, 2 * k:2 * k + 2, 0:D], l[:, 2 * k:2 * k + 2, 0:D])
                    for k in range(2)]

        flat = "p (c n) -> p c n"
        setup_pieces = halves(t["w0T"], w0h, w0l)
        N_L0 = len(setup_pieces)
        N_W1 = N_L0 + 2 * (GROUPS - 2)
        N_E1, N_E0, N_E2, N_L3 = N_W1 + 2, N_W1 + 4, N_W1 + 6, N_W1 + 8

        def staged(n, piece):
            return stage[n % 2][:, 0:piece[1] * piece[2]].rearrange(flat, c=piece[1])

        def load_piece(sp, n, par, piece):
            if not isinstance(n, int) or n >= 2:
                sp.wait_ge(w_lo, n - 1)
            sp.dma_start(staged(par, piece), piece[0]).then_inc(stage_in[par], 16)

        def split_hi(act, n, par, nth, piece, scaled=False):
            act.wait_ge(stage_in[par], 16 * nth)
            act.activation(piece[3], staged(par, piece), ACT.Copy,
                           scale=wscale if scaled else 1.0).then_inc(w_hi, 1)

        def split_lo(dve, n, par, piece, scaled=False):
            dve.wait_ge(w_hi, n + 1)
            if isinstance(n, int) and N_E1 < n <= N_E0:
                dve.wait_ge(w_lo, n)
            if scaled:
                dve.scalar_tensor_tensor(out=piece[4], in0=staged(par, piece), scalar=wscale,
                                         in1=piece[3].bitcast(F32), op0=ALU.mult,
                                         op1=ALU.subtract).then_inc(w_lo, 1)
            else:
                dve.tensor_tensor(piece[4], staged(par, piece), piece[3].bitcast(F32),
                                  ALU.subtract).then_inc(w_lo, 1)

        def cond_view(bank):
            return ps[bank][:, :].rearrange(flat, c=C)

        THREE = ((0, 1), (0, 0), (1, 0))
        STEPS = [(a, w, c) for a, w in THREE for c in range(C)]

        def cond(pe, G, tt, first=False):
            if not first:
                pe.wait_ge(c_sum, G.tiles + tt + 1 - GT)
            if G.L == 0:
                pe.wait_ge(phase_in, 16 * (G.g + 1))
                dst = ps[tt][:, :].rearrange("p (c b o) -> p c b o", c=PH, b=TB)
                for b in range(TB):
                    for tap in range(3):
                        mm = pe.matmul(dst[:, :, b, :], xs[:, TB * tt + b, tap:tap + P],
                                       conv_w[:, tap, :].rearrange("k (c o) -> k c o", c=PH),
                                       start=(tap == 0), stop=(tap == 2))
            else:
                pe.wait_ge(mix_in[G.j], 16 * TB * (GROUPS // 2 * (G.L - 1) + G.i + 1))
                pe.wait_ge(xs_copy, G.tiles - 2 * GROUPS + tt + 1)
                for c in range(C):
                    mm = pe.matmul(ps[tt][:, c * P:(c + 1) * P], x_tile(tt)[:, c * P:(c + 1) * P],
                                   mix[G.j][:, tt, :], start=True, stop=True)
            mm.then_inc(cond_mm, 1)

        def x_tile(tt):
            return xs[:, TB * tt:TB * (tt + 1), :].rearrange("p b m -> p (b m)")[:, 0:D]

        def cond_ready(pe, G, tt, k):
            if k == 0:
                pe.wait_ge(c_hi, G.tiles + tt + 1)
            if STEPS[k][0] == 1 and STEPS[k][2] == 0:
                pe.wait_ge(c_lo, G.tiles + tt + 1)

        def out_free(pe, n):
            pe.wait_ge(x_new, n)

        def dense(pe, G, tt, wh, wl):
            out_free(pe, G.outs + tt + 1)
            for k, (a, w, c) in enumerate(STEPS):
                cond_ready(pe, G, tt, k)
                mm = pe.matmul(ps[OUT[tt]][:, :], (ch, cl)[a][G.j][:, c, tt * P:(tt + 1) * P],
                               (wh, wl)[w][:, c, 0:D], start=(k == 0), stop=(k == len(STEPS) - 1))
            mm.then_inc(out_mm, 1)

        def l1_main(pe, G, tt, steps=range(len(STEPS))):
            if steps[0] == 0:
                out_free(pe, G.outs + tt + 1)
            for k in steps:
                a, w, c = STEPS[k]
                cond_ready(pe, G, tt, k)
                for bank, lo, hi in ((OUT[tt], 0, WA), (SIDE[tt], WA, WA + WB)):
                    mm = pe.matmul(ps[bank][:, 0:hi - lo], (ch, cl)[a][G.j][:, c, tt * P:(tt + 1) * P],
                                   (l1h, l1l)[w][:, c, lo:hi], start=(k == 0), stop=(k == len(STEPS) - 1))
            if steps[-1] == len(STEPS) - 1:
                mm.then_inc(main_mm, 1)

        def l1_turn(pe, G, tt):
            pe.wait_ge(hs_done, GT * G.g + tt + 1)
            pe.transpose(ps[6 + tt][:, 0:P], hs[:, tt, :], ident[:, :]).then_inc(ht_mm, 1)

        def l1_adapt(pe, G, tt):
            pe.wait_ge(ht_lo, GT * G.g + tt + 1)
            for a, w in THREE:
                for bank, lo in ((OUT[tt], 0), (SIDE[tt], HALF)):
                    mm = pe.matmul(ps[bank][:, 0:HALF], (hth, htl)[a][:, tt, :], (lbh, lbl)[w][:, lo:lo + HALF],
                                   start=False, stop=True, skip_group_check=True)
            mm.then_inc(out_mm, 1)

        def gate_logits(pe, G):
            pe.wait_ge(c_lo, G.tiles + GT)
            for c in range(C):
                for w in (1, 0):
                    pe.matmul(ps[6][0:GM, 0:GR], gw[:, c, :], (ch, cl)[w][G.j][:, c, :],
                              start=(c == 0 and w == 1), stop=(c == C - 1 and w == 0))
            pe.wait_ge(abs_done, GT * (G.g + 1))
            pe.matmul(ps[6][:, GR:GR + 2 * GT * TB], ones[:, :], absum[:, :, :].rearrange("p k b -> p (k b)"),
                      start=True, stop=True).then_inc(gate_mm, 1)

        def gate_turn(pe, G):
            pe.wait_ge(logit_done, G.g + 1)
            for tt in range(GT):
                mm = pe.matmul(ps[7][:, 4 * tt:4 * tt + E2], gl[:, 1, tt * P:(tt + 1) * P], gate_sum,
                               start=True, stop=True)
            mm.then_inc(gatet_mm, 1)

        def gate_top(pe, G):
            pe.wait_ge(top_done, G.g + 1)
            pe.matmul(ps[6][:, 0:2 * GT * E2], token0[:, :], top[:, :, :, :].rearrange("p k t e -> p (k t e)"),
                      start=True, stop=True).then_inc(top_mm, 1)

        def expert_in(pe, G, e):
            for k in range(2):
                n = 2 * E2 * G.g + 2 * e + k + 1
                pe.wait_ge(act_f, n)
                for f in (2 * k, 2 * k + 1):
                    for c in range(C):
                        for a, w in THREE:
                            mm = pe.matmul(ps[SIDE[k]][:, (f % 2) * GR:(f % 2 + 1) * GR],
                                           (w1h, w1l)[a][:, e, c, f * P:(f + 1) * P], (ch, cl)[w][G.j][:, c, :],
                                           start=(c == 0 and (a, w) == THREE[0]),
                                           stop=(c == C - 1 and (a, w) == THREE[-1]))
                mm.then_inc(pre_mm, 1)

        def expert_out(pe, G, e):
            buf = (3 * G.j + e) % 2
            pe.wait_ge(act_lo, 2 * E2 * G.g + 2 * e + 2 + FIRST)
            pe.wait_ge(w_lo, (N_E0, N_E1, N_E2)[e])
            wh, wl = ((w0h, w0l), (w5h, w5l), (l1h, l1l))[e]
            for tt in range(GT):
                out_free(pe, G.outs + 2 * e + tt + 1)
                for c in range(C):
                    for a, w in THREE:
                        mm = pe.matmul(ps[OUT[tt]][:, :], (ah, al)[a][buf][:, c, tt * P:(tt + 1) * P],
                                       (wh, wl)[w][:, c, 0:D], start=(c == 0 and (a, w) == THREE[0]),
                                       stop=(c == C - 1 and (a, w) == THREE[-1]))
                mm.then_inc(out_mm, 1)

        def cond_hi(act, G, tt):
            act.wait_ge(c_sum, G.tiles + tt + 1)
            act.activation(ch[G.j][:, :, tt * P:(tt + 1) * P], cf[:, tt, :, :], ACT.Copy).then_inc(c_hi, 1)

        def copy_x(act, G, tt, before):
            act.wait_ge(cond_mm, before.tiles + tt + 1)
            act.wait_ge(x_new, Group(G.L - 1, G.i, G.j).x_count(tt))
            act.activation(x_tile(tt), x[:, G.rows(tt), :], ACT.Copy).then_inc(xs_copy, 1)

        def ahead_act(act, G, tiles=range(GT)):
            n1, n2 = G.later(1), G.later(2)
            for tt in tiles:
                if n1:
                    cond_hi(act, n1, tt)
                if n2 and n2.L:
                    copy_x(act, n2, tt, n1)

        def expert_act(act, G, e):
            buf = (3 * G.j + e) % 2
            for k in range(2):
                n = 2 * E2 * G.g + 2 * e + k + 1
                act.wait_ge(pre_mm, n)
                act.wait_ge(act_lo, n)
                for f in range(2):
                    a = act.activation(af[:, k, f, :], ps[SIDE[k]][:, f * GR:(f + 1) * GR],
                                       (ACT.Tanh, ACT.Gelu, ACT.Silu)[e],
                                       bias=b1c[:, e * C + 2 * k + f:e * C + 2 * k + f + 1])
                a.then_inc(act_f, 1)
                act.wait_ge(out_mm, G.outs + 2 * e - 2)
                act.wait_ge(act_f, n + FIRST)
                act.activation(ah[buf][:, 2 * k:2 * k + 2, :], af[:, k, :, :], ACT.Copy).then_inc(act_hi, 1)

        def linker(dve, base):
            n = [0]

            def link(ins):
                n[0] += 1
                ins.then_inc(chain, 1)
                dve.wait_ge(chain, base + n[0])
            return link, n

        def cond_sum(dve, G, tt, first=False):
            dve.wait_ge(rowbias_in[G.j], 16 * (GROUPS // 2 * G.L + G.i + 1))
            dve.wait_ge(cond_mm, G.tiles + tt + 1)
            if not first:
                dve.wait_ge(c_lo, G.tiles + tt + 1 - GT)
            dve.tensor_tensor(cf[:, tt, :, :], cond_view(tt),
                              rowbias[G.j][:, tt * P:(tt + 1) * P].unsqueeze(1).to_broadcast([P, C, P]),
                              ALU.add).then_inc(c_sum, 1)
            if G.L == 2:
                dve.wait_ge(c_sum, G.tiles + tt + 1)
                v = cf[:, tt, :, :].rearrange("p c (b r) -> p b c r", b=TB)
                for k, (lo, hi) in enumerate(((0, VIS), (VIS, S))):
                    r = dve.tensor_reduce(absum[:, k, tt * TB:(tt + 1) * TB], v[:, :, :, lo:hi], AX.XY, ALU.add,
                                          apply_absolute_value=True)
                r.then_inc(abs_done, 1)

        def ahead_dve(dve, G):
            n1 = G.later(1)
            if n1:
                for tt in range(GT):
                    cond_sum(dve, n1, tt)

        def add_out(dve, G, tt):
            dve.wait_ge(xb_done, GROUPS * min(G.L, 2) + G.g + 1)
            dve.wait_ge(out_mm, G.outs + tt + 1)
            row = x[:, G.rows(tt), :]
            if G.L == 1:
                dve.tensor_tensor(row[:, 0:HALF], ps[OUT[tt]][:, 0:HALF], row[:, 0:HALF], ALU.add)
                dve.tensor_tensor(row[:, HALF:D], ps[SIDE[tt]][:, 0:HALF], row[:, HALF:D], ALU.add)\
                   .then_inc(x_new, 1)
            else:
                dve.tensor_tensor(row, ps[OUT[tt]][:, :], row, ALU.add).then_inc(x_new, 1)

        def add_expert(dve, G, e, tt):
            n = G.outs + 2 * e + tt + 1
            dve.wait_ge(out_mm, n)
            if e == 0:
                dve.wait_ge(bias_new, E2 * GT * (G.g + 1))
            else:
                dve.wait_ge(x_new, n)
            row = x[:, G.rows(tt), :]
            dve.scalar_tensor_tensor(out=row, in0=ps[OUT[tt]][:, :], scalar=coef[:, tt, e:e + 1], in1=row,
                                     op0=ALU.mult, op1=ALU.add).then_inc(x_new, 1)

        def add_expert_biases(dve, G):
            dve.wait_ge(bias_in, 16 * 3)
            for e in range(E2):
                for tt in range(GT):
                    if e:
                        dve.wait_ge(bias_new, GT * (E2 * G.g + e - 1) + tt + 1)
                    row = x[:, G.rows(tt), :]
                    dve.scalar_tensor_tensor(out=row, in0=bias[:, e, :], scalar=coef[:, tt, e:e + 1], in1=row,
                                             op0=ALU.mult, op1=ALU.add).then_inc(bias_new, 1)

        def router(dve, G, tt, link):
            z, zs, cum, kz, sup, kk, w, one = (sz[:, tt, k, :] for k in range(8))
            count, total, inv, tau = (sc[:, tt, k:k + 1] for k in range(4))
            dve.wait_ge(main_mm, GT * G.g + tt + 1)
            link(dve.tensor_tensor(z, ps[SIDE[tt]][:, HALF:HALF + E1], brouter, ALU.add))
            dve.memset(sc[:, tt, :], 0.0)
            link(dve.max(zs, z))
            dve.tensor_tensor(kz, zs, ranks8, ALU.mult)
            link(dve.tensor_tensor_scan(cum, ones[:, 0:E1], zs, 0.0, ALU.mult, ALU.add))
            link(dve.scalar_tensor_tensor(out=sup, in0=kz, scalar=1.0, in1=cum, op0=ALU.add, op1=ALU.is_gt,
                                          accum_out=count))
            dve.scalar_tensor_tensor(out=kk, in0=ranks8, scalar=count, in1=cum, op0=ALU.is_equal,
                                     op1=ALU.mult, accum_out=total)
            link(dve.reciprocal(inv, count))
            link(dve.tensor_scalar(tau, total, -1.0, inv, ALU.add, ALU.mult))
            link(dve.tensor_scalar(w, z, tau, 0.0, ALU.subtract, ALU.max))
            dve.tensor_tensor(hs[:, tt, :].rearrange("p (e r) -> p e r", e=E1),
                              ps[OUT[tt]][:, HALF:WA].rearrange("p (e r) -> p e r", e=E1),
                              w.unsqueeze(2).to_broadcast([P, E1, R1]), ALU.mult).then_inc(hs_done, 1)

        def turned_lo(dve, G, tt):
            dve.wait_ge(ht_hi, GT * G.g + tt + 1)
            dve.tensor_tensor(htl[:, tt, :], ps[6 + tt][:, 0:P], hth[:, tt, :].bitcast(F32), ALU.subtract)\
               .then_inc(ht_lo, 1)

        def gate_ratio(dve, G, link):
            dve.wait_ge(gate_mm, G.g + 1)
            vis, text = (ps[6][0:GK, GR + k * GT * TB:GR + (k + 1) * GT * TB] for k in range(2))
            dve.tensor_scalar(gl[:, 0, :], ps[6][0:GK, 0:GR], gate_tail[:, 1:2], None, ALU.add)
            link(dve.tensor_scalar(ratio[:, 0, :], vis, 1.0 / (VIS * D), 1e-8, ALU.mult, ALU.add))
            link(dve.reciprocal(ratio[:, 1, :], ratio[:, 0, :]))
            link(dve.scalar_tensor_tensor(out=ratio[:, 2, :], in0=text, scalar=1.0 / ((S - VIS) * D),
                                          in1=ratio[:, 1, :], op0=ALU.mult, op1=ALU.mult))
            by_batch = "e (b r) -> e b r"
            dve.scalar_tensor_tensor(out=gl[:, 1, :].rearrange(by_batch, r=S),
                                     in0=ratio[:, 2, :].unsqueeze(2).to_broadcast([GK, GT * TB, S]),
                                     scalar=gate_tail[:, 0:1], in1=gl[:, 0, :].rearrange(by_batch, r=S),
                                     op0=ALU.mult, op1=ALU.add).then_inc(logit_done, 1)

        def wide(v):
            return v.unsqueeze(2).to_broadcast([P, GT, E2])

        def gate_softmax(dve, G, link):
            dve.wait_ge(gatet_mm, G.g + 1)
            logits = ps[7][:, 0:4 * GT].rearrange("p (t e) -> p t e", t=GT)[:, :, 0:E2]
            link(dve.tensor_reduce(g1[:, 0, :], logits, AX.X, ALU.max))
            dve.tensor_tensor(g3[:, 0, :, :], logits, wide(g1[:, 0, :]), ALU.subtract).then_inc(gate_sub, 1)
            dve.wait_ge(gate_exp, G.g + 1)
            link(dve.tensor_reduce(g1[:, 1, :], g3[:, 1, :, :], AX.X, ALU.add))
            link(dve.reciprocal(g1[:, 2, :], g1[:, 1, :]))
            link(dve.tensor_tensor(g3[:, 2, :, :], g3[:, 1, :, :], wide(g1[:, 2, :]), ALU.mult))
            s0, s1, s2 = (g3[:, 2, :, e] for e in range(E2))
            dve.tensor_reduce(g1[:, 3, :], g3[:, 2, :, :], AX.X, ALU.max)
            dve.tensor_tensor(g1[:, 4, :], s0, s1, ALU.max)
            dve.tensor_tensor(g1[:, 5, :], s0, s1, ALU.min)
            dve.tensor_tensor(g1[:, 6, :], s0, s1, ALU.is_ge)
            dve.tensor_tensor(g1[:, 7, :], s0, s2, ALU.is_ge)
            link(dve.tensor_tensor(g1[:, 8, :], s1, s2, ALU.is_ge))
            dve.tensor_tensor(g1[:, 9, :], g1[:, 4, :], s2, ALU.min)
            dve.tensor_tensor(g3[:, 3, :, 0], g1[:, 6, :], g1[:, 7, :], ALU.add)
            dve.tensor_tensor(g1[:, 10, :], g1[:, 8, :], g1[:, 6, :], ALU.subtract)
            link(dve.tensor_tensor(g1[:, 11, :], g1[:, 7, :], g1[:, 8, :], ALU.add))
            dve.tensor_scalar(g3[:, 3, :, 1], g1[:, 10, :], 1.0, None, ALU.add)
            dve.tensor_tensor(g1[:, 12, :], g1[:, 5, :], g1[:, 9, :], ALU.max)
            link(dve.tensor_scalar(g3[:, 3, :, 2], g1[:, 11, :], -1.0, 2.0, ALU.mult, ALU.add))
            dve.tensor_scalar(top[:, 0, :, :], g3[:, 3, :, :], 2.0, None, ALU.is_equal)
            dve.tensor_scalar(top[:, 1, :, :], g3[:, 3, :, :], 1.0, None, ALU.is_equal).then_inc(top_done, 1)
            link(dve.tensor_tensor(g1[:, 13, :], g1[:, 3, :], g1[:, 12, :], ALU.add))
            link(dve.tensor_scalar(g1[:, 14, :], g1[:, 13, :], 1e-8, None, ALU.add))
            link(dve.reciprocal(g1[:, 15, :], g1[:, 14, :]))
            dve.tensor_tensor(g1[:, 0, :], g1[:, 3, :], g1[:, 15, :], ALU.mult)
            link(dve.tensor_tensor(g1[:, 1, :], g1[:, 12, :], g1[:, 15, :], ALU.mult))

        def gate_coef(dve, G, link):
            dve.wait_ge(top_mm, G.g + 1)
            ranked = ps[6][:, 0:2 * GT * E2].rearrange("p (k t e) -> p k t e", k=2, t=GT)
            dve.tensor_tensor(g3[:, 4, :, :], ranked[:, 0, :, :], wide(g1[:, 0, :]), ALU.mult)
            link(dve.tensor_tensor(g3[:, 5, :, :], ranked[:, 1, :, :], wide(g1[:, 1, :]), ALU.mult))
            link(dve.tensor_tensor(coef[:, :, :], g3[:, 4, :, :], g3[:, 5, :, :], ALU.add))

        def cond_lo(pool, G, tt):
            pool.wait_ge(c_hi, G.tiles + tt + 1)
            pool.tensor_tensor(cl[G.j][:, :, tt * P:(tt + 1) * P], cf[:, tt, :, :],
                               ch[G.j][:, :, tt * P:(tt + 1) * P].bitcast(F32), ALU.subtract).then_inc(c_lo, 1)

        def add_bias(pool, G):
            if G.L == 0:
                pool.wait_ge(x_in[G.j], 16 * (G.i + 1))
            else:
                pool.wait_ge(xs_copy, G.tiles - 2 * GROUPS + GT)
            rows = x[:, bass.ds(G.rows(0), GT), :]
            pool.tensor_tensor(rows, rows, bias[:, G.L % 3, :].unsqueeze(1).to_broadcast([P, GT, D]), ALU.add)\
                .then_inc(xb_done, 1)

        def ahead_pool(pool, G):
            n1 = G.later(1)
            if n1:
                for tt in range(GT):
                    cond_lo(pool, n1, tt)

        def load_rowbias(sp, G):
            src = rowbias_d[G.L].rearrange("(g a r) -> g a r", a=1, r=GR)
            src = src[bass.ds(G.g, 1), :, :].rearrange("g a r -> (g a) r").to_broadcast([P, GR])
            sp.dma_start(rowbias[G.j][:, :], src).then_inc(rowbias_in[G.j], 16)

        def load_mix(sp, G):
            src = mix_d[G.L - 1].rearrange("(g t b) (i o) -> g b i t o", t=GT, b=TB, i=S)
            for b in range(TB):
                sp.dma_start(mix[G.j][b * S:(b + 1) * S, :, b * S:(b + 1) * S],
                             src[bass.ds(G.g, 1), b].rearrange("g i t o -> (g i) t o")).then_inc(mix_in[G.j], 16)

        def load_x(sp, G):
            sp.dma_start(x[:, bass.ds(G.rows(0), GT), :],
                         x_v[bass.ds(G.g, 1)].rearrange("g p t d -> (g p) t d")).then_inc(x_in[G.j], 16)

        def load_phases(sp, G):
            src = t["phases"].rearrange("p (g b) m -> g p b m", g=GROUPS)
            sp.dma_start(xs[:, :, 1:1 + P], src[bass.ds(G.g, 1)].rearrange("g p b m -> (g p) b m"))\
              .then_inc(phase_in, 16)

        def store_y(sp, G):
            for tt in range(GT):
                sp.wait_ge(x_new, G.x_count(tt))
                sp.dma_start(out_v[bass.ds(G.g, 1)][:, :, tt, :].rearrange("g p d -> (g p) d"),
                             x[:, G.rows(tt), :]).then_inc(y_out[tt], 16)

        def prefetch(sp, G):
            n1, n2 = G.later(1), G.later(2)
            sp.wait_ge(cond_mm, G.tiles + GT)
            if n2 and n2.L:
                load_mix(sp, n2)
            if n2:
                sp.wait_ge(c_sum, G.tiles + GT)
                load_rowbias(sp, n2)
            if n2 and n2.L == 0:
                sp.wait_ge(cond_mm, n1.tiles + GT)
                load_phases(sp, n2)
                sp.wait_ge(x_in[G.j], 16 * (G.i + 1))
                sp.wait_ge(agg_out, 16 * 6)
                load_x(sp, n2)

        def layer(eng, L, step):
            if L == 2:
                for j in range(2):
                    step(Group(L, 0, j))
            with eng.Fori(1 if L == 2 else 0, PAIRS) as i:
                for j in range(2):
                    step(Group(L, i, j))
            for j in range(2):
                step(Group(L, PAIRS, j))

        def first_of(G):
            return isinstance(G.i, int) and G.g == 0

        G0 = Group(0, 0, 0)

        with ExitStack() as tmp:
            NETS = (("condT", B), ("cwT", S), ("netb", 2 * 3), ("netw", 2 * 3 * P), ("netw2", 3 * KM))
            NET0 = B + S + 2 * 3 + 3 * P
            netpack = sb("net_pack", [P, sum(w for _, w in NETS)], where=tmp)
            at = [0]

            def part(width):
                at[0] += width
                return netpack[:, at[0] - width:at[0]]

            condT, cwT, netb, netw, netw2 = (part(w) for _, w in NETS)
            netw = netw.rearrange("p (k l n) -> p k l n", k=2, l=3)
            netb = netb.rearrange("p (k l) -> p k l", k=2)
            netw2 = netw2.rearrange("p (l n) -> p l n", l=3)
            rows64 = sb("rows64", [B, S + 3 * KM], where=tmp)
            fside, netb2 = rows64[:, 0:S], rows64[:, S:]
            kern = sb("mix_kernels", [SPLIT, 3 * AGG], where=tmp)
            kern_split = sb("mix_kernels_split", [SPLIT, 3, AGG], F32R, where=tmp)
            hid = sb("net_hidden", [P, 2, 3, B], where=tmp)
            att = sb("att", [B, 4, 3, KM], where=tmp)
            attm = sb("att_stat", [B, 3, 3], where=tmp)
            att_split = sb("att_split", [B, 3, SPLIT], where=tmp)
            attT = sb("att_t", [SPLIT, 3, B], F32R, where=tmp)
            agg = x[0:B, TILES - 7:TILES, :].rearrange("b t d -> b (t d)")[:, 0:3 * AGG]
            agg = agg.rearrange("b (l n) -> b l n", l=3)
            ctx0 = sb("ctx0", [B, S], where=tmp)
            lora = sb("lora0", [P, 2 * D + 1], where=tmp)
            lbs = sb("lora_b0_scaled", [P, D], where=tmp)
            AGG_BANKS, BIAS_BANK = ((4, 5), (2, 3), (6, 7)), 2

            def store_mixed(eng, L):
                eng.wait_ge(agg_act, L + 2)
                eng.wait_ge(agg_dve, L + 1)
                eng.dma_start(mix_d[L], agg[:, L, 0:S * S]).then_inc(agg_out, 16)
                eng.dma_start(rowbias_d[L + 1].rearrange("(b o) -> b o", o=S), agg[:, L, S * S:AGG])\
                  .then_inc(agg_out, 16)

            def split_kern(eng, L):
                eng.wait_ge(kern_hi, L + 1)
                eng.tensor_tensor(kern_split[32:64, L, :], kern[32:64, L * AGG:(L + 1) * AGG],
                                  kern_split[32:64, L, :].bitcast(F32), ALU.subtract).then_inc(kern_lo, 1)

            def setup_sync(sp):
                sp.dma_start(netpack[:, 0:NET0], t["netpack"][:, 0:NET0]).then_inc(net0_in, 16)
                sp.dma_start(conv_w[:, :, :], t["conv_w"]).then_inc(conv_in, 16)
                sp.wait_ge(zeroed, 1)
                load_phases(sp, G0)
                sp.dma_start(rows64[:, :], t["rows64"].to_broadcast([B, S + 3 * KM])).then_inc(nets_in, 16)
                sp.dma_start(netpack[:, NET0:], t["netpack"][:, NET0:]).then_inc(nets_in, 16)
                sp.dma_start(lora[:, :], t["lora0"]).then_inc(lora_in, 16)
                sp.wait_ge(zeroed, 2)
                for k in range(3):
                    sp.dma_start(kern[32 * k:32 * k + KM, :], t["kern"]).then_inc(kern_in, 16)
                sp.dma_start(ident[:, :], t["ident"]).then_inc(ident_in, 16)
                for n in range(2):
                    load_piece(sp, n, n, setup_pieces[n])
                sp.wait_ge(net_dve, 1)
                sp.dma_start(rowbias_d[0].rearrange("(b o) -> b o", o=S), ctx0[:, :]).then_inc(ctx_out, 16)
                sp.dma_start(small[:, :], t["small"]).then_inc(const_in, 16)
                sp.dma_start(wide_row[:, :], t["wide_row"].to_broadcast([P, E1 + 1])).then_inc(const_in, 16)
                sp.dma_start(token0[:, :], t["token0"]).then_inc(const_in, 16)
                sp.wait_ge(ctx_out, 16)
                for j in range(2):
                    load_rowbias(sp, Group(0, 0, j))
                sp.wait_ge(cond_mm, GT)
                load_phases(sp, Group(0, 0, 1))
                for k in range(2):
                    sp.dma_start(bias[:, k, :], t[f"bias{k}"].to_broadcast([P, D])).then_inc(bias_in, 16)
                for j in range(2):
                    load_x(sp, Group(0, 0, j))

            def setup_gpsimd(pool):
                pool.memset(ones[:, :], 1.0).then_inc(ones_set, 1)
                pool.memset(xs[:, :, :], 0.0).then_inc(zeroed, 1)
                pool.memset(kern[:, :], 0.0).then_inc(zeroed, 1)
                pool.memset(att_split[:, :, :], 0.0).then_inc(zeroed, 1)
                pool.memset(gw[:, :, :].bitcast(F32), 0.0).then_inc(zeroed, 1)
                for k in range(FIRST):
                    pool.memset(mix[k][:, :, :], 0.0).then_inc(act_lo, 1)
                pool.wait_ge(act_lo, FIRST)
                split_kern(pool, 2)
                pool.wait_ge(kern_lo, 3)
                cond_lo(pool, G0, 0)
                pool.wait_ge(agg_act, 3)
                pool.wait_ge(small_hi, 1)
                half = C // FIRST
                for k in range(FIRST):
                    c = slice(k * half, (k + 1) * half)
                    pool.tensor_tensor(gw[:, c, 32:32 + E2], gate_raw[:, c, :], gw[:, c, 0:E2].bitcast(F32),
                                       ALU.subtract).then_inc(x_new, 1)
                cond_lo(pool, G0, 1)

            def setup_tensor(pe):
                pe.wait_ge(ones_set, 1)
                for _ in range(WARM_UP):
                    pe.matmul(ps[7][:, 0:P], ones[:, :], ones[:, :], start=True, stop=True)
                pe.wait_ge(net0_in, 16)
                pe.matmul(ps[3][0:B, 0:S], condT, cwT, start=True, stop=True).then_inc(net_mm, 1)
                for L in range(3):
                    mm = pe.matmul(ps[2][:, B * L:B * L + B], netw[:, 0, L, :], condT, start=True, stop=True)
                mm.then_inc(net_mm, 1)
                pe.wait_ge(conv_in, 16)
                cond(pe, G0, 0, first=True)
                pe.wait_ge(nets_in, 16 * 2)
                pe.wait_ge(net_act, 1)
                pe.wait_ge(net_dve, 1)
                for L in range(3):
                    mm = pe.matmul(ps[3][:, B * L:B * L + B], netw[:, 1, L, :], hid[:, 0, L, :],
                                   start=True, stop=True)
                mm.then_inc(net_mm, 1)
                cond(pe, G0, 1, first=True)
                pe.wait_ge(net_act, 2)
                for L in range(3):
                    mm = pe.matmul(ps[2][0:B, KM * L:KM * (L + 1)], hid[:, 1, L, :], netw2[:, L, :],
                                   start=True, stop=True)
                mm.then_inc(net_mm, 1)
                pe.wait_ge(net_dve, 2)
                for c in range(C):
                    if c == C - 1:
                        pe.wait_ge(ident_in, 16)
                        pe.wait_ge(net_dve, 4)
                        for L in range(3):
                            mm = pe.transpose(ps[3][0:SPLIT, B * L:B * (L + 1)], att_split[:, L, :],
                                              ident[0:B, 0:B])
                        mm.then_inc(net_mm, 1)
                    pe.matmul(ps[4 + c][:, :], lora[:, c * P:(c + 1) * P], lbs[:, :], start=True, stop=True)\
                      .then_inc(lora_mm, 1)
                pe.wait_ge(net_act, 4)
                pe.wait_ge(kern_lo, 3)
                for L in range(3):
                    mm = pe.matmul(ps[BIAS_BANK][0:B, L * S:(L + 1) * S], attT[:, L, :], kern_split[:, L, 2 * D:AGG],
                                   start=True, stop=True)
                mm.then_inc(agg_mm, 1)
                for L in range(3):
                    if L != 1:
                        pe.wait_ge(w_sum, 1 + L // 2)
                    if L == 1:
                        pe.wait_ge(agg_act, 1)
                    for k in range(2):
                        mm = pe.matmul(ps[AGG_BANKS[L][k]][0:B, :], attT[:, L, :], kern_split[:, L, k * D:(k + 1) * D],
                                       start=True, stop=True)
                    mm.then_inc(agg_mm, 1)

            def setup_scalar(act):
                act.wait_ge(net0_in, 16)
                for k, bank in enumerate((2, 3)):
                    act.wait_ge(net_mm, k + 2)
                    for L in range(3):
                        a = act.activation(hid[:, k, L, :], ps[bank][:, B * L:B * L + B], ACT.Gelu,
                                           bias=netb[:, k, L:L + 1])
                    a.then_inc(net_act, 1)
                    if k == 0:
                        act.wait_ge(kern_in, 16 * 3)
                        for L in range(3):
                            act.activation(kern_split[:, L, :], kern[:, L * AGG:(L + 1) * AGG], ACT.Copy)\
                               .then_inc(kern_hi, 1)
                act.wait_ge(net_dve, 3)
                act.activation(att[:, 2, :, :], att[:, 1, :, :], ACT.Exp).then_inc(net_act, 1)
                act.wait_ge(net_mm, 5)
                act.activation(attT[:, :, :], ps[3][0:SPLIT, 0:3 * B].rearrange("p (l b) -> p l b", l=3), ACT.Copy)\
                   .then_inc(net_act, 1)
                act.wait_ge(agg_mm, 1)
                act.activation(agg[:, :, 2 * D:AGG], ps[BIAS_BANK][0:B, 0:3 * S].rearrange("p (l o) -> p l o", l=3),
                               ACT.Copy).then_inc(agg_act, 1)
                for n in range(2):
                    act.wait_ge(w_sum, n + 1)
                    split_hi(act, n, n, 1, setup_pieces[n])
                act.wait_ge(const_in, 16 * CONST_IN)
                act.wait_ge(zeroed, 4)
                act.activation(gw[:, :, 0:E2], gate_raw, ACT.Copy).then_inc(small_hi, 1)
                cond_hi(act, G0, 0)
                for L in range(3):
                    act.wait_ge(agg_mm, L + 2)
                    act.activation(agg[:, L, 0:D], ps[AGG_BANKS[L][0]][0:B, :], ACT.Copy)\
                       .then_inc(agg_act, 1)
                    if L == 0:
                        cond_hi(act, G0, 1)
                for L in range(3):
                    store_mixed(act, L)

            def setup_vector(dve):
                link, n = linker(dve, 0)
                dve.wait_ge(nets_in, 16 * 2)
                dve.wait_ge(net_mm, 1)
                dve.tensor_tensor(ctx0[:, :], ps[3][0:B, 0:S], fside, ALU.add).then_inc(net_dve, 1)
                dve.wait_ge(lora_in, 16)
                dve.tensor_scalar(lbs[:, :], lora[:, D:2 * D], lora[:, 2 * D:2 * D + 1], 2.0, ALU.mult, ALU.mult)\
                   .then_inc(net_dve, 1)
                for L in range(2):
                    split_kern(dve, L)
                by_net = "p (l k) -> p l k"
                dve.wait_ge(net_mm, 4)
                link(dve.tensor_tensor(att[:, 0, :, :], ps[2][0:B, 0:3 * KM].rearrange(by_net, l=3),
                                       netb2.rearrange(by_net, l=3), ALU.add))
                link(dve.tensor_reduce(attm[:, 0, :], att[:, 0, :, :], AX.X, ALU.max))
                dve.tensor_tensor(att[:, 1, :, :], att[:, 0, :, :],
                                  attm[:, 0, :].unsqueeze(2).to_broadcast([B, 3, KM]), ALU.subtract)\
                   .then_inc(net_dve, 1)

                def add_adapters(k):
                    dve.wait_ge(stage_in[k], 16)
                    for c in range(2):
                        dve.wait_ge(lora_mm, 2 * k + c + 1)
                        rows = stage[k][:, c * D:(c + 1) * D]
                        a = dve.tensor_tensor(rows, ps[4 + 2 * k + c][:, :], rows, ALU.add)
                    a.then_inc(w_sum, 1)

                dve.wait_ge(net_act, 3)
                link(dve.tensor_reduce(attm[:, 1, :], att[:, 2, :, :], AX.X, ALU.add))
                link(dve.reciprocal(attm[:, 2, :], attm[:, 1, :]))
                link(dve.tensor_tensor(att[:, 3, :, :], att[:, 2, :, :],
                                       attm[:, 2, :].unsqueeze(2).to_broadcast([B, 3, KM]), ALU.mult))
                dve.wait_ge(zeroed, 3)
                dve.tensor_copy(att_split[:, :, 0:KM].bitcast(F32R), att[:, 3, :, :])
                link(dve.tensor_copy(att_split[:, :, 32:32 + KM].bitcast(F32R), att[:, 3, :, :]))
                dve.tensor_tensor(att_split[:, :, 64:64 + KM], att[:, 3, :, :], att_split[:, :, 32:32 + KM],
                                  ALU.subtract).then_inc(net_dve, 1)
                for k in range(2):
                    add_adapters(k)
                cond_sum(dve, G0, 0, first=True)
                cond_sum(dve, G0, 1, first=True)
                for k in range(2):
                    split_lo(dve, k, k, setup_pieces[k])
                for L in range(3):
                    dve.wait_ge(agg_mm, L + 2)
                    dve.tensor_copy(agg[:, L, D:2 * D], ps[AGG_BANKS[L][1]][0:B, :]).then_inc(agg_dve, 1)
                assert n[0] == CHAIN0

        w1h, w1l = sb("w1_hi", [P, E2, C, D], F32R), sb("w1_lo", [P, E2, C, D], F32R)

        def l1_piece(G):
            g, by_group = bass.ds(G.g, 1), "p (g n) -> p g n"
            hi, lo = (r[:, :].rearrange(by_group, n=L1PIECE)[:, g, :] for r in l1row)
            return N_L0 + 2 * G.g, 0, 2 + G.g, (t["l1row"][:, g, :], 1, L1PIECE, hi, lo)

        def w1_piece(G):
            e, c = bass.ds(G.i, 1), slice(2 * G.j, 2 * G.j + 2)
            hi, lo = (w[:, e, c, :].rearrange("p e c f -> p (e c) f") for w in (w1h, w1l))
            return N_L0 + 2 * G.g + 1, 1, 2 + G.g, (
                t["w1"][e, :, c, :].rearrange("e p c f -> (e p) c f"), 2, D, hi, lo)

        static_pieces = (halves(t["w2"][1], w5h, w5l) + halves(t["w2"][0], w0h, w0l) +
                         halves(t["w2"][2], l1h, l1l) + halves(t["w3T"], w1h[:, 0], w1l[:, 0]))

        def pieces_of(G):
            if G.L == 0 and not isinstance(G.i, int):
                return [l1_piece(G), w1_piece(G)]
            if G.L in (0, 1) and isinstance(G.i, int):
                return [fixed_piece(2 * G.L + G.j)]
            return []

        def fixed_piece(k):
            n = N_W1 + k
            return n, n % 2, n // 2 + 1, static_pieces[k]

        with nc.Block() as block:
            @block.sync
            def _(sp):
                def step(G):
                    for n, par, _, piece in pieces_of(G):
                        load_piece(sp, n, par, piece)
                    prefetch(sp, G)

                setup_sync(sp)
                for L in range(3):
                    if L == 2:
                        for k in (4, 5):
                            n, par, _, piece = fixed_piece(k)
                            load_piece(sp, n, par, piece)
                    layer(sp, L, step)
                    if L == 1:
                        sp.wait_ge(xb_done, 2 * GROUPS)
                        sp.dma_start(bias[:, :, :].rearrange("p e d -> p (e d)"),
                                     t["b2"].to_broadcast([P, E2 * D])).then_inc(bias_in, 16)
                    if L == 2:
                        sp.wait_ge(bias_new, E2 * GT * GROUPS)
                        sp.dma_start(bias[:, 0, :], t["bias3"].to_broadcast([P, D])).then_inc(bias_in, 16)
                        for k in (6, 7):
                            n, par, _, piece = fixed_piece(k)
                            load_piece(sp, n, par, piece)

                def last(G):
                    prefetch(sp, G)
                    store_y(sp, G)

                layer(sp, 3, last)
                for j in range(2):
                    sp.wait_ge(y_out[j], 16 * GROUPS)

            @block.tensor
            def _(pe):
                def step0(G):
                    for tt in range(GT):
                        cond(pe, G.later(1), tt)
                    pe.wait_ge(w_lo, N_L0)
                    for tt in range(GT):
                        dense(pe, G, tt, w0h, w0l)

                EARLY, MIDDLE, LATE = range(8), range(8, 11), range(11, len(STEPS))

                def step1(G):
                    n1 = G.later(1)
                    for tt, main in ((0, (G, 1)), (1, (n1, 0))):
                        runs = main[0].L == 1
                        if runs:
                            l1_main(pe, *main, EARLY)
                        l1_turn(pe, G, tt)
                        if runs:
                            l1_main(pe, *main, MIDDLE)
                        else:
                            cond(pe, G.later(2), 1)
                        l1_adapt(pe, G, tt)
                        if runs:
                            l1_main(pe, *main, LATE)
                        if tt == 0:
                            cond(pe, n1, 1)
                            if n1.L == 2:
                                cond(pe, G.later(2), 0)
                        elif runs:
                            cond(pe, G.later(2), 0)

                def step2(G):
                    gate_logits(pe, G)
                    if first_of(G):
                        pe.wait_ge(x_new, G.outs + FIRST)
                    else:
                        for tt in range(GT):
                            cond(pe, G.later(1), tt)
                    expert_in(pe, G, 0)
                    gate_turn(pe, G)
                    expert_in(pe, G, 1)
                    gate_top(pe, G)
                    expert_out(pe, G, 0)
                    expert_in(pe, G, 2)
                    expert_out(pe, G, 1)
                    expert_out(pe, G, 2)

                def step3(G):
                    n1 = G.later(1)
                    if n1:
                        for tt in range(GT):
                            cond(pe, n1, tt)
                    for tt in range(GT):
                        dense(pe, G, tt, w1h[:, 0], w1l[:, 0])

                setup_tensor(pe)
                layer(pe, 0, step0)
                pe.wait_ge(w_lo, N_W1)
                l1_main(pe, Group(1, 0, 0), 0)
                cond(pe, Group(1, 0, 1), 0)
                layer(pe, 1, step1)
                layer(pe, 2, step2)
                pe.wait_ge(w_lo, N_L3)
                layer(pe, 3, step3)

            @block.scalar
            def _(act):
                def step0(G):
                    pieces = pieces_of(G)
                    for tt in range(GT):
                        ahead_act(act, G, [tt])
                        for p in pieces[tt:tt + 1]:
                            split_hi(act, *p)

                def step1(G):
                    n1, n2 = G.later(1), G.later(2)
                    for tt in range(GT):
                        copy_x(act, n2, tt, n1)
                        act.wait_ge(ht_mm, GT * G.g + tt + 1)
                        act.activation(hth[:, tt, :], ps[6 + tt][:, 0:P], ACT.Copy).then_inc(ht_hi, 1)
                        cond_hi(act, n1, tt)
                    for p in pieces_of(G):
                        split_hi(act, *p)

                def step2(G):
                    ahead_act(act, G)
                    expert_act(act, G, 0)
                    act.wait_ge(gate_sub, G.g + 1)
                    act.activation(g3[:, 1, :, :], g3[:, 0, :, :], ACT.Exp).then_inc(gate_exp, 1)
                    expert_act(act, G, 1)
                    if first_of(G):
                        act.wait_ge(out_mm, 4 * GROUPS)
                        for k in (4, 5):
                            split_hi(act, *fixed_piece(k))
                    expert_act(act, G, 2)

                setup_scalar(act)
                for k in range(FIRST):
                    act.activation(hth[:, k, :], ident[:, :], ACT.Copy).then_inc(act_f, 1)
                layer(act, 0, step0)
                act.wait_ge(out_mm, 2 * GROUPS)
                layer(act, 1, step1)
                layer(act, 2, step2)
                act.wait_ge(pre_mm, 2 * E2 * GROUPS)
                for k in (6, 7):
                    split_hi(act, *fixed_piece(k), scaled=True)
                layer(act, 3, lambda G: ahead_act(act, G))

            @block.vector
            def _(dve):
                def step0(G):
                    pieces = pieces_of(G)
                    for tt in range(GT):
                        cond_sum(dve, G.later(1), tt)
                        for n, par, _, piece in pieces[tt:tt + 1]:
                            split_lo(dve, n, par, piece)
                    for tt in range(GT):
                        add_out(dve, G, tt)

                def step1(G):
                    link, n = linker(dve, CHAIN0 + CHAIN1 * G.g)
                    for tt in range(GT):
                        router(dve, G, tt, link)
                        cond_sum(dve, G.later(1), tt)
                        turned_lo(dve, G, tt)
                        add_out(dve, G, tt)
                    assert n[0] == CHAIN1, n

                def step2(G):
                    link, n = linker(dve, CHAIN0 + CHAIN1 * GROUPS + CHAIN2 * G.g)
                    gate_ratio(dve, G, link)
                    ahead_dve(dve, G)
                    gate_softmax(dve, G, link)
                    gate_coef(dve, G, link)
                    add_expert_biases(dve, G)
                    assert n[0] == CHAIN2, n
                    for tt in range(GT):
                        add_expert(dve, G, 0, tt)
                        if first_of(G):
                            k, par, _, piece = fixed_piece(4 + tt)
                            split_lo(dve, k, par, piece)
                    last = isinstance(G.i, int) and G.g == GROUPS - 1
                    for tt in range(GT):
                        add_expert(dve, G, 1, tt)
                        if last:
                            k, par, _, piece = fixed_piece(6 + tt)
                            split_lo(dve, k, par, piece, scaled=True)
                    for tt in range(GT):
                        add_expert(dve, G, 2, tt)

                def step3(G):
                    ahead_dve(dve, G)
                    for tt in range(GT):
                        add_out(dve, G, tt)

                setup_vector(dve)
                layer(dve, 0, step0)
                layer(dve, 1, step1)
                layer(dve, 2, step2)
                layer(dve, 3, step3)

            @block.gpsimd
            def _(pool):
                def step(G):
                    add_bias(pool, G)
                    ahead_pool(pool, G)
                    if G.L == 1:
                        for n, par, _, piece in pieces_of(G):
                            split_lo(pool, n, par, piece)

                def step2(G):
                    ahead_pool(pool, G)
                    for e in range(E2):
                        buf = (3 * G.j + e) % 2
                        for k in range(2):
                            pool.wait_ge(act_hi, 2 * E2 * G.g + 2 * e + k + 1)
                            pool.tensor_tensor(al[buf][:, 2 * k:2 * k + 2, :], af[:, k, :, :],
                                               ah[buf][:, 2 * k:2 * k + 2, :].bitcast(F32), ALU.subtract)\
                                .then_inc(act_lo, 1)

                setup_gpsimd(pool)
                for L, count in ((0, 2), (1, 2), (2, 0), (3, 4)):
                    if L != 2:
                        pool.wait_ge(bias_in, 16 * count)
                    layer(pool, L, step2 if L == 2 else step)


def lay_out(i):
    import numpy as np

    a = {k: np.asarray(v) for k, v in i.items()}
    f = np.float32
    q = {}
    x = a["x"]
    q["x"] = x.reshape(ROWS, D)
    q["phases"] = x.reshape(B, S, D // PH, PH).transpose(3, 1, 0, 2).reshape(P, B, D // PH)
    w = a["L0_cond_weight"]
    per, taps = w.shape[1], w.shape[2]
    cw = np.zeros((PH, S, 3, PH, S), f)
    for qi in range(PH):
        for tap in range(3):
            for po in range(PH):
                k = PH * (tap - 1) + qi - po + taps // 2
                if 0 <= k < taps:
                    for g in range(S // per):
                        r = slice(g * per, (g + 1) * per)
                        cw[qi, r, tap, po, r] = w[r, :, k].T
    q["conv_w"] = cw.reshape(P, 3, P)
    q["w0T"] = a["L0_ffn_W"].T.reshape(P, PH, D)
    q["lora0"] = np.concatenate([
        a["L0_ffn_lora_A"].reshape(P, D // PH, PH).transpose(0, 2, 1).reshape(P, D),
        a["L0_ffn_lora_B"].transpose(0, 2, 1).reshape(P, D),
        np.repeat(a["L0_ffn_lora_weights"], R1).reshape(P, 1)], 1)
    nets = [{k: a[f"L{L}_cond_{k}"] for k in ("W0", "b0", "W1", "b1", "W2", "b2", "weight", "bias_k")}
            for L in (1, 2, 3)]
    q["netpack"] = np.concatenate(
        [a["cond_128"].T, a["L0_cond_c_weight"].T] + [n[k].reshape(P, 1) for k in ("b0", "b1") for n in nets] +
        [n[k] for k in ("W0", "W1") for n in nets] + [n["W2"] for n in nets], 1)
    q["rows64"] = np.concatenate([a["fside_S_0"]] + [n["b2"] for n in nets]).reshape(1, S + 3 * KM)
    q["kern"] = np.stack([np.concatenate([n["weight"][..., 0].transpose(0, 2, 1).reshape(KM, S * S),
                                          n["bias_k"]], 1) for n in nets], 1).reshape(KM, 3 * AGG)

    def chunks(m):
        return m.reshape(C, P, -1).transpose(1, 0, 2)

    base, router = a["L1_ffn_W_base"].T, a["L1_ffn_W_router"].T
    adapt = a["L1_ffn_lora_A"].transpose(1, 0, 2).reshape(D, E1 * R1)
    l1 = chunks(np.concatenate([base[:, :HALF], adapt, base[:, HALF:], router], 1)).reshape(P, -1)
    l1 = np.concatenate([l1, a["L1_ffn_lora_B"].reshape(E1 * R1, D)], 1)
    q["l1row"] = np.pad(l1, ((0, 0), (0, (GROUPS - 2) * L1PIECE - L1W))).reshape(P, GROUPS - 2, L1PIECE)
    q["w1"] = np.stack([chunks(m) for m in a["L2_ffn_w1"]])
    q["w2"] = np.stack([chunks(m) for m in a["L2_ffn_w2"]])
    q["b2"] = a["L2_ffn_b2"].reshape(1, E2 * D)
    small = [np.tile(np.arange(1, E1 + 1, dtype=f), (P, 1)),
             (np.arange(P)[:, None] % 32 == np.arange(E2)[None, :]).astype(f),
             a["L2_ffn_b1"].reshape(E2 * C, P).T,
             np.pad(np.stack([a["L2_ffn_gate_w"][D], a["L2_ffn_gate_b"]], 1), ((0, P - E2), (0, 0))),
             chunks(a["L2_ffn_gate_w"][:D]).reshape(P, C * E2)]
    q["small"] = np.concatenate(small, 1)
    q["wide_row"] = np.concatenate([a["L1_ffn_b_router"], a["L3_ffn_weight_scale"]]).reshape(1, E1 + 1)
    q["w3T"] = chunks(a["L3_ffn_weight"].T)
    q["bias0"] = a["L0_ffn_bias"].reshape(1, D)
    q["bias1"] = a["L1_ffn_b_base"].reshape(1, D)
    q["bias3"] = a["L3_ffn_bias"].reshape(1, D)
    q["ident"] = np.eye(P, dtype=f)
    q["token0"] = (np.arange(P)[:, None] == np.arange(P)[None, :] // S * S).astype(f)
    return {k: np.ascontiguousarray(v) for k, v in q.items()}


def kernel(**inputs):
    import numpy as np
    import concourse.bacc as bacc
    from concourse.bass_utils import run_bass_kernel_spmd

    nc = bacc.Bacc("TRN2", target_bir_lowering=False, num_devices=1)
    arrays = lay_out(inputs)
    arrays = {"in_" + k: v for k, v in arrays.items()}
    t = {k[3:]: nc.dram_tensor(k, list(v.shape), mybir.dt.from_np(v.dtype), kind="ExternalInput").ap()
         for k, v in arrays.items()}
    t["out"] = nc.dram_tensor("out", [ROWS, D], F32, kind="ExternalOutput").ap()
    build(nc, t)
    r = run_bass_kernel_spmd(nc, [arrays], core_ids=[0])
    return np.asarray(r.results[0]["out"]).reshape(B, S, D)
```
